# Optimizing a Trainium2 kernel written in Bass

```python
import numpy as np
import jax
import jax.numpy as jnp

def _softmax(x, axis=-1):
    return jax.nn.softmax(x, axis=axis)
def _gelu(x):
    return jax.nn.gelu(x, approximate=True)
def _silu(x):
    return jax.nn.silu(x)
def _sigmoid(x):
    return jax.nn.sigmoid(x)
def _layernorm(x, axis=-1, eps=1e-5):
    m = jnp.mean(x, axis=axis, keepdims=True)
    v = jnp.var(x, axis=axis, keepdims=True)
    return (x - m) / jnp.sqrt(v + eps)
def _scatter_add(tgt, idx, src, axis=0):
    return tgt.at[idx].add(src)
def _segment_sum(src, seg, n):
    return jax.ops.segment_sum(src, seg, n)

kernel_name = 'mk_conv_attn_hybrid_d2_conv_nchw256_051231'

def setup_inputs(seed: int = 0):
    np.random.seed(seed)
    _w = jnp.asarray
    def _rec_inputs():
        import jax
        import jax.numpy as jnp
        _gk = jax.random.key(seed)
        x = -0.000929 + 1 * jax.random.normal(jax.random.fold_in(_gk, 1), (1, 256, 64, 64), jnp.float32)
        return x
    x = _rec_inputs()
    def _L0_conv_setup():
        import jax, jax.numpy as jnp
        import numpy as np
        from functools import partial
        DIM = 256
        HEADS = 8
        HEAD_DIM = DIM // HEADS
        SCALES = (1, 2, 4)
        B, H, W = (1, 64, 64)

        def _dwconv3x3(x, w, b):
            y = jax.lax.conv_general_dilated(x, w, window_strides=(1, 1), padding='SAME', feature_group_count=x.shape[1], dimension_numbers=('NCHW', 'OIHW', 'NCHW'))
            return y + b[None, :, None, None]

        def _pwconv(x, w, b):
            return jnp.einsum('bchw,oc->bohw', x, w) + b[None, :, None, None]

        def _avg_pool(x, s):
            Bb, C, Hh, Ww = x.shape
            return x.reshape(Bb, C, Hh // s, s, Ww // s, s).mean(axis=(3, 5))
        key = jax.random.key(seed)
        ks = jax.random.split(key, 9)
        sc = 0.05
        return {'x': jax.random.normal(ks[0], (B, DIM, H, W), dtype=jnp.float32), 'dw_w': jax.random.normal(ks[1], (3, DIM, 1, 3, 3), dtype=jnp.float32) * sc, 'dw_b': jax.random.normal(ks[2], (3, DIM), dtype=jnp.float32) * sc, 'pw_w': jax.random.normal(ks[3], (3, 3 * DIM, DIM), dtype=jnp.float32) * sc, 'pw_b': jax.random.normal(ks[4], (3, 3 * DIM), dtype=jnp.float32) * sc, 'pos_w': jax.random.normal(ks[5], (3, DIM, 1, 3, 3), dtype=jnp.float32) * sc, 'pos_b': jax.random.normal(ks[6], (3, DIM), dtype=jnp.float32) * sc, 'fusion_w': jax.random.normal(ks[7], (DIM, 3 * DIM), dtype=jnp.float32) * sc, 'fusion_b': jax.random.normal(ks[8], (DIM,), dtype=jnp.float32) * sc}
    _L0_conv_all = _L0_conv_setup()
    _L0_conv_in = {k: v for k, v in _L0_conv_all.items() if k in ('dw_w', 'dw_b', 'pw_w', 'pw_b', 'pos_w', 'pos_b', 'fusion_w', 'fusion_b', )}
    del _L0_conv_all

    def _L1_attn_setup():
        import jax, jax.numpy as jnp
        import numpy as np
        import math
        H = 8
        DH = 16
        DEPTH = 1
        LAMBDA_INIT = 0.8 - 0.6 * math.exp(-0.3 * DEPTH)
        LN_EPS = 1e-05
        key = jax.random.key(seed)
        ks = jax.random.split(key, 12)
        dim = 256
        inner = 2 * H * DH
        b, n = (2, 2048)
        s = lambda fan_in: 1.0 / math.sqrt(fan_in)
        return {'x': jax.random.normal(ks[0], (b, n, dim), jnp.float32), 'Wq': jax.random.normal(ks[1], (dim, inner), jnp.float32) * s(dim), 'Wkv': jax.random.normal(ks[2], (dim, 2 * inner), jnp.float32) * s(dim), 'Wout': jax.random.normal(ks[3], (inner, dim), jnp.float32) * s(inner), 'bout': jnp.zeros((dim,), jnp.float32), 'Wg': jax.random.normal(ks[4], (dim, inner), jnp.float32) * s(dim), 'bg': jnp.ones((inner,), jnp.float32), 'lq1': jax.random.normal(ks[5], (DH,), jnp.float32) * 0.1, 'lk1': jax.random.normal(ks[6], (DH,), jnp.float32) * 0.1, 'lq2': jax.random.normal(ks[7], (DH,), jnp.float32) * 0.1, 'lk2': jax.random.normal(ks[8], (DH,), jnp.float32) * 0.1, 'ln_gamma': jnp.ones((2 * DH,), jnp.float32), 'ln_beta': jnp.zeros((2 * DH,), jnp.float32)}
    _L1_attn_all = _L1_attn_setup()
    _L1_attn_in = {k: v for k, v in _L1_attn_all.items() if k in ('Wq', 'Wkv', 'Wout', 'bout', 'Wg', 'bg', 'lq1', 'lk1', 'lq2', 'lk2', 'ln_gamma', 'ln_beta', )}
    del _L1_attn_all

    def _L1_ffn_setup():
        import jax, jax.numpy as jnp
        import numpy as np
        B, S, D = (8, 4096, 256)
        H = 4 * D
        CAPACITY = 0.5
        key = jax.random.key(seed)
        ks = jax.random.split(key, 6)
        x = jax.random.normal(ks[0], (B, S, D), dtype=jnp.float32)
        attention_mask = jnp.zeros((B, 1, 1, S), dtype=jnp.float32)
        wr = jax.random.normal(ks[1], (D, 1), dtype=jnp.float32) * 0.02
        br = jnp.zeros((1,), dtype=jnp.float32)
        w1 = jax.random.normal(ks[2], (D, H), dtype=jnp.float32) * 0.02
        b1 = jnp.zeros((H,), dtype=jnp.float32)
        w2 = jax.random.normal(ks[3], (H, D), dtype=jnp.float32) * 0.02
        b2 = jnp.zeros((D,), dtype=jnp.float32)
        return {'x': x, 'attention_mask': attention_mask, 'wr': wr, 'br': br, 'w1': w1, 'b1': b1, 'w2': w2, 'b2': b2}
    _L1_ffn_all = _L1_ffn_setup()
    _L1_ffn_in = {k: v for k, v in _L1_ffn_all.items() if k in ('attention_mask', 'wr', 'br', 'w1', 'b1', 'w2', 'b2', )}
    del _L1_ffn_all

    return {
        "x": x,
        "L0_conv_dw_w": _L0_conv_in["dw_w"],
        "L0_conv_dw_b": _L0_conv_in["dw_b"],
        "L0_conv_pw_w": _L0_conv_in["pw_w"],
        "L0_conv_pw_b": _L0_conv_in["pw_b"],
        "L0_conv_pos_w": _L0_conv_in["pos_w"],
        "L0_conv_pos_b": _L0_conv_in["pos_b"],
        "L0_conv_fusion_w": _L0_conv_in["fusion_w"],
        "L0_conv_fusion_b": _L0_conv_in["fusion_b"],
        "L1_attn_Wq": _L1_attn_in["Wq"],
        "L1_attn_Wkv": _L1_attn_in["Wkv"],
        "L1_attn_Wout": _L1_attn_in["Wout"],
        "L1_attn_bout": _L1_attn_in["bout"],
        "L1_attn_Wg": _L1_attn_in["Wg"],
        "L1_attn_bg": _L1_attn_in["bg"],
        "L1_attn_lq1": _L1_attn_in["lq1"],
        "L1_attn_lk1": _L1_attn_in["lk1"],
        "L1_attn_lq2": _L1_attn_in["lq2"],
        "L1_attn_lk2": _L1_attn_in["lk2"],
        "L1_attn_ln_gamma": _L1_attn_in["ln_gamma"],
        "L1_attn_ln_beta": _L1_attn_in["ln_beta"],
        "L1_ffn_attention_mask": _L1_ffn_in["attention_mask"],
        "L1_ffn_wr": _L1_ffn_in["wr"],
        "L1_ffn_br": _L1_ffn_in["br"],
        "L1_ffn_w1": _L1_ffn_in["w1"],
        "L1_ffn_b1": _L1_ffn_in["b1"],
        "L1_ffn_w2": _L1_ffn_in["w2"],
        "L1_ffn_b2": _L1_ffn_in["b2"],
    }

def reference(x, L0_conv_dw_w, L0_conv_dw_b, L0_conv_pw_w, L0_conv_pw_b, L0_conv_pos_w, L0_conv_pos_b, L0_conv_fusion_w, L0_conv_fusion_b, L1_attn_Wq, L1_attn_Wkv, L1_attn_Wout, L1_attn_bout, L1_attn_Wg, L1_attn_bg, L1_attn_lq1, L1_attn_lk1, L1_attn_lq2, L1_attn_lk2, L1_attn_ln_gamma, L1_attn_ln_beta, L1_ffn_attention_mask, L1_ffn_wr, L1_ffn_br, L1_ffn_w1, L1_ffn_b1, L1_ffn_w2, L1_ffn_b2):
    import jax
    import jax.numpy as jnp
    def _L0_conv_ref(x, dw_w, dw_b, pw_w, pw_b, pos_w, pos_b, fusion_w, fusion_b):
        import jax, jax.numpy as jnp
        import numpy as np
        from functools import partial
        DIM = 256
        HEADS = 8
        HEAD_DIM = DIM // HEADS
        SCALES = (1, 2, 4)
        B, H, W = (1, 64, 64)

        def _dwconv3x3(x, w, b):
            y = jax.lax.conv_general_dilated(x, w, window_strides=(1, 1), padding='SAME', feature_group_count=x.shape[1], dimension_numbers=('NCHW', 'OIHW', 'NCHW'))
            return y + b[None, :, None, None]

        def _pwconv(x, w, b):
            return jnp.einsum('bchw,oc->bohw', x, w) + b[None, :, None, None]

        def _avg_pool(x, s):
            Bb, C, Hh, Ww = x.shape
            return x.reshape(Bb, C, Hh // s, s, Ww // s, s).mean(axis=(3, 5))
        Bb, C, Hh, Ww = x.shape
        outputs = []
        for i, scale in enumerate(SCALES):
            xs = _avg_pool(x, scale) if scale > 1 else x
            x_dw = _dwconv3x3(xs, dw_w[i], dw_b[i])
            qkv = _pwconv(x_dw, pw_w[i], pw_b[i])
            q, k, v = jnp.split(qkv, 3, axis=1)
            pos = _dwconv3x3(xs, pos_w[i], pos_b[i])
            q = q + pos
            k = k + pos
            Hs, Ws = (xs.shape[2], xs.shape[3])
            Ns = Hs * Ws
            q = q.reshape(Bb, HEADS, HEAD_DIM, Ns)
            k = k.reshape(Bb, HEADS, HEAD_DIM, Ns)
            v = v.reshape(Bb, HEADS, HEAD_DIM, Ns)
            attn = jnp.einsum('bhdn,bhdm->bhnm', q, k) / HEAD_DIM ** 0.5
            attn = jax.nn.softmax(attn, axis=-1)
            out = jnp.einsum('bhnm,bhdm->bhdn', attn, v)
            out = out.reshape(Bb, C, Hs, Ws)
            if scale > 1:
                out = jax.image.resize(out, (Bb, C, Hh, Ww), method='bilinear')
            outputs.append(out)
        cat = jnp.concatenate(outputs, axis=1)
        return jnp.einsum('bchw,oc->bohw', cat, fusion_w) + fusion_b[None, :, None, None]

    def _L1_attn_ref(x, Wq, Wkv, Wout, bout, Wg, bg, lq1, lk1, lq2, lk2, ln_gamma, ln_beta):
        import jax, jax.numpy as jnp
        import numpy as np
        import math
        H = 8
        DH = 16
        DEPTH = 1
        LAMBDA_INIT = 0.8 - 0.6 * math.exp(-0.3 * DEPTH)
        LN_EPS = 1e-05
        b, n, dim = x.shape
        scale = DH ** (-0.5)
        q = x @ Wq
        kv = x @ Wkv
        k, v = jnp.split(kv, 2, axis=-1)
        q = q.reshape(b, n, 2 * H, DH).transpose(0, 2, 1, 3) * scale
        k = k.reshape(b, n, 2 * H, DH).transpose(0, 2, 1, 3)
        v = v.reshape(b, n, H, 2 * DH).transpose(0, 2, 1, 3)
        dots = jnp.einsum('bhid,bhjd->bhij', q, k)
        attn = jax.nn.softmax(dots, axis=-1)
        lam1 = jnp.exp(jnp.sum(lq1 * lk1))
        lam2 = jnp.exp(jnp.sum(lq2 * lk2))
        lam = lam1 - lam2 + LAMBDA_INIT
        attn = attn.reshape(b, H, 2, n, n)
        attn = attn[:, :, 0] - lam * attn[:, :, 1]
        out = jnp.einsum('bhij,bhjd->bhid', attn, v)
        mu = jnp.mean(out, axis=-1, keepdims=True)
        var = jnp.var(out, axis=-1, keepdims=True)
        out = (out - mu) * jax.lax.rsqrt(var + LN_EPS) * ln_gamma + ln_beta
        out = out * (1.0 - LAMBDA_INIT)
        out = out.transpose(0, 2, 1, 3).reshape(b, n, H * 2 * DH)
        gates = x @ Wg + bg
        out = out * jax.nn.sigmoid(gates)
        return out @ Wout + bout

    def _L1_ffn_ref(x, attention_mask, wr, br, w1, b1, w2, b2):
        import jax, jax.numpy as jnp
        import numpy as np
        B, S, D = (8, 4096, 256)
        H = 4 * D
        CAPACITY = 0.5
        b, s, d = x.shape
        weights = (jnp.einsum('bsd,do->bso', x, wr) + br)[..., 0]
        k = max(1, int(CAPACITY * s))
        kk = k - 1 if k > 1 else 1
        _, idx = jax.lax.top_k(weights, k)
        sel_idx = idx[:, :kk]
        sel = jnp.take_along_axis(x, sel_idx[:, :, None], axis=1)
        h = jax.nn.gelu(jnp.einsum('bkd,dh->bkh', sel, w1) + b1)
        y = jnp.einsum('bkh,hd->bkd', h, w2) + b2
        w_sel = jnp.take_along_axis(weights, sel_idx, axis=1)
        y = y * w_sel[..., None]
        batch_idx = jnp.arange(b)[:, None]
        processed = jnp.zeros_like(x).at[batch_idx, sel_idx].set(y)
        return processed + x

    def _gn(v, G=32, eps=1e-5):
        B_, C_, H_, W_ = v.shape
        g = v.reshape(B_, G, C_ // G, H_, W_)
        m = jnp.mean(g, axis=(2, 3, 4), keepdims=True)
        s = jnp.var(g, axis=(2, 3, 4), keepdims=True)
        return ((g - m) / jnp.sqrt(s + eps)).reshape(v.shape)

    def _ln_c(v, eps=1e-6):
        m = jnp.mean(v, axis=1, keepdims=True)
        s = jnp.var(v, axis=1, keepdims=True)
        return (v - m) / jnp.sqrt(s + eps)

    def _ln_t(v, eps=1e-5):
        m = jnp.mean(v, axis=-1, keepdims=True)
        s = jnp.var(v, axis=-1, keepdims=True)
        return (v - m) / jnp.sqrt(s + eps)

    def _to_tokens(v):
        B_, C_, H_, W_ = v.shape
        return v.reshape(B_, C_, H_ * W_).transpose(0, 2, 1)
    def _from_tokens(t, like):
        B_, C_, H_, W_ = like.shape
        return t.transpose(0, 2, 1).reshape(B_, C_, H_, W_)

    x = x + _L0_conv_ref(_gn(x), L0_conv_dw_w, L0_conv_dw_b, L0_conv_pw_w, L0_conv_pw_b, L0_conv_pos_w, L0_conv_pos_b, L0_conv_fusion_w, L0_conv_fusion_b)
    t = _to_tokens(x)
    t = t + _L1_attn_ref(_ln_t(t), L1_attn_Wq, L1_attn_Wkv, L1_attn_Wout, L1_attn_bout, L1_attn_Wg, L1_attn_bg, L1_attn_lq1, L1_attn_lk1, L1_attn_lq2, L1_attn_lk2, L1_attn_ln_gamma, L1_attn_ln_beta)
    t = t + _L1_ffn_ref(_ln_t(t), L1_ffn_attention_mask, L1_ffn_wr, L1_ffn_br, L1_ffn_w1, L1_ffn_b1, L1_ffn_w2, L1_ffn_b2)
    x = _from_tokens(t, x)
    return x


_drawn_inputs = setup_inputs


def setup_inputs(seed=0):
    import zlib

    import numpy as np

    out = dict(_drawn_inputs(seed))
    spreads = {'L1_attn_bout': (0.0, 0.1),
     'L1_attn_bg': (1.0, 0.6),
     'L1_attn_ln_gamma': (1.0, 0.2),
     'L1_attn_ln_beta': (0.0, 0.1),
     'L1_ffn_b1': (0.0, 0.8),
     'L1_ffn_b2': (0.0, 0.8)}
    factors = {'L0_conv_dw_w': 8.0,
     'L0_conv_pos_w': 8.0,
     'L0_conv_pos_b': 8.0,
     'L1_attn_lq1': 8.0,
     'L1_attn_lq2': 6.483,
     'L1_attn_lk2': 4.204,
     'L1_ffn_wr': 3.347,
     'L1_ffn_w1': 6.069,
     'L1_ffn_w2': 5.684}
    for name, (base, spread) in spreads.items():
        noise = np.random.default_rng([zlib.crc32(name.encode()), seed]).standard_normal(out[name].shape)
        drawn = base * np.exp(spread * noise) if base else spread * noise
        out[name] = jnp.asarray(drawn.astype(out[name].dtype))
    for name, factor in factors.items():
        out[name] = (out[name] * factor).astype(out[name].dtype)
    return out
```

```python
import math
from contextlib import ExitStack

import concourse.bass as bass
from concourse import mybir

F32 = mybir.dt.float32
F32R = mybir.dt.float32r
ACT = mybir.ActivationFunctionType
ALU = mybir.AluOpType
AX = mybir.AxisListType


HEAD_START = 1


class AttentionPlan:

    def __init__(self, name, maps, tokens, width, part_rows, v_cols, v_shared):
        self.name, self.maps, self.tokens, self.width = name, maps, tokens, width
        self.part_rows, self.v_cols, self.v_shared = part_rows, v_cols, v_shared
        self.key_tiles = tokens // 128
        self.blocks = tokens // width
        self.units = maps * self.blocks
        self.pairs = self.key_tiles // 2
        self.q_tiles = width // 128
        self.key_chunk = min(512, tokens)
        self.chunks = tokens // self.key_chunk
        self.maxima = self.q_tiles * self.chunks
        self.lead = self.chunks
        self.sums = v_cols + 1
        self.column_tile = 32 if self.sums <= 32 else 64
        self.groups = min(128 // self.column_tile, self.key_tiles)
        self.ring = 4 if self.pairs % 4 == 0 else 2
        self.batch = 2 if self.pairs >= 2 else 1
        self.sum_step = min(2, self.pairs - 1)
        self.shift_step = self.pairs - 3 if self.pairs >= 8 else max(0, self.pairs - 2)


class Slot:

    def __init__(self, engine, plan, pair_of_maps, parity, first, odd, block):
        self.unit, self.odd, self.parity, self.pair_of_maps = engine.snap(first), odd, parity, pair_of_maps
        self.blocks, self.block = plan.blocks, block
        self.last = block == plan.blocks - 1

    def maps_ahead(self, n):
        return 0 if self.block is None else (self.block + n) // self.blocks

    def map_parity(self, n):
        return (self.parity + self.maps_ahead(n)) % 2

    def map_turn(self, n):
        return self.pair_of_maps + (self.parity + self.maps_ahead(n)) // 2

    def enters(self, n):
        return self.block is not None and (self.block + n) % self.blocks == 0

    def turn_of(self, n):
        return (self.unit - self.odd) // 2 + (self.odd + n) // 2


def each_unit(engine, plan, body):
    blocks = plan.blocks
    with engine.Fori(0, plan.maps // 2) as pair_of_maps:
        for parity in range(2):
            first = (pair_of_maps * 2 + parity) * blocks
            looped = blocks - 2 if blocks > 4 else 0
            if looped:
                with engine.Fori(0, looped // 2) as turn:
                    for odd in range(2):
                        body(Slot(engine, plan, pair_of_maps, parity, first + turn * 2 + odd, odd, None))
            for block in range(looped, blocks):
                odd = (parity * blocks + block) % 2
                body(Slot(engine, plan, pair_of_maps, parity, first + block, odd, block))


def attention(nc, plan, q_scratch, k_scratch, v_scratch, out_scratch):
    n, w, ring = plan.name, plan.width, plan.ring
    rows = 3 * plan.part_rows
    with nc.cleanup_on_exit(), ExitStack() as ctx:
        def sb(what, shape, dt=F32):
            return ctx.enter_context(nc.sbuf_tensor(f"{n}_{what}", shape, dt))

        def ps(what, shape):
            return ctx.enter_context(nc.psum_tensor(f"{n}_{what}", shape, F32))

        def sem(what):
            return nc.alloc_semaphore(f"{n}_{what}")

        keys = [sb(f"keys{i}", [97, plan.tokens], F32R) for i in range(2)]
        q_max = [sb(f"q_max{i}", [96, w], F32R) for i in range(2)]
        q_exp = [sb(f"q_exp{i}", [97, w], F32R) for i in range(2)]
        values = [sb(f"values{i}", [128, plan.key_tiles, plan.column_tile]) for i in range(2)]
        probs = sb("probs", [128, ring, 2, w])
        maxima = sb("maxima", [128, 2, plan.maxima])
        shift = sb("shift", [128, plan.q_tiles, 97], F32R)
        ident = sb("ident", [128, 128])
        ident_r = sb("ident_r", [128, 128], F32R)
        fold = sb("fold", [128, plan.sums])
        out_t = sb("out_t", [128, w])
        recip = sb("recip", [128, plan.q_tiles])
        result = sb("result", [128, 2, plan.q_tiles, 32])
        scores = [ps(f"scores{i}", [128, 2, 512]) for i in range(2)]
        max_scores = [ps(f"max_scores{i}", [128, 512]) for i in range(2)]
        weighted = ps("weighted", [128, 512])
        aux = ps("aux", [128, 512])

        keys_loaded = [sem(f"keys_loaded{i}") for i in range(2)]
        values_loaded = [sem(f"values_loaded{i}") for i in range(2)]
        q_max_loaded = [sem(f"q_max_loaded{i}") for i in range(2)]
        q_exp_loaded = [sem(f"q_exp_loaded{i}") for i in range(2)]
        result_stored = [sem(f"result_stored{i}") for i in range(2)]
        consts_made = sem("consts_made")
        cleared = sem("cleared")
        const_ready = sem("const_ready")
        scores_ready = sem("scores_ready")
        probs_ready = sem("probs_ready")
        probs_free = sem("probs_free")
        max_scores_ready = sem("max_scores_ready")
        max_scores_used = sem("max_scores_used")
        shift_ready = sem("shift_ready")
        shift_turned = sem("shift_turned")
        shift_placed = sem("shift_placed")
        out_copied = sem("out_copied")
        sums_ready = sem("sums_ready")
        recip_ready = sem("recip_ready")
        result_ready = sem("result_ready")
        block = ctx.enter_context(nc.Block())

        P, J, T = plan.pairs, plan.maxima, plan.q_tiles
        units = plan.units

        @block.gpsimd
        def _(pool):
            nc.gpsimd.memset(ident[:, :], 0.0).then_inc(consts_made, 1)
            nc.gpsimd.memset(fold[:, :], 0.0).then_inc(consts_made, 1)
            pool.wait_ge(consts_made, 2)
            nc.gpsimd.affine_select(out=ident[:, :], in_=ident[:, :], compare_op=ALU.not_equal, fill=1.0, base=0,
                                    pattern=[[-1, 128]], channel_multiplier=1).then_inc(consts_made, 1)
            for g in range(plan.groups):
                pool.wait_ge(consts_made, 3 + g)
                nc.gpsimd.affine_select(out=fold[:, :], in_=fold[:, :], compare_op=ALU.not_equal, fill=1.0,
                                        base=-plan.column_tile * g, pattern=[[-1, plan.sums]],
                                        channel_multiplier=1).then_inc(consts_made, 1)

        @block.sync
        def _(sp):
            for i in range(2):
                sp.sem_inc(result_stored[i], HEAD_START)
            sp.wait_ge(const_ready, 1)
            for i in range(2):
                sp.dma_start(q_max[i][0:rows, :].bitcast(F32), q_scratch[i]).then_inc(q_max_loaded[i], 16)
                sp.dma_start(keys[i][0:rows, :].bitcast(F32), k_scratch[i]).then_inc(keys_loaded[i], 16)
                sp.dma_start(q_exp[i][0:rows, :].bitcast(F32), q_scratch[i]).then_inc(q_exp_loaded[i], 16)
                sp.dma_start(values[i][:, :, 0:plan.v_cols],
                             v_scratch[0 if plan.v_shared else i]).then_inc(values_loaded[i], 16)
            sp.wait_ge(max_scores_ready, J)
            sp.dma_start(q_max[0][0:rows, :].bitcast(F32), q_scratch[2 % units]).then_inc(q_max_loaded[0], 16)

            def unit(s):
                sp.wait_ge(max_scores_ready, (s.unit + 2) * J)
                sp.dma_start(q_max[1 - s.odd][0:rows, :].bitcast(F32), q_scratch[(s.unit + 3) % units])\
                    .then_inc(q_max_loaded[1 - s.odd], 16)
                sp.wait_ge(scores_ready, (s.unit + 1) * P)
                sp.dma_start(q_exp[s.odd][0:rows, :].bitcast(F32), q_scratch[(s.unit + 2) % units])\
                    .then_inc(q_exp_loaded[s.odd], 16)
                if s.last:
                    sp.dma_start(keys[s.parity][0:rows, :].bitcast(F32),
                                 k_scratch[(s.pair_of_maps * 2 + s.parity + 2) % plan.maps])\
                        .then_inc(keys_loaded[s.parity], 16)
                    sp.wait_ge(probs_free, (s.unit + 1) * P + ring)
                    head = ((s.pair_of_maps + 1) % (plan.maps // 2) if plan.v_shared
                            else (s.pair_of_maps * 2 + s.parity + 2) % plan.maps)
                    sp.dma_start(values[s.parity][:, :, 0:plan.v_cols], v_scratch[head])\
                        .then_inc(values_loaded[s.parity], 16)
                sp.wait_ge(result_ready, s.unit + 1)
                sp.dma_start(out_scratch[s.unit], result[:, s.odd, :, :]).then_inc(result_stored[s.odd], 16)
            each_unit(sp, plan, unit)
            sp.wait_ge(result_ready, units + 1)
            sp.dma_start(out_scratch[units], result[:, units % 2, :, :]).then_inc(result_stored[units % 2], 16)
            for i in range(2):
                sp.wait_ge(result_stored[i], HEAD_START + 16 * ((units + 2 - i) // 2))
            for i in range(2):
                sp.wait_ge(keys_loaded[i], 16 * (plan.maps // 2 + 1))
                sp.wait_ge(values_loaded[i], 16 * (plan.maps // 2 + 1))
                sp.wait_ge(q_exp_loaded[i], 16 * (units // 2 + 1))
                sp.wait_ge(q_max_loaded[i], 16 * (units // 2 + 1 + (i == 0)))

        @block.scalar
        def _(act):
            act.sem_inc(out_copied, HEAD_START)
            act.sem_inc(probs_ready, HEAD_START)
            def place_shift(odd):
                nc.scalar.activation(q_exp[odd][96:97, :], aux[96:97, 0:w], ACT.Copy).then_inc(shift_placed, 1)

            act.wait_ge(shift_turned, 1)
            place_shift(0)

            def unit(s):
                for p in range(P):
                    at = (s.odd * P + p) if P < 4 else p
                    act.wait_ge(scores_ready, s.unit * P + (p + 1))
                    act.wait_ge(probs_free, s.unit * P + (p + 1))
                    nc.scalar.activation(probs[:, at % ring, :, :], scores[at % 2][:, :, 0:w],
                                         ACT.Exp).then_inc(probs_ready, 1)
                    if p == plan.shift_step:
                        act.wait_ge(shift_turned, s.unit + 2)
                        place_shift(1 - s.odd)
                act.wait_ge(probs_free, (s.unit + 1) * P + ring)
                act.wait_ge(sums_ready, s.unit + 1)
                nc.scalar.activation(out_t[:, :], weighted[:, 0:w], ACT.Copy).then_inc(out_copied, 1)
            each_unit(act, plan, unit)

        @block.vector
        def _(dve):
            for i in range(2):
                nc.vector.memset(keys[i][:, :].bitcast(F32), 0.0).then_inc(cleared, 1)
                nc.vector.memset(q_max[i][:, :].bitcast(F32), 0.0).then_inc(cleared, 1)
                nc.vector.memset(q_exp[i][:, :].bitcast(F32), 0.0).then_inc(cleared, 1)
                nc.vector.memset(values[i][:, :, :], 0.0).then_inc(cleared, 1)
            nc.vector.memset(shift[:, :, :].bitcast(F32), 0.0).then_inc(cleared, 1)
            nc.vector.memset(out_t[:, :], 1.0).then_inc(cleared, 1)
            dve.wait_ge(cleared, 10)
            dve.wait_ge(consts_made, 3 + plan.groups)
            for i in range(2):
                nc.vector.memset(keys[i][96:97, :].bitcast(F32), 1.0).then_inc(cleared, 1)
                nc.vector.memset(values[i][:, :, plan.v_cols:plan.v_cols + 1], 1.0).then_inc(cleared, 1)
            nc.vector.tensor_copy(ident_r[:, :], ident[:, :]).then_inc(cleared, 1)
            dve.wait_ge(cleared, 15)
            dve.sem_inc(const_ready, 1)

            def row_maxima(made, odd, j):
                dve.wait_ge(max_scores_ready, made + 1)
                nc.vector.tensor_reduce(maxima[:, odd, j:j + 1], max_scores[j % 2][:, 0:plan.key_chunk], AX.X,
                                        ALU.max).then_inc(max_scores_used, 1)
                if j == J - 1:
                    dve.wait_ge(max_scores_used, made + 1)
                    nc.vector.tensor_reduce(
                        shift[:, :, 96], maxima[:, odd, :].rearrange("p (t c) -> p t c", c=plan.chunks), AX.X,
                        ALU.max, negate=True).then_inc(shift_ready, 1)

            def normalise(number, odd, stores_before):
                dve.wait_ge(sums_ready, number + 1)
                sums = aux[:, 0:T * plan.sums].rearrange("p (t c) -> p t c", c=plan.sums)
                nc.vector.reciprocal(recip[:, :], sums[:, :, plan.v_cols]).then_inc(recip_ready, 1)
                dve.wait_ge(recip_ready, number + 1)
                dve.wait_ge(result_stored[odd], HEAD_START + stores_before)
                nc.vector.tensor_tensor(result[:, odd, :, :], sums[:, :, 0:32],
                                        recip[:, :].unsqueeze(2).to_broadcast([128, T, 32]),
                                        ALU.mult).then_inc(result_ready, 1)

            for j in range(J):
                row_maxima(j, 0, j)
            for j in range(plan.lead):
                row_maxima(J + j, 1, j)

            def unit(s):
                for p in range(P):
                    for i in range(2):
                        j = plan.lead + 2 * p + i
                        row_maxima((s.unit + 1) * J + j, (s.odd + 1 + j // J) % 2, j % J)
                    if p == plan.sum_step:
                        normalise(s.unit, s.odd, s.turn_of(0) * 16)
            each_unit(dve, plan, unit)
            normalise(units, units % 2, units // 2 * 16)

        @block.tensor
        def _(pe):
            def max_product(made, odd, j, k_parity):
                if not (isinstance(made, int) and made < 2):
                    pe.wait_ge(max_scores_used, made - 1)
                t, c = divmod(j, plan.chunks)
                nc.tensor.matmul(max_scores[j % 2][:, 0:plan.key_chunk], q_max[odd][:, t * 128:(t + 1) * 128],
                                 keys[k_parity][0:96, c * plan.key_chunk:(c + 1) * plan.key_chunk],
                                 start=True, stop=True).then_inc(max_scores_ready, 1)

            def turn_shift():
                for t in range(T):
                    last = nc.tensor.matmul(aux[0:97, t * 128:(t + 1) * 128], shift[:, t, :], ident_r[:, :],
                                            start=True, stop=True)
                last.then_inc(shift_turned, 1)

            def score_product(odd, k_parity, p, slot):
                for i in range(2):
                    kt = 2 * p + i
                    last = nc.tensor.matmul(scores[slot][:, i, 0:w], keys[k_parity][:, kt * 128:(kt + 1) * 128],
                                            q_exp[odd][:, :], start=True, stop=True)
                last.then_inc(scores_ready, 1)

            def fold_groups():
                for t in range(T):
                    last = nc.tensor.matmul(aux[:, t * plan.sums:(t + 1) * plan.sums],
                                            out_t[:, t * 128:(t + 1) * 128], fold[:, :], start=True, stop=True)
                last.then_inc(sums_ready, 1)

            pe.wait_ge(const_ready, 1)
            pe.wait_ge(q_max_loaded[0], 16)
            pe.wait_ge(keys_loaded[0], 16)
            for j in range(J):
                max_product(j, 0, j, 0)
            pe.wait_ge(q_max_loaded[1], 16)
            pe.wait_ge(keys_loaded[1], 16)
            for j in range(plan.lead):
                max_product(J + j, 1, j, 0 if plan.blocks > 1 else 1)
            pe.wait_ge(shift_ready, 1)
            turn_shift()
            pe.wait_ge(q_exp_loaded[0], 16)
            pe.wait_ge(q_exp_loaded[1], 16)
            pe.wait_ge(shift_placed, 1)
            score_product(0, 0, 0, 0)
            pe.sem_inc(probs_free, ring)

            def unit(s):
                def scores_of_next(p):
                    at = (s.odd * P + p + 1) if P < 4 else p + 1
                    pe.wait_ge(probs_ready, HEAD_START + s.unit * P + p)
                    if p < P - 1:
                        score_product(s.odd, s.parity, p + 1, at % 2)
                    else:
                        pe.wait_ge(q_exp_loaded[1 - s.odd], (s.turn_of(1) + 1) * 16)
                        pe.wait_ge(shift_placed, s.unit + 2)
                        score_product(1 - s.odd, s.map_parity(1), 0, at % 2)

                for p in range(P):
                    late = p == plan.shift_step and p == P - 1
                    if not late:
                        scores_of_next(p)
                    for i in range(2):
                        j = plan.lead + 2 * p + i
                        ahead = 1 + j // J
                        if j == J:
                            pe.wait_ge(q_max_loaded[s.odd], (s.turn_of(2) + 1) * 16)
                            if s.enters(2):
                                pe.wait_ge(keys_loaded[s.map_parity(2)], (s.map_turn(2) + 1) * 16)
                        max_product((s.unit + 1) * J + j, (s.odd + ahead) % 2, j % J, s.map_parity(ahead))
                    if p == plan.sum_step:
                        pe.wait_ge(out_copied, HEAD_START + s.unit)
                        fold_groups()
                    if p == plan.shift_step:
                        pe.wait_ge(shift_ready, s.unit + 2)
                        pe.wait_ge(result_ready, s.unit + 1)
                        turn_shift()
                    if late:
                        scores_of_next(p)
                    if p % plan.batch == plan.batch - 1:
                        if p == plan.batch - 1:
                            pe.wait_ge(values_loaded[s.parity], (s.map_turn(0) + 1) * 16)
                            pe.wait_ge(out_copied, HEAD_START + s.unit)
                        pe.wait_ge(probs_ready, HEAD_START + s.unit * P + (p + 1))
                        for kt in range(2 * (p - plan.batch + 1), 2 * (p + 1)):
                            at = (s.odd * P + kt // 2) if P < 4 else kt // 2
                            g = kt % plan.groups
                            last = nc.tensor.matmul(
                                weighted[g * plan.column_tile:(g + 1) * plan.column_tile, 0:w],
                                values[s.parity][:, kt, :], probs[:, at % ring, kt % 2, :],
                                start=kt < plan.groups, stop=kt >= plan.key_tiles - plan.groups)
                        last.then_inc(probs_free, plan.batch)
            each_unit(pe, plan, unit)
            pe.wait_ge(out_copied, HEAD_START + units)
            fold_groups()


class Steps:

    def __init__(self, engine, sem, turn=0, per_turn=0):
        self.engine, self.sem, self.base, self.n, self.per_turn = engine, sem, turn * per_turn, 0, per_turn

    def __call__(self, instruction):
        self.n += 1
        instruction.then_inc(self.sem, 1)
        return self.n

    def wait(self, n=None):
        self.engine.wait_ge(self.sem, self.base + (self.n if n is None else n))

    def link(self, instruction):
        self(instruction)
        self.wait()


DIM, SIDE, TOKENS = 256, 64, 4096
HALVES = DIM // 128
SCALES = (1, 2, 4)
HEADS = 8
BLOCK = 512


def make_identity(nc, pool, ident, made):
    nc.gpsimd.memset(ident[:, :], 0.0).then_inc(made, 1)
    pool.wait_ge(made, 1)
    nc.gpsimd.affine_select(out=ident[:, :], in_=ident[:, :], compare_op=ALU.not_equal, fill=1.0, base=0,
                            pattern=[[-1, 128]], channel_multiplier=1).then_inc(made, 1)


def convolutions(nc, x, dw_w, dw_b, pos_w, pos_b, dw_scratch, pos_scratch):
    group = 8
    with nc.cleanup_on_exit(), ExitStack() as ctx:
        def sb(what, shape, dt=F32):
            return ctx.enter_context(nc.sbuf_tensor(f"cv_{what}", shape, dt))

        def sem(what):
            return nc.alloc_semaphore(f"cv_{what}")

        sides = [SIDE // s for s in SCALES]
        x_in = sb("x_in", [128, HALVES, TOKENS])
        padded = [sb(f"padded{i}", [128, HALVES, d + 2, d + 2]) for i, d in enumerate(sides)]
        taps = sb("taps", [128, 3, HALVES, 2, 9])
        biases = sb("biases", [128, 3, HALVES, 2])
        diagonal = [sb(f"diagonal{i}", [128, HALVES, 9, 128]) for i in range(3)]
        dw_out = [sb(f"dw_out{i}", [128, HALVES, d, d]) for i, d in enumerate(sides)]
        pos_out = sb("pos_out", [128, 4, BLOCK])
        ident = sb("ident", [128, 128])
        group_mean = sb("group_mean", [128, 128])
        stats = sb("stats", [128, HALVES, 8, 6])
        moments = sb("moments", [128, HALVES, 2])
        group_moments = sb("group_moments", [128, HALVES, 2])
        spread = sb("spread", [128, HALVES, 4])
        groups_ps = ctx.enter_context(nc.psum_tensor("cv_groups", [128, 512], F32))
        pos_ps = [ctx.enter_context(nc.psum_tensor(f"cv_pos{i}", [128, 512], F32)) for i in range(4)]

        x_loaded = [sem(f"x_loaded{i}") for i in range(HALVES)]
        weights_loaded = sem("weights_loaded")
        identity_made = sem("identity_made")
        group_made = sem("group_made")
        borders_cleared = sem("borders_cleared")
        dve_steps = sem("dve_steps")
        moments_ready = sem("moments_ready")
        groups_ready = sem("groups_ready")
        variance_ready = sem("variance_ready")
        deviation_ready = sem("deviation_ready")
        scaled_ready = sem("scaled_ready")
        diagonal_ready = sem("diagonal_ready")
        dw_ready = sem("dw_ready")
        pos_product = sem("pos_product")
        pos_copied = sem("pos_copied")
        pos_stored = [sem(f"pos_stored{i}") for i in range(4)]
        dw_stored = sem("dw_stored")
        block = ctx.enter_context(nc.Block())

        pieces = []
        for i, d in enumerate(sides):
            rows = min(BLOCK // d, d)
            pieces += [(i, h, r, rows) for r in range(0, d, rows) for h in range(HALVES)]

        @block.sync
        def _(sp):
            for h in range(HALVES):
                sp.dma_start(x_in[:, h, :], x[h * 128:(h + 1) * 128, :]).then_inc(x_loaded[h], 16)
            for i in range(3):
                for h in range(HALVES):
                    at = slice(h * 128, (h + 1) * 128)
                    for j, (w, b) in enumerate(((dw_w, dw_b), (pos_w, pos_b))):
                        sp.dma_start(taps[:, i, h, j, :], w[i, at, :]).then_inc(weights_loaded, 16)
                        sp.dma_start(biases[:, i, h, j:j + 1], b[i, at, :]).then_inc(weights_loaded, 16)
            for i in range(3):
                sp.wait_ge(dw_ready, 2 * i + 2)
                sp.dma_start(dw_scratch[i].rearrange("h p n -> p h n"),
                             dw_out[i][:, :, :, :].rearrange("p h r c -> p h (r c)")).then_inc(dw_stored, 16)
            sp.wait_ge(dw_stored, 48)

        @block.gpsimd
        def _(pool):
            make_identity(nc, pool, ident, identity_made)
            nc.gpsimd.memset(group_mean[:, :], 1.0 / group).then_inc(group_made, 1)
            view = group_mean[:, :].rearrange("p (g c) -> p g c", c=group)
            pool.wait_ge(group_made, 1)
            nc.gpsimd.affine_select(out=view, in_=view, compare_op=ALU.is_ge, fill=0.0, base=0,
                                    pattern=[[-group, 128 // group], [0, group]], channel_multiplier=1)\
                .then_inc(group_made, 1)
            pool.wait_ge(group_made, 2)
            nc.gpsimd.affine_select(out=view, in_=view, compare_op=ALU.is_ge, fill=0.0, base=group - 1,
                                    pattern=[[group, 128 // group], [0, group]], channel_multiplier=-1)\
                .then_inc(group_made, 1)
            for i in range(3):
                nc.gpsimd.memset(padded[i][:, :, :, :], 0.0).then_inc(borders_cleared, 1)

        @block.scalar
        def _(act):
            act.wait_ge(variance_ready, 1)
            nc.scalar.activation(spread[:, :, 1], spread[:, :, 0], ACT.Sqrt).then_inc(deviation_ready, 1)
            act.wait_ge(weights_loaded, 16 * 24)
            for n, (i, h, r, rows) in enumerate(pieces):
                act.wait_ge(pos_product, n + 1)
                if n >= 4:
                    act.wait_ge(pos_stored[n % 4], 16 * (n // 4))
                w = rows * sides[i]
                nc.scalar.activation(pos_out[:, n % 4, 0:w], pos_ps[n % 4][:, 0:w], ACT.Identity,
                                     bias=biases[:, i, h, 1:2]).then_inc(pos_copied, 1)
                act.wait_ge(pos_copied, n + 1)
                act.dma_start(pos_scratch[i][h][:, r * sides[i]:r * sides[i] + w], pos_out[:, n % 4, 0:w])\
                    .then_inc(pos_stored[n % 4], 16)
            for k in range(4):
                act.wait_ge(pos_stored[k], 16 * len(range(k, len(pieces), 4)))

        @block.tensor
        def _(pe):
            pe.wait_ge(moments_ready, 1)
            pe.wait_ge(group_made, 3)
            nc.tensor.matmul(groups_ps[:, 0:4], group_mean[:, :],
                             moments[:, :, :].rearrange("p h m -> p (h m)"), start=True, stop=True)\
                .then_inc(groups_ready, 1)
            for n, (i, h, r, rows) in enumerate(pieces):
                pe.wait_ge(scaled_ready, i + 1)
                pe.wait_ge(diagonal_ready, i + 1)
                if n >= 4:
                    pe.wait_ge(pos_copied, n - 3)
                d = sides[i]
                for k in range(9):
                    last = nc.tensor.matmul(pos_ps[n % 4][:, 0:rows * d], diagonal[i][:, h, k, :],
                                            padded[i][:, h, r + k // 3:r + k // 3 + rows, k % 3:k % 3 + d],
                                            start=k == 0, stop=k == 8)
                last.then_inc(pos_product, 1)

        @block.vector
        def _(dve):
            step = Steps(dve, dve_steps)
            for h in range(HALVES):
                dve.wait_ge(x_loaded[h], 16)
                for c in range(8):
                    step(nc.vector.bn_stats(stats[:, h, c, :], x_in[:, h, c * 512:(c + 1) * 512]))
            step.wait()
            for h in range(HALVES):
                step(nc.vector.bn_aggr(moments[:, h, :], stats[:, h, :, :].rearrange("p c s -> p (c s)")))
            step.wait()
            step.link(nc.vector.tensor_tensor(spread[:, :, 2], moments[:, :, 0], moments[:, :, 0], ALU.mult))
            nc.vector.tensor_tensor(moments[:, :, 1], moments[:, :, 1], spread[:, :, 2], ALU.add)\
                .then_inc(moments_ready, 1)
            dve.wait_ge(groups_ready, 1)
            step.link(nc.vector.tensor_copy(group_moments[:, :, :],
                                            groups_ps[:, 0:4].rearrange("p (h m) -> p h m", m=2)))
            step.link(nc.vector.tensor_tensor(spread[:, :, 3], group_moments[:, :, 0], group_moments[:, :, 0],
                                              ALU.mult))
            step.link(nc.vector.tensor_tensor(spread[:, :, 2], group_moments[:, :, 1], spread[:, :, 3],
                                              ALU.subtract))
            nc.vector.tensor_scalar(spread[:, :, 0], spread[:, :, 2], 1e-5, None, ALU.add)\
                .then_inc(variance_ready, 1)
            inverse_root(nc, dve, step, deviation_ready, 1, spread[:, :, 0], spread[:, :, 1], spread[:, :, 2])
            dve.wait_ge(borders_cleared, 3)
            for h in range(HALVES):
                step(nc.vector.tensor_scalar(
                    padded[0][:, h, 1:SIDE + 1, 1:SIDE + 1], x_in[:, h, :].rearrange("p (r c) -> p r c", c=SIDE),
                    group_moments[:, h, 0:1], spread[:, h, 1:2], ALU.subtract, ALU.mult))
            step.wait()
            dve.sem_inc(scaled_ready, 1)
            dve.wait_ge(weights_loaded, 16 * 24)
            dve.wait_ge(identity_made, 2)

            def diagonals(i):
                for h in range(HALVES):
                    for k in range(9):
                        step(nc.vector.tensor_scalar(diagonal[i][:, h, k, :], ident[:, :],
                                                     taps[:, i, h, 1, k:k + 1], None, ALU.mult))
                step.wait()
                dve.sem_inc(diagonal_ready, 1)

            diagonals(0)
            for i in (1, 2):
                d = sides[i]
                for h in range(HALVES):
                    fine = padded[i - 1][:, h, 1:2 * d + 1, 1:2 * d + 1].rearrange("p (r a) c -> p r a c", a=2)
                    rows = x_in[:, h, 0:2 * d * d].rearrange("p (r c) -> p r c", c=2 * d)
                    step.link(nc.vector.tensor_tensor(rows, fine[:, :, 0, :], fine[:, :, 1, :], ALU.add))
                    pairs = rows.rearrange("p r (c b) -> p r c b", b=2)
                    sums = x_in[:, h, 2048:2048 + d * d].rearrange("p (r c) -> p r c", c=d)
                    step.link(nc.vector.tensor_tensor(sums, pairs[:, :, :, 0], pairs[:, :, :, 1], ALU.add))
                    step.link(nc.vector.tensor_scalar(padded[i][:, h, 1:d + 1, 1:d + 1], sums, 0.25, None,
                                                      ALU.mult))
                dve.sem_inc(scaled_ready, 1)
                diagonals(i)
            for i, d in enumerate(sides):
                for k in range(9):
                    for h in range(HALVES):
                        shifted = padded[i][:, h, k // 3:k // 3 + d, k % 3:k % 3 + d]
                        tap = taps[:, i, h, 0, k:k + 1]
                        if k == 0:
                            step(nc.vector.tensor_scalar(dw_out[i][:, h, :, :], shifted, tap,
                                                         biases[:, i, h, 0:1], ALU.mult, ALU.add))
                            continue
                        step.wait(step.n - 1 + (h if k == 8 else 0))
                        done = nc.vector.scalar_tensor_tensor(dw_out[i][:, h, :, :], shifted, tap,
                                                              dw_out[i][:, h, :, :], ALU.mult, ALU.add)
                        if k < 8:
                            step(done)
                        else:
                            done.then_inc(dw_ready, 1)


def each_block(engine, blocks, body):
    if blocks == 1:
        body(0, 0, 0)
        return
    with engine.Fori(0, blocks // 2) as turn:
        for odd in range(2):
            body(engine.snap(turn * 2 + odd), odd, turn)


def project_scale(nc, i, plan, dw_scratch, pos_scratch, pw_wt, pw_b, q_scratch, k_scratch, v_scratch):
    width, blocks = plan.width, plan.blocks
    tiles = width // 128
    scale = (DIM // HEADS) ** -0.5
    with nc.cleanup_on_exit(), ExitStack() as ctx:
        def sb(what, shape, dt=F32):
            return ctx.enter_context(nc.sbuf_tensor(f"pj{i}_{what}", shape, dt))

        def sem(what):
            return nc.alloc_semaphore(f"pj{i}_{what}")

        weights = sb("weights", [128, HALVES, 3 * DIM])
        qk_bias = sb("qk_bias", [128, 4])
        v_bias = sb("v_bias", [128, DIM])
        conv = [sb(f"conv{k}", [128, HALVES, width]) for k in range(2)]
        pos = [sb(f"pos{k}", [128, HALVES, width]) for k in range(2)]
        whole = sb("whole", [128, 4, width])
        high = [sb(f"high{k}", [128, 4, width], F32R) for k in range(2)]
        low = [sb(f"low{k}", [128, 4, width], F32R) for k in range(2)]
        v_out = [sb(f"v_out{k}", [128, tiles, DIM]) for k in range(2)]
        qk_ps = [ctx.enter_context(nc.psum_tensor(f"pj{i}_qk{m}", [128, 512], F32)) for m in range(4)]
        v_ps = [ctx.enter_context(nc.psum_tensor(f"pj{i}_v{m}", [128, 512], F32)) for m in range(2)]

        weights_loaded = sem("weights_loaded")
        conv_loaded = [sem(f"conv_loaded{k}") for k in range(2)]
        pos_loaded = [sem(f"pos_loaded{k}") for k in range(2)]
        qk_ready = sem("qk_ready")
        v_ready = sem("v_ready")
        whole_ready = sem("whole_ready")
        high_ready = sem("high_ready")
        low_ready = sem("low_ready")
        v_copied = sem("v_copied")
        parts_stored = [sem(f"parts_stored{k}") for k in range(2)]
        v_stored = [sem(f"v_stored{k}") for k in range(2)]
        block = ctx.enter_context(nc.Block())
        v_groups = tiles // 2

        @block.sync
        def _(sp):
            sp.dma_start(weights[:, :, :], pw_wt[i].rearrange("(h p) n -> p h n", p=128)).then_inc(weights_loaded, 16)
            for m in range(4):
                sp.dma_start(qk_bias[:, m:m + 1], pw_b[i, m * 128:(m + 1) * 128, :]).then_inc(weights_loaded, 16)
            sp.dma_start(v_bias[:, :], pw_b[i, 2 * DIM:3 * DIM, 0].partition_broadcast(128))\
                .then_inc(weights_loaded, 16)

            def load(b, odd, turn):
                sp.wait_ge(v_copied, HEAD_START + b * v_groups)
                sp.dma_start(conv[odd][:, :, :],
                             dw_scratch[i].rearrange("h p (b n) -> b p h n", n=width)[b]).then_inc(conv_loaded[odd], 16)
                sp.dma_start(pos[odd][:, :, :],
                             pos_scratch[i].rearrange("h p (b n) -> b p h n", n=width)[b]).then_inc(pos_loaded[odd], 16)
            each_block(sp, blocks, load)

        @block.tensor
        def _(pe):
            pe.wait_ge(weights_loaded, 16 * 6)

            def products(b, odd, turn):
                pe.wait_ge(conv_loaded[odd], (turn + 1) * 16)
                for m in range(4):
                    pe.wait_ge(whole_ready, HEAD_START + b * 4)
                    for h in range(HALVES):
                        last = nc.tensor.matmul(qk_ps[m][:, 0:width], weights[:, h, m * 128:(m + 1) * 128],
                                                conv[odd][:, h, :], start=h == 0, stop=h == HALVES - 1)
                    last.then_inc(qk_ready, 1)
                for g in range(v_groups):
                    pe.wait_ge(v_copied, HEAD_START + (b + 1) * v_groups)
                    for t in range(2):
                        at = (2 * g + t) * 128
                        for h in range(HALVES):
                            last = nc.tensor.matmul(v_ps[g][:, t * DIM:(t + 1) * DIM], conv[odd][:, h, at:at + 128],
                                                    weights[:, h, 2 * DIM:3 * DIM], start=h == 0,
                                                    stop=h == HALVES - 1)
                    last.then_inc(v_ready, 1)
            each_block(pe, blocks, products)

        @block.vector
        def _(dve):
            dve.sem_inc(whole_ready, HEAD_START)
            dve.sem_inc(low_ready, HEAD_START)
            dve.sem_inc(v_copied, HEAD_START + v_groups)
            dve.wait_ge(weights_loaded, 16 * 6)

            def block_out(b, odd, turn):
                dve.wait_ge(pos_loaded[odd], (turn + 1) * 16)
                for m in range(4):
                    dve.wait_ge(qk_ready, b * 4 + (m + 1))
                    if m == 0:
                        dve.wait_ge(low_ready, HEAD_START + b * 4)
                        dve.wait_ge(high_ready, HEAD_START + b * 4)
                    nc.vector.scalar_tensor_tensor(whole[:, m, :], qk_ps[m][:, 0:width], qk_bias[:, m:m + 1],
                                                   pos[odd][:, m % 2, :], ALU.add, ALU.add)\
                        .then_inc(whole_ready, 1)
                dve.wait_ge(parts_stored[odd], HEAD_START + turn * 16 * 12)
                for m in range(4):
                    dve.wait_ge(high_ready, HEAD_START + b * 4 + (m + 1))
                    nc.vector.scalar_tensor_tensor(low[odd][:, m, :], whole[:, m, :], scale if m < 2 else 1.0,
                                                   high[odd][:, m, :].bitcast(F32), ALU.mult, ALU.subtract)\
                        .then_inc(low_ready, 1)
                dve.wait_ge(v_stored[odd], HEAD_START + turn * 16 * tiles)
                for g in range(v_groups):
                    dve.wait_ge(v_ready, b * v_groups + (g + 1))
                    nc.vector.tensor_tensor(v_out[odd][:, 2 * g:2 * g + 2, :],
                                            v_ps[g][:, :].rearrange("p (t c) -> p t c", t=2),
                                            v_bias[:, :].unsqueeze(1).to_broadcast([128, 2, DIM]), ALU.add)\
                        .then_inc(v_copied, 1)
            each_block(dve, blocks, block_out)

        @block.scalar
        def _(act):
            act.sem_inc(high_ready, HEAD_START)
            for stored in parts_stored:
                act.sem_inc(stored, HEAD_START)
            for stored in v_stored:
                act.sem_inc(stored, HEAD_START)
            q_view = q_scratch.rearrange("(h b) (s d) n -> b s h d n", b=blocks, s=3)
            k_view = k_scratch.rearrange("h (s d) (b n) -> b s h d n", s=3, n=width)
            v_view = v_scratch.rearrange("h p (b t) d -> b t p h d", t=tiles)


            def highs(b, odd, turn):
                act.wait_ge(parts_stored[odd], HEAD_START + turn * 16 * 12)
                for m in range(4):
                    act.wait_ge(whole_ready, HEAD_START + b * 4 + (m + 1))
                    nc.scalar.activation(high[odd][:, m, :], whole[:, m, :], ACT.Copy,
                                         scale=scale if m < 2 else 1.0).then_inc(high_ready, 1)
                act.wait_ge(low_ready, HEAD_START + (b + 1) * 4)
                for m in range(4):
                    view = q_view if m < 2 else k_view
                    for s, part in enumerate((high, high, low) if m < 2 else (high, low, high)):
                        act.dma_start(view[b, s, 4 * (m % 2):4 * (m % 2) + 4],
                                       part[odd][:, m, :].bitcast(F32)).then_inc(parts_stored[odd], 16)
                act.wait_ge(v_copied, HEAD_START + (b + 2) * v_groups)
                for t in range(tiles):
                    act.dma_start(v_view[b, t], v_out[odd][:, t, :].rearrange("p (h d) -> p h d", h=HEADS))\
                        .then_inc(v_stored[odd], 16)
            each_block(act, blocks, highs)
            for k in range(min(2, blocks)):
                act.wait_ge(parts_stored[k], HEAD_START + 16 * 12 * max(1, blocks // 2))
                act.wait_ge(v_stored[k], HEAD_START + 16 * tiles * max(1, blocks // 2))


def inverse_root(nc, dve, step, root_ready, number, value, root, work):
    dve.wait_ge(root_ready, number)
    step.link(nc.vector.reciprocal(root, root))
    step.link(nc.vector.tensor_tensor(work, root, root, ALU.mult))
    step.link(nc.vector.tensor_tensor(work, work, value, ALU.mult))
    step.link(nc.vector.tensor_scalar(work, work, -0.5, 1.5, ALU.mult, ALU.add))
    step.link(nc.vector.tensor_tensor(root, root, work, ALU.mult))


def fuse_coarse_scales(nc, plans, x, fusion_wt, fusion_b, att_scratch, base_scratch):
    with nc.cleanup_on_exit(), ExitStack() as ctx:
        def sb(what, shape, dt=F32):
            return ctx.enter_context(nc.sbuf_tensor(f"fc_{what}", shape, dt))

        def sem(what):
            return nc.alloc_semaphore(f"fc_{what}")

        coarse = [1, 2]
        tiles = {i: plans[i].tokens // 128 for i in coarse}
        tokens = {i: sb(f"tokens{i}", [128, tiles[i], DIM]) for i in coarse}
        channels = {i: sb(f"channels{i}", [128, HALVES, plans[i].tokens]) for i in coarse}
        fused = {i: sb(f"fused{i}", [128, HALVES, SIDE // SCALES[i], SIDE // SCALES[i]]) for i in coarse}
        wide = {i: sb(f"wide{i}", [128, HALVES, SIDE // SCALES[i], SIDE]) for i in coarse}
        weights = sb("weights", [128, 6, DIM])
        bias = sb("bias", [128, HALVES])
        base = sb("base", [128, HALVES, SIDE, SIDE])
        ident = sb("ident", [128, 128])
        turned_ps = [ctx.enter_context(nc.psum_tensor(f"fc_turned_ps{k}", [128, 512], F32)) for k in range(2)]
        fused_ps = [ctx.enter_context(nc.psum_tensor(f"fc_fused_ps{k}", [128, 512], F32)) for k in range(2)]

        loaded = sem("loaded")
        tokens_loaded = {i: sem(f"tokens{i}_loaded") for i in coarse}
        identity_made = sem("identity_made")
        turned = sem("turned")
        turned_copied = sem("turned_copied")
        fused_ready = sem("fused_ready")
        fused_copied = sem("fused_copied")
        steps = sem("steps")
        base_ready = sem("base_ready")
        stored = sem("stored")
        block = ctx.enter_context(nc.Block())

        pieces = [(i, t, min(4, tiles[i])) for i in coarse for t in range(0, tiles[i], 4)]

        @block.sync
        def _(sp):
            for i in coarse:
                p = plans[i]
                for h in range(HEADS):
                    for b in range(p.blocks):
                        sp.dma_start(tokens[i][:, b * p.q_tiles:(b + 1) * p.q_tiles, h * 32:(h + 1) * 32],
                                     att_scratch[i][h * p.blocks + b + 1].rearrange("p (t d) -> p t d", d=32))\
                            .then_inc(tokens_loaded[i], 16)
            sp.dma_start(base[:, :, :, :].rearrange("p h r c -> p h (r c)"),
                         x.rearrange("(h p) n -> p h n", p=128)).then_inc(loaded, 16)
            sp.dma_start(weights[:, :, :], fusion_wt.rearrange("(k p) n -> p k n", p=128)).then_inc(loaded, 16)
            for h in range(HALVES):
                sp.dma_start(bias[:, h:h + 1], fusion_b[h * 128:(h + 1) * 128, :]).then_inc(loaded, 16)
            for h in range(HALVES):
                sp.wait_ge(base_ready, h + 1)
                sp.dma_start(base_scratch[h], base[:, h, :, :].rearrange("p r c -> p (r c)")).then_inc(stored, 16)
            sp.wait_ge(stored, 32)

        @block.gpsimd
        def _(pool):
            make_identity(nc, pool, ident, identity_made)

        @block.tensor
        def _(pe):
            pe.wait_ge(identity_made, 2)
            n = 0
            for i, first, count in pieces:
                pe.wait_ge(tokens_loaded[i], 16 * HEADS * plans[i].blocks)
                for h in range(HALVES):
                    if n >= 2:
                        pe.wait_ge(turned_copied, n - 1)
                    for t in range(count):
                        last = nc.tensor.transpose(turned_ps[n % 2][:, t * 128:(t + 1) * 128],
                                                   tokens[i][:, first + t, h * 128:(h + 1) * 128], ident[:, :])
                    last.then_inc(turned, 1)
                    n += 1
            pe.wait_ge(turned_copied, n)
            pe.wait_ge(loaded, 64)
            n = 0
            for i, first, count in pieces:
                for m in range(HALVES):
                    if n >= 2:
                        pe.wait_ge(fused_copied, n - 1)
                    for h in range(HALVES):
                        last = nc.tensor.matmul(fused_ps[n % 2][:, 0:count * 128],
                                                weights[:, 2 * i + h, m * 128:(m + 1) * 128],
                                                channels[i][:, h, first * 128:(first + count) * 128],
                                                start=h == 0, stop=h == HALVES - 1)
                    last.then_inc(fused_ready, 1)
                    n += 1

        @block.scalar
        def _(act):
            n = 0
            for i, first, count in pieces:
                for h in range(HALVES):
                    act.wait_ge(turned, n + 1)
                    nc.scalar.activation(channels[i][:, h, first * 128:(first + count) * 128],
                                         turned_ps[n % 2][:, 0:count * 128], ACT.Copy).then_inc(turned_copied, 1)
                    n += 1
            n = 0
            for i, first, count in pieces:
                flat = fused[i][:, :, :, :].rearrange("p h r c -> p h (r c)")
                for m in range(HALVES):
                    act.wait_ge(fused_ready, n + 1)
                    nc.scalar.activation(flat[:, m, first * 128:(first + count) * 128],
                                         fused_ps[n % 2][:, 0:count * 128], ACT.Copy).then_inc(fused_copied, 1)
                    n += 1

        @block.vector
        def _(dve):
            step = Steps(dve, steps)
            dve.wait_ge(loaded, 64)
            for h in range(HALVES):
                step.link(nc.vector.tensor_scalar(base[:, h, :, :], base[:, h, :, :], bias[:, h:h + 1], None, ALU.add))
            dve.wait_ge(fused_copied, 2 * len(pieces))

            def phases(f):
                for r in range(f):
                    c = (r + 0.5) / f - 0.5
                    yield r, 1 - abs(c), abs(c), -1 if c < 0 else 1

            for h in range(HALVES):
                for i in coarse:
                    f = SCALES[i]
                    d = SIDE // f
                    source = fused[i][:, h, :, :]
                    columns = wide[i][:, h, :, :].rearrange("p r (c f) -> p r c f", f=f)
                    for r, near, far, side in phases(f):
                        step.link(nc.vector.tensor_scalar(columns[:, :, :, r], source, near, None, ALU.mult))
                        here, there = (slice(1, d), slice(0, d - 1)) if side < 0 else (slice(0, d - 1), slice(1, d))
                        edge = slice(0, 1) if side < 0 else slice(d - 1, d)
                        for to, of in ((here, there), (edge, edge)):
                            step.link(nc.vector.scalar_tensor_tensor(
                                columns[:, :, to, r], source[:, :, of], far, columns[:, :, to, r],
                                ALU.mult, ALU.add))
                    rows = base[:, h, :, :].rearrange("p (r f) c -> p r f c", f=f)
                    source = wide[i][:, h, :, :]
                    for r, near, far, side in phases(f):
                        here, there = (slice(1, d), slice(0, d - 1)) if side < 0 else (slice(0, d - 1), slice(1, d))
                        edge = slice(0, 1) if side < 0 else slice(d - 1, d)
                        for to, of, weight in ((slice(0, d), slice(0, d), near), (here, there, far),
                                               (edge, edge, far)):
                            step.link(nc.vector.scalar_tensor_tensor(
                                rows[:, to, r, :], source[:, of, :], weight, rows[:, to, r, :],
                                ALU.mult, ALU.add))
                dve.sem_inc(base_ready, 1)


TILES = BLOCK // 128
BLOCKS = TOKENS // BLOCK


def normed_tokens(nc, dve, step, tokens, normed, stats, moments, root, work, variance_ready, root_ready, number):
    for t in range(TILES):
        step(nc.vector.bn_stats(stats[:, t, :], tokens[:, t, :]))
    step.wait()
    mean, variance, apart, within = (moments[:, k, :] for k in range(4))
    step(nc.vector.tensor_tensor(mean, stats[:, :, 1], stats[:, :, 4], ALU.add))
    step(nc.vector.tensor_tensor(apart, stats[:, :, 1], stats[:, :, 4], ALU.subtract))
    step(nc.vector.tensor_tensor(within, stats[:, :, 2], stats[:, :, 5], ALU.add))
    step.wait()
    step(nc.vector.tensor_scalar(mean, mean, 0.5, None, ALU.mult))
    step.link(nc.vector.tensor_tensor(apart, apart, apart, ALU.mult))
    step.link(nc.vector.tensor_scalar(apart, apart, 0.25, 1e-5, ALU.mult, ALU.add))
    nc.vector.scalar_tensor_tensor(variance, within, 1.0 / DIM, apart, ALU.mult, ALU.add)\
        .then_inc(variance_ready, 1)
    inverse_root(nc, dve, step, root_ready, number, variance, root[:, :], work[:, :])
    for t in range(TILES):
        step(nc.vector.tensor_scalar(normed[:, t, :], tokens[:, t, :], moments[:, 0, t:t + 1], root[:, t:t + 1],
                                     ALU.subtract, ALU.mult))
    step.wait()


def fuse_fine_scale(nc, plan, fusion_wt, att_scratch, base_scratch, t1_scratch, n1_scratch):
    with nc.cleanup_on_exit(), ExitStack() as ctx:
        def sb(what, shape, dt=F32):
            return ctx.enter_context(nc.sbuf_tensor(f"ff_{what}", shape, dt))

        def sem(what):
            return nc.alloc_semaphore(f"ff_{what}")

        def pair(what, shape, dt=F32):
            return [sb(f"{what}{k}", shape, dt) for k in range(2)]

        weights = sb("weights", [128, HALVES, DIM])
        ident = sb("ident", [128, 128])
        att = pair("att", [128, TILES, DIM])
        base = pair("base", [128, HALVES, BLOCK])
        channels = pair("channels", [128, HALVES, BLOCK])
        tokens = pair("tokens", [128, TILES, DIM])
        normed = pair("normed", [128, TILES, DIM])
        turned = pair("turned", [128, HALVES, BLOCK])
        stats = sb("stats", [128, TILES, 6])
        moments = sb("moments", [128, 4, TILES])
        root = sb("root", [128, TILES])
        work = sb("work", [128, TILES])
        att_ps = [ctx.enter_context(nc.psum_tensor(f"ff_att_ps{k}", [128, 512], F32)) for k in range(2)]
        tokens_ps = [ctx.enter_context(nc.psum_tensor(f"ff_tokens_ps{k}", [128, 512], F32)) for k in range(2)]
        normed_ps = [ctx.enter_context(nc.psum_tensor(f"ff_normed_ps{k}", [128, 512], F32)) for k in range(2)]

        weights_loaded = sem("weights_loaded")
        identity_made = sem("identity_made")
        att_loaded = [sem(f"att_loaded{k}") for k in range(2)]
        base_loaded = [sem(f"base_loaded{k}") for k in range(2)]
        att_turned = sem("att_turned")
        att_copied = sem("att_copied")
        tokens_ready = sem("tokens_ready")
        tokens_copied = sem("tokens_copied")
        steps = sem("steps")
        variance_ready = sem("variance_ready")
        root_ready = sem("root_ready")
        normed_ready = sem("normed_ready")
        normed_turned = sem("normed_turned")
        normed_copied = sem("normed_copied")
        tokens_stored = [sem(f"tokens_stored{k}") for k in range(2)]
        turned_stored = [sem(f"turned_stored{k}") for k in range(2)]
        block = ctx.enter_context(nc.Block())

        @block.sync
        def _(sp):
            sp.dma_start(weights[:, :, :], fusion_wt[0:DIM, :].rearrange("(k p) n -> p k n", p=128))\
                .then_inc(weights_loaded, 16)
            view = att_scratch[1:plan.units + 1].rearrange("(h b) p (t d) -> h b p t d", b=plan.blocks, d=32)

            def load(b, odd, turn):
                sp.wait_ge(tokens_copied, HEAD_START + b * TILES)
                for h in range(HEADS):
                    sp.dma_start(att[odd][:, :, h * 32:(h + 1) * 32], view[h, b]).then_inc(att_loaded[odd], 16)
                sp.dma_start(base[odd][:, :, :], base_scratch.rearrange("h p (b n) -> b p h n", n=BLOCK)[b])\
                    .then_inc(base_loaded[odd], 16)
            each_block(sp, BLOCKS, load)

        @block.gpsimd
        def _(pool):
            make_identity(nc, pool, ident, identity_made)

        @block.tensor
        def _(pe):
            pe.wait_ge(identity_made, 2)
            pe.wait_ge(weights_loaded, 16)

            def products(b, odd, turn):
                pe.wait_ge(att_loaded[odd], (turn + 1) * 16 * HEADS)
                pe.wait_ge(att_copied, HEAD_START + b * HALVES)
                for h in range(HALVES):
                    for t in range(TILES):
                        last = nc.tensor.transpose(att_ps[h][:, t * 128:(t + 1) * 128],
                                                   att[odd][:, t, h * 128:(h + 1) * 128], ident[:, :])
                    last.then_inc(att_turned, 1)
                pe.wait_ge(att_copied, HEAD_START + (b + 1) * HALVES)
                pe.wait_ge(base_loaded[odd], (turn + 1) * 16)
                pe.wait_ge(tokens_copied, HEAD_START + (b + 1) * TILES)
                for t in range(TILES):
                    at = slice(t * 128, (t + 1) * 128)
                    out = tokens_ps[t // 2][:, (t % 2) * DIM:(t % 2 + 1) * DIM]
                    nc.tensor.matmul(out, channels[odd][:, 0, at], weights[:, 0, :], start=True, stop=False)
                    for h in range(HALVES):
                        nc.tensor.matmul(out[:, h * 128:(h + 1) * 128], base[odd][:, h, at], ident[:, :],
                                         start=False, stop=False, skip_group_check=True)
                    last = nc.tensor.matmul(out, channels[odd][:, 1, at], weights[:, 1, :], start=False, stop=True)
                    if t % 2:
                        last.then_inc(tokens_ready, 1)
                pe.wait_ge(normed_ready, b + 1)
                pe.wait_ge(normed_copied, HEAD_START + b * HALVES)
                for h in range(HALVES):
                    for t in range(TILES):
                        last = nc.tensor.transpose(normed_ps[h][:, t * 128:(t + 1) * 128],
                                                   normed[odd][:, t, h * 128:(h + 1) * 128], ident[:, :])
                    last.then_inc(normed_turned, 1)
            each_block(pe, BLOCKS, products)

        @block.scalar
        def _(act):
            act.sem_inc(att_copied, HEAD_START)
            act.sem_inc(normed_copied, HEAD_START)
            for stored in tokens_stored:
                act.sem_inc(stored, HEAD_START)
            for stored in turned_stored:
                act.sem_inc(stored, HEAD_START)
            def copies(b, odd, turn):
                for h in range(HALVES):
                    act.wait_ge(att_turned, b * HALVES + (h + 1))
                    nc.scalar.activation(channels[odd][:, h, :], att_ps[h][:, :], ACT.Copy).then_inc(att_copied, 1)
                act.wait_ge(variance_ready, b + 1)
                nc.scalar.activation(root[:, :], moments[:, 1, :], ACT.Sqrt).then_inc(root_ready, 1)
                act.wait_ge(turned_stored[odd], HEAD_START + turn * 16)
                for h in range(HALVES):
                    act.wait_ge(normed_turned, b * HALVES + (h + 1))
                    nc.scalar.activation(turned[odd][:, h, :], normed_ps[h][:, :], ACT.Copy)\
                        .then_inc(normed_copied, 1)
                act.wait_ge(tokens_copied, HEAD_START + (b + 2) * TILES)
                act.dma_start(t1_scratch[b], tokens[odd][:, :, :]).then_inc(tokens_stored[odd], 16)
                act.wait_ge(normed_copied, HEAD_START + (b + 1) * HALVES)
                act.dma_start(n1_scratch[b], turned[odd][:, :, :]).then_inc(turned_stored[odd], 16)
            each_block(act, BLOCKS, copies)
            for k in range(2):
                act.wait_ge(tokens_stored[k], HEAD_START + 16 * BLOCKS // 2)
                act.wait_ge(turned_stored[k], HEAD_START + 16 * BLOCKS // 2)

        @block.vector
        def _(dve):
            dve.sem_inc(tokens_copied, HEAD_START + TILES)

            def norm(b, odd, turn):
                step = Steps(dve, steps, b, 19)
                dve.wait_ge(tokens_stored[odd], HEAD_START + turn * 16)
                for t in range(TILES):
                    dve.wait_ge(tokens_ready, b * (TILES // 2) + (t // 2 + 1))
                    nc.vector.tensor_copy(tokens[odd][:, t, :], tokens_ps[t // 2][:, (t % 2) * DIM:(t % 2 + 1) * DIM])\
                        .then_inc(tokens_copied, 1)
                dve.wait_ge(tokens_copied, HEAD_START + (b + 2) * TILES)
                normed_tokens(nc, dve, step, tokens[odd], normed[odd], stats, moments, root, work, variance_ready,
                              root_ready, b + 1)
                assert step.n == step.per_turn
                dve.sem_inc(normed_ready, 1)
            each_block(dve, BLOCKS, norm)


MAPS = 16
MAP_DIM = 16
LAMBDA_INIT = 0.8 - 0.6 * math.exp(-0.3)
HIDDEN = 4 * DIM


def project_tokens(nc, n1_scratch, wqk, wvg, bg, q_scratch, k_scratch, v_scratch, gate_scratch):
    scale = MAP_DIM ** -0.5
    with nc.cleanup_on_exit(), ExitStack() as ctx:
        def sb(what, shape, dt=F32):
            return ctx.enter_context(nc.sbuf_tensor(f"pt_{what}", shape, dt))

        def sem(what):
            return nc.alloc_semaphore(f"pt_{what}")

        def pair(what, shape, dt=F32):
            return [sb(f"{what}{k}", shape, dt) for k in range(2)]

        qk_weights = sb("qk_weights", [128, HALVES, 2 * DIM])
        vg_weights = sb("vg_weights", [128, HALVES, 2 * DIM])
        gate_bias = sb("gate_bias", [128, DIM])
        normed = pair("normed", [128, HALVES, BLOCK])
        high = pair("high", [128, 4, BLOCK], F32R)
        low = pair("low", [128, 4, BLOCK], F32R)
        value_mean = pair("value_mean", [128, TILES, HEADS])
        centred = pair("centred", [128, TILES, HEADS, 32])
        raw_gates = pair("raw_gates", [128, TILES, DIM])
        gates = pair("gates", [128, TILES, DIM])
        qk_ps = [ctx.enter_context(nc.psum_tensor(f"pt_qk{m}", [128, 512], F32)) for m in range(4)]
        vg_ps = [ctx.enter_context(nc.psum_tensor(f"pt_vg{m}", [128, 512], F32)) for m in range(4)]

        weights_loaded = sem("weights_loaded")
        normed_loaded = [sem(f"normed_loaded{k}") for k in range(2)]
        qk_ready = sem("qk_ready")
        vg_ready = sem("vg_ready")
        high_ready = sem("high_ready")
        low_ready = sem("low_ready")
        mean_ready = sem("mean_ready")
        values_ready = sem("values_ready")
        raw_gates_ready = sem("raw_gates_ready")
        gates_ready = sem("gates_ready")
        parts_stored = [sem(f"parts_stored{k}") for k in range(2)]
        values_stored = [sem(f"values_stored{k}") for k in range(2)]
        gates_stored = [sem(f"gates_stored{k}") for k in range(2)]
        block = ctx.enter_context(nc.Block())

        @block.sync
        def _(sp):
            sp.dma_start(qk_weights[:, :, :], wqk.rearrange("(k p) n -> p k n", p=128)).then_inc(weights_loaded, 16)
            sp.dma_start(vg_weights[:, :, :], wvg.rearrange("(k p) n -> p k n", p=128)).then_inc(weights_loaded, 16)
            sp.dma_start(gate_bias[:, :], bg.partition_broadcast(128)).then_inc(weights_loaded, 16)

            def load(b, odd, turn):
                sp.wait_ge(raw_gates_ready, HEAD_START + b * TILES)
                sp.dma_start(normed[odd][:, :, :], n1_scratch[b]).then_inc(normed_loaded[odd], 16)
            each_block(sp, BLOCKS, load)

        @block.tensor
        def _(pe):
            pe.wait_ge(weights_loaded, 48)

            def products(b, odd, turn):
                pe.wait_ge(normed_loaded[odd], (turn + 1) * 16)
                pe.wait_ge(low_ready, HEAD_START + b * 4)
                for m in range(4):
                    for h in range(HALVES):
                        last = nc.tensor.matmul(qk_ps[m][:, :], qk_weights[:, h, m * 128:(m + 1) * 128],
                                                normed[odd][:, h, :], start=h == 0, stop=h == HALVES - 1)
                    last.then_inc(qk_ready, 1)
                pe.wait_ge(raw_gates_ready, HEAD_START + (b + 1) * TILES)
                for t in range(TILES):
                    for h in range(HALVES):
                        last = nc.tensor.matmul(vg_ps[t][:, :], normed[odd][:, h, t * 128:(t + 1) * 128],
                                                vg_weights[:, h, :], start=h == 0, stop=h == HALVES - 1)
                    last.then_inc(vg_ready, 1)
            each_block(pe, BLOCKS, products)

        @block.vector
        def _(dve):
            dve.sem_inc(low_ready, HEAD_START)
            dve.sem_inc(raw_gates_ready, HEAD_START + TILES)
            dve.wait_ge(weights_loaded, 48)

            def sums(b, odd, turn):
                dve.wait_ge(parts_stored[odd], HEAD_START + turn * 16 * 12)
                for m in range(4):
                    dve.wait_ge(high_ready, b * 4 + (m + 1))
                    nc.vector.scalar_tensor_tensor(low[odd][:, m, :], qk_ps[m][:, :], scale if m < 2 else 1.0,
                                                   high[odd][:, m, :].bitcast(F32), ALU.mult, ALU.subtract)\
                        .then_inc(low_ready, 1)
                dve.wait_ge(values_stored[odd], HEAD_START + turn * 16 * TILES)
                for t in range(TILES):
                    values = vg_ps[t][:, 0:DIM].rearrange("p (h d) -> p h d", d=32)
                    dve.wait_ge(vg_ready, b * TILES + (t + 1))
                    nc.vector.tensor_reduce(value_mean[odd][:, t, :], values, AX.X, ALU.add).then_inc(mean_ready, 1)
                    if t == 0:
                        dve.wait_ge(gates_ready, HEAD_START + b)
                    dve.wait_ge(mean_ready, 2 * (b * TILES + t) + 1)
                    nc.vector.tensor_scalar(value_mean[odd][:, t, :], value_mean[odd][:, t, :], 1.0 / 32, None,
                                            ALU.mult).then_inc(mean_ready, 1)
                    dve.wait_ge(mean_ready, 2 * (b * TILES + t) + 2)
                    nc.vector.tensor_tensor(
                        centred[odd][:, t, :, :], values,
                        value_mean[odd][:, t, :].unsqueeze(2).to_broadcast([128, HEADS, 32]), ALU.subtract)\
                        .then_inc(values_ready, 1)
                    nc.vector.tensor_tensor(raw_gates[odd][:, t, :], vg_ps[t][:, DIM:2 * DIM], gate_bias[:, :],
                                            ALU.add).then_inc(raw_gates_ready, 1)
            each_block(dve, BLOCKS, sums)

        @block.scalar
        def _(act):
            for stored in parts_stored:
                act.sem_inc(stored, HEAD_START)
            for stored in values_stored:
                act.sem_inc(stored, HEAD_START)
            for stored in gates_stored:
                act.sem_inc(stored, HEAD_START)
            act.sem_inc(gates_ready, HEAD_START)
            q_view = q_scratch.rearrange("(h b) (s d) n -> b s h d n", b=BLOCKS, s=3)
            k_view = k_scratch.rearrange("h (s d) (b n) -> b s h d n", s=3, n=BLOCK)
            v_view = v_scratch.rearrange("h p (b t) d -> b t p h d", t=TILES)

            def parts(b, odd, turn):
                act.wait_ge(parts_stored[odd], HEAD_START + turn * 16 * 12)
                for m in range(4):
                    act.wait_ge(qk_ready, b * 4 + (m + 1))
                    nc.scalar.activation(high[odd][:, m, :], qk_ps[m][:, :], ACT.Copy,
                                         scale=scale if m < 2 else 1.0).then_inc(high_ready, 1)
                act.wait_ge(low_ready, HEAD_START + (b + 1) * 4)
                for m in range(4):
                    view = q_view if m < 2 else k_view
                    for s, part in enumerate((high, high, low) if m < 2 else (high, low, high)):
                        act.dma_start(view[b, s, 8 * (m % 2):8 * (m % 2) + 8],
                                      part[odd][:, m, :].bitcast(F32)).then_inc(parts_stored[odd], 16)
                act.wait_ge(raw_gates_ready, HEAD_START + (b + 2) * TILES)
                act.wait_ge(gates_stored[odd], HEAD_START + turn * 16)
                nc.scalar.activation(gates[odd][:, :, :], raw_gates[odd][:, :, :], ACT.Sigmoid)\
                    .then_inc(gates_ready, 1)
                act.wait_ge(values_ready, (b + 1) * TILES)
                for t in range(TILES):
                    act.dma_start(v_view[b, t], centred[odd][:, t, :, 0:31]).then_inc(values_stored[odd], 16)
                act.wait_ge(gates_ready, HEAD_START + b + 1)
                act.dma_start(gate_scratch[b], gates[odd][:, :, :]).then_inc(gates_stored[odd], 16)
            each_block(act, BLOCKS, parts)
            for k in range(2):
                act.wait_ge(parts_stored[k], HEAD_START + 16 * 12 * BLOCKS // 2)
                act.wait_ge(values_stored[k], HEAD_START + 16 * TILES * BLOCKS // 2)
                act.wait_ge(gates_stored[k], HEAD_START + 16 * BLOCKS // 2)


def finish_attention(nc, plan, att_scratch, gate_scratch, t1_scratch, lambdas, gamma, beta, w_out, b_out, w_route,
                     b_route, n2_scratch, sum_scratch, route_scratch):
    with nc.cleanup_on_exit(), ExitStack() as ctx:
        def sb(what, shape, dt=F32):
            return ctx.enter_context(nc.sbuf_tensor(f"fa_{what}", shape, dt))

        def sem(what):
            return nc.alloc_semaphore(f"fa_{what}")

        def pair(what, shape, dt=F32):
            return [sb(f"{what}{k}", shape, dt) for k in range(2)]

        rows = TILES * HEADS
        weights = sb("weights", [128, HALVES, DIM])
        ident = sb("ident", [128, 128])
        out_bias = sb("out_bias", [128, DIM])
        route_weights = sb("route_weights", [128, DIM])
        route_bias = sb("route_bias", [128, 1])
        head_scale = sb("head_scale", [128, 32])
        head_shift = sb("head_shift", [128, 32])
        vectors = sb("vectors", [128, 4, MAP_DIM])
        dots = sb("dots", [128, 2])
        dot_junk = sb("dot_junk", [128, MAP_DIM])
        powers = sb("powers", [128, 2])
        minus_lambda = sb("minus_lambda", [128, 1])
        maps = pair("maps", [128, rows, 2, 32])
        t1 = pair("t1", [128, TILES, DIM])
        gates = pair("gates", [128, TILES, DIM])
        heads = sb("heads", [128, rows, 32])
        squares = sb("squares", [128, rows, 32])
        variance = sb("variance", [128, rows])
        head_root = sb("head_root", [128, rows])
        head_work = sb("head_work", [128, rows])
        channels = sb("channels", [128, HALVES, BLOCK])
        tokens = sb("tokens", [128, TILES, DIM])
        normed = sb("normed", [128, TILES, DIM])
        junk = sb("junk", [128, DIM])
        total = pair("total", [128, TILES, DIM])
        turned = pair("turned", [128, HALVES, BLOCK])
        stats = sb("stats", [128, TILES, 6])
        moments = sb("moments", [128, 4, TILES])
        root = sb("root", [128, TILES])
        work = sb("work", [128, TILES])
        routed = sb("routed", [128, TILES])
        route = pair("route", [128, TILES])
        heads_ps = [ctx.enter_context(nc.psum_tensor(f"fa_heads_ps{k}", [128, 512], F32)) for k in range(2)]
        tokens_ps = [ctx.enter_context(nc.psum_tensor(f"fa_tokens_ps{k}", [128, 512], F32)) for k in range(2)]
        normed_ps = [ctx.enter_context(nc.psum_tensor(f"fa_normed_ps{k}", [128, 512], F32)) for k in range(2)]

        weights_loaded = sem("weights_loaded")
        identity_made = sem("identity_made")
        dots_ready = sem("dots_ready")
        powers_ready = sem("powers_ready")
        maps_loaded = [sem(f"maps_loaded{k}") for k in range(2)]
        t1_loaded = [sem(f"t1_loaded{k}") for k in range(2)]
        gates_loaded = [sem(f"gates_loaded{k}") for k in range(2)]
        const_steps = sem("const_steps")
        steps = sem("steps")
        heads_variance_ready = sem("heads_variance_ready")
        heads_root_ready = sem("heads_root_ready")
        heads_ready = sem("heads_ready")
        heads_turned = sem("heads_turned")
        heads_copied = sem("heads_copied")
        tokens_ready = sem("tokens_ready")
        variance_ready = sem("variance_ready")
        root_ready = sem("root_ready")
        normed_ready = sem("normed_ready")
        normed_turned = sem("normed_turned")
        normed_copied = sem("normed_copied")
        total_ready = sem("total_ready")
        turned_stored = [sem(f"turned_stored{k}") for k in range(2)]
        total_stored = [sem(f"total_stored{k}") for k in range(2)]
        route_stored = [sem(f"route_stored{k}") for k in range(2)]
        block = ctx.enter_context(nc.Block())

        @block.sync
        def _(sp):
            for k in range(4):
                sp.dma_start(vectors[:, k, :], lambdas[k].partition_broadcast(128)).then_inc(weights_loaded, 16)
            sp.dma_start(head_scale[:, :], gamma.partition_broadcast(128)).then_inc(weights_loaded, 16)
            sp.dma_start(head_shift[:, :], beta.partition_broadcast(128)).then_inc(weights_loaded, 16)
            sp.dma_start(weights[:, :, :], w_out.rearrange("(k p) n -> p k n", p=128)).then_inc(weights_loaded, 16)
            sp.dma_start(out_bias[:, :], b_out.partition_broadcast(128)).then_inc(weights_loaded, 16)
            sp.dma_start(route_weights[:, :], w_route.partition_broadcast(128)).then_inc(weights_loaded, 16)
            sp.dma_start(route_bias[:, :], b_route.partition_broadcast(128)).then_inc(weights_loaded, 16)
            view = att_scratch[1:plan.units + 1].rearrange("(h b) p (t d) -> h b p t d", b=BLOCKS, d=32)

            def load(b, odd, turn):
                sp.wait_ge(total_ready, HEAD_START + b)
                for a in range(MAPS):
                    sp.dma_start(maps[odd][:, :, a % 2, :].rearrange("p (t h) d -> p t h d", h=HEADS)[:, :, a // 2, :],
                                 view[a, b]).then_inc(maps_loaded[odd], 16)
                sp.dma_start(t1[odd][:, :, :], t1_scratch[b]).then_inc(t1_loaded[odd], 16)
                sp.dma_start(gates[odd][:, :, :], gate_scratch[b]).then_inc(gates_loaded[odd], 16)
            each_block(sp, BLOCKS, load)

        @block.gpsimd
        def _(pool):
            make_identity(nc, pool, ident, identity_made)

        @block.tensor
        def _(pe):
            pe.wait_ge(identity_made, 2)
            pe.wait_ge(weights_loaded, 160)

            def products(b, odd, turn):
                pe.wait_ge(heads_ready, b + 1)
                view = heads[:, :, :].rearrange("p (t h) d -> p t (h d)", h=HEADS)
                for h in range(HALVES):
                    for t in range(TILES):
                        last = nc.tensor.transpose(heads_ps[h][:, t * 128:(t + 1) * 128],
                                                   view[:, t, h * 128:(h + 1) * 128], ident[:, :])
                    last.then_inc(heads_turned, 1)
                pe.wait_ge(heads_copied, HEAD_START + (b + 1) * HALVES)
                for t in range(TILES):
                    out = tokens_ps[t // 2][:, (t % 2) * DIM:(t % 2 + 1) * DIM]
                    for h in range(HALVES):
                        last = nc.tensor.matmul(out, channels[:, h, t * 128:(t + 1) * 128], weights[:, h, :],
                                                start=h == 0, stop=h == HALVES - 1)
                    if t % 2:
                        last.then_inc(tokens_ready, 1)
                pe.wait_ge(normed_ready, b + 1)
                pe.wait_ge(normed_copied, HEAD_START + b * HALVES)
                for h in range(HALVES):
                    for t in range(TILES):
                        last = nc.tensor.transpose(normed_ps[h][:, t * 128:(t + 1) * 128],
                                                   normed[:, t, h * 128:(h + 1) * 128], ident[:, :])
                    last.then_inc(normed_turned, 1)
            each_block(pe, BLOCKS, products)

        @block.scalar
        def _(act):
            act.sem_inc(normed_copied, HEAD_START)
            for stored in turned_stored:
                act.sem_inc(stored, HEAD_START)
            act.sem_inc(heads_copied, HEAD_START)
            for stored in route_stored:
                act.sem_inc(stored, HEAD_START)
            for stored in total_stored:
                act.sem_inc(stored, HEAD_START)
            act.wait_ge(dots_ready, 2)
            nc.scalar.activation(powers[:, :], dots[:, :], ACT.Exp).then_inc(powers_ready, 1)

            def copies(b, odd, turn):
                act.wait_ge(heads_variance_ready, b + 1)
                nc.scalar.activation(head_root[:, :], variance[:, :], ACT.Sqrt).then_inc(heads_root_ready, 1)
                for h in range(HALVES):
                    act.wait_ge(heads_turned, b * HALVES + (h + 1))
                    nc.scalar.activation(channels[:, h, :], heads_ps[h][:, :], ACT.Copy).then_inc(heads_copied, 1)
                act.wait_ge(variance_ready, b + 1)
                nc.scalar.activation(root[:, :], moments[:, 1, :], ACT.Sqrt).then_inc(root_ready, 1)
                act.wait_ge(turned_stored[odd], HEAD_START + turn * 16)
                for h in range(HALVES):
                    act.wait_ge(normed_turned, b * HALVES + (h + 1))
                    nc.scalar.activation(turned[odd][:, h, :], normed_ps[h][:, :], ACT.Copy)\
                        .then_inc(normed_copied, 1)
                act.wait_ge(total_ready, HEAD_START + b + 2)
                act.dma_start(sum_scratch[b], total[odd][:, :, :]).then_inc(total_stored[odd], 16)
                act.dma_start(route_scratch[b], route[odd][:, :]).then_inc(route_stored[odd], 16)
                act.wait_ge(normed_copied, HEAD_START + (b + 1) * HALVES)
                act.dma_start(n2_scratch[b], turned[odd][:, :, :]).then_inc(turned_stored[odd], 16)
            each_block(act, BLOCKS, copies)
            for k in range(2):
                act.wait_ge(turned_stored[k], HEAD_START + 16 * BLOCKS // 2)
                act.wait_ge(total_stored[k], HEAD_START + 16 * BLOCKS // 2)
                act.wait_ge(route_stored[k], HEAD_START + 16 * BLOCKS // 2)

        @block.vector
        def _(dve):
            dve.sem_inc(total_ready, HEAD_START + 1)
            dve.wait_ge(weights_loaded, 160)
            const = Steps(dve, const_steps)
            for k in range(2):
                nc.vector.tensor_tensor_reduce(out=dot_junk[:, :], in0=vectors[:, 2 * k, :],
                                               in1=vectors[:, 2 * k + 1, :], scale=1.0, scalar=0.0, op0=ALU.mult,
                                               op1=ALU.add, accum_out=dots[:, k:k + 1]).then_inc(dots_ready, 1)
                dve.wait_ge(dots_ready, k + 1)
            dve.wait_ge(powers_ready, 1)
            const.link(nc.vector.tensor_tensor(minus_lambda[:, :], powers[:, 1:2], powers[:, 0:1], ALU.subtract))
            const.link(nc.vector.tensor_scalar(minus_lambda[:, :], minus_lambda[:, :], -LAMBDA_INIT, None, ALU.add))
            const.link(nc.vector.tensor_scalar(head_scale[:, :], head_scale[:, :], 1 - LAMBDA_INIT, None, ALU.mult))
            const.link(nc.vector.tensor_scalar(head_shift[:, :], head_shift[:, :], 1 - LAMBDA_INIT, None, ALU.mult))

            def finish(b, odd, turn):
                step = Steps(dve, steps, b, 39)
                dve.wait_ge(maps_loaded[odd], (turn + 1) * 16 * MAPS)
                dve.wait_ge(heads_copied, HEAD_START + b * HALVES)
                step.link(nc.vector.scalar_tensor_tensor(heads[:, :, 0:31], maps[odd][:, :, 1, 0:31],
                                                         minus_lambda[:, 0:1], maps[odd][:, :, 0, 0:31],
                                                         ALU.mult, ALU.add))
                step.link(nc.vector.tensor_reduce(heads[:, :, 31], heads[:, :, 0:31], AX.X, ALU.add, negate=True))
                step.link(nc.vector.tensor_tensor(squares[:, :, :], heads[:, :, :], heads[:, :, :], ALU.mult))
                step.link(nc.vector.tensor_reduce(variance[:, :], squares[:, :, :], AX.X, ALU.add))
                nc.vector.tensor_scalar(variance[:, :], variance[:, :], 1.0 / 32, 1e-5, ALU.mult, ALU.add)\
                    .then_inc(heads_variance_ready, 1)
                inverse_root(nc, dve, step, heads_root_ready, b + 1, variance[:, :], head_root[:, :],
                             head_work[:, :])
                step.link(nc.vector.tensor_tensor(heads[:, :, :], heads[:, :, :],
                                                  head_root[:, :].unsqueeze(2).to_broadcast([128, rows, 32]),
                                                  ALU.mult))
                step.link(nc.vector.tensor_tensor(heads[:, :, :], heads[:, :, :],
                                                  head_scale[:, :].unsqueeze(1).to_broadcast([128, rows, 32]),
                                                  ALU.mult))
                step.link(nc.vector.tensor_tensor(heads[:, :, :], heads[:, :, :],
                                                  head_shift[:, :].unsqueeze(1).to_broadcast([128, rows, 32]),
                                                  ALU.add))
                dve.wait_ge(gates_loaded[odd], (turn + 1) * 16)
                nc.vector.tensor_tensor(heads[:, :, :].rearrange("p r d -> p (r d)"),
                                        heads[:, :, :].rearrange("p r d -> p (r d)"),
                                        gates[odd][:, :, :].rearrange("p t c -> p (t c)"), ALU.mult)\
                    .then_inc(heads_ready, 1)
                dve.wait_ge(t1_loaded[odd], (turn + 1) * 16)
                step.link(nc.vector.tensor_tensor(t1[odd][:, :, :], t1[odd][:, :, :],
                                                  out_bias[:, :].unsqueeze(1).to_broadcast([128, TILES, DIM]),
                                                  ALU.add))
                for k in range(2):
                    dve.wait_ge(tokens_ready, b * 2 + (k + 1))
                    step(nc.vector.tensor_tensor(tokens[:, 2 * k:2 * k + 2, :],
                                                 tokens_ps[k][:, :].rearrange("p (t c) -> p t c", t=2),
                                                 t1[odd][:, 2 * k:2 * k + 2, :], ALU.add))
                step.wait()
                dve.wait_ge(normed_copied, HEAD_START + b * HALVES)
                normed_tokens(nc, dve, step, tokens, normed, stats, moments, root, work, variance_ready,
                              root_ready, b + 1)
                dve.sem_inc(normed_ready, 1)
                for t in range(TILES):
                    step.link(nc.vector.tensor_tensor_reduce(
                        out=junk[:, :], in0=normed[:, t, :], in1=route_weights[:, :], scale=1.0, scalar=0.0,
                        op0=ALU.mult, op1=ALU.add, accum_out=routed[:, t:t + 1]))
                dve.wait_ge(route_stored[odd], HEAD_START + turn * 16)
                dve.wait_ge(total_stored[odd], HEAD_START + turn * 16)
                step.link(nc.vector.tensor_scalar(route[odd][:, :], routed[:, :], route_bias[:, 0:1], None,
                                                  ALU.add))
                nc.vector.tensor_tensor(total[odd][:, :, :], tokens[:, :, :], normed[:, :, :], ALU.add)\
                    .then_inc(total_ready, 1)
                assert step.n == step.per_turn, step.n
            each_block(dve, BLOCKS, finish)


def feed_forward(nc, n2_scratch, sum_scratch, route_scratch, route_rows, w1, b1, w2, b2, out):
    kept = TOKENS // 2 - 1
    hidden_tiles = HIDDEN // 128
    with nc.cleanup_on_exit(), ExitStack() as ctx:
        def sb(what, shape, dt=F32):
            return ctx.enter_context(nc.sbuf_tensor(f"fn_{what}", shape, dt))

        def sem(what):
            return nc.alloc_semaphore(f"fn_{what}")

        def pair(what, shape, dt=F32):
            return [sb(f"{what}{k}", shape, dt) for k in range(2)]

        up = sb("up", [128, HALVES, HIDDEN])
        down = sb("down", [128, hidden_tiles, DIM])
        up_bias = sb("up_bias", [128, hidden_tiles])
        down_bias = sb("down_bias", [128, DIM])
        ident = sb("ident", [128, 128])
        earlier = sb("earlier", [128, 128])
        normed = pair("normed", [128, HALVES, BLOCK])
        total = pair("total", [128, TILES, DIM])
        hidden = sb("hidden", [128, hidden_tiles, BLOCK])
        all_routes = sb("all_routes", [128, TOKENS])
        route = sb("route", [128, BLOCKS * TILES])
        compared = sb("compared", [128, TOKENS])
        counts = sb("counts", [128, BLOCKS * TILES, 4])
        rank = sb("rank", [128, BLOCKS * TILES, 3])
        share = sb("share", [128, BLOCKS * TILES])
        result = sb("result", [128, TILES, DIM])
        turned = pair("turned", [128, HALVES, BLOCK])
        hidden_ps = [ctx.enter_context(nc.psum_tensor(f"fn_hidden_ps{k}", [128, 512], F32)) for k in range(2)]
        result_ps = [ctx.enter_context(nc.psum_tensor(f"fn_result_ps{k}", [128, 512], F32)) for k in range(2)]
        turned_ps = [ctx.enter_context(nc.psum_tensor(f"fn_turned_ps{k}", [128, 512], F32)) for k in range(2)]

        weights_loaded = sem("weights_loaded")
        routes_written = sem("routes_written")
        routes_loaded = sem("routes_loaded")
        identity_made = sem("identity_made")
        earlier_made = sem("earlier_made")
        normed_loaded = [sem(f"normed_loaded{k}") for k in range(2)]
        total_loaded = [sem(f"total_loaded{k}") for k in range(2)]
        up_ready = sem("up_ready")
        hidden_ready = sem("hidden_ready")
        down_ready = sem("down_ready")
        counted = sem("counted")
        ranked = sem("ranked")
        steps = sem("steps")
        result_ready = sem("result_ready")
        turned_ready = sem("turned_ready")
        turned_copied = sem("turned_copied")
        out_stored = [sem(f"out_stored{k}") for k in range(2)]
        block = ctx.enter_context(nc.Block())

        @block.sync
        def _(sp):
            with nc.allow_non_contiguous_dma(reason="4096 words in all"):
                for b in range(BLOCKS):
                    sp.dma_start(route_rows[b].rearrange("(t p) -> p t", p=128), route_scratch[b])\
                        .then_inc(routes_written, 16)
            sp.dma_start(up[:, :, :], w1.rearrange("(k p) n -> p k n", p=128)).then_inc(weights_loaded, 16)
            sp.dma_start(down[:, :, :], w2.rearrange("(k p) n -> p k n", p=128)).then_inc(weights_loaded, 16)
            for m in range(hidden_tiles):
                sp.dma_start(up_bias[:, m:m + 1], b1[m * 128:(m + 1) * 128, :]).then_inc(weights_loaded, 16)
            sp.dma_start(down_bias[:, :], b2.partition_broadcast(128)).then_inc(weights_loaded, 16)
            sp.wait_ge(routes_written, 16 * BLOCKS)
            sp.dma_start(all_routes[:, :], route_rows.rearrange("b n -> (b n)").partition_broadcast(128))\
                .then_inc(routes_loaded, 16)
            sp.dma_start(route[:, :].rearrange("p (b t) -> p b t", t=TILES),
                         route_scratch.rearrange("b p t -> p b t")).then_inc(routes_loaded, 16)

            def load(b, odd, turn):
                sp.wait_ge(result_ready, HEAD_START + b)
                sp.dma_start(normed[odd][:, :, :], n2_scratch[b]).then_inc(normed_loaded[odd], 16)
                sp.dma_start(total[odd][:, :, :], sum_scratch[b]).then_inc(total_loaded[odd], 16)
            each_block(sp, BLOCKS, load)

        @block.gpsimd
        def _(pool):
            make_identity(nc, pool, ident, identity_made)
            nc.gpsimd.memset(earlier[:, :], 1.0).then_inc(earlier_made, 1)
            pool.wait_ge(earlier_made, 1)
            nc.gpsimd.affine_select(out=earlier[:, :], in_=earlier[:, :], compare_op=ALU.is_gt, fill=0.0, base=0,
                                    pattern=[[-1, 128]], channel_multiplier=1).then_inc(earlier_made, 1)

        @block.tensor
        def _(pe):
            pe.sem_inc(down_ready, HEAD_START)
            pe.wait_ge(identity_made, 2)
            pe.wait_ge(weights_loaded, 16 * (3 + hidden_tiles))

            def products(b, odd, turn):
                pe.wait_ge(normed_loaded[odd], (turn + 1) * 16)
                for m in range(hidden_tiles):
                    pe.wait_ge(hidden_ready, HEAD_START + b * hidden_tiles + m)
                    for h in range(HALVES):
                        last = nc.tensor.matmul(hidden_ps[m % 2][:, :], up[:, h, m * 128:(m + 1) * 128],
                                                normed[odd][:, h, :], start=h == 0, stop=h == HALVES - 1)
                    last.then_inc(up_ready, 1)
                pe.wait_ge(hidden_ready, HEAD_START + (b + 1) * hidden_tiles + 1)
                pe.wait_ge(result_ready, HEAD_START + b + 1)
                for t in range(TILES):
                    for m in range(hidden_tiles):
                        last = nc.tensor.matmul(result_ps[t // 2][:, (t % 2) * DIM:(t % 2 + 1) * DIM],
                                                hidden[:, m, t * 128:(t + 1) * 128], down[:, m, :],
                                                start=m == 0, stop=m == hidden_tiles - 1)
                    if t % 2:
                        last.then_inc(down_ready, 1)
                pe.wait_ge(result_ready, HEAD_START + b + 2)
                pe.wait_ge(turned_copied, HEAD_START + b * HALVES)
                for h in range(HALVES):
                    for t in range(TILES):
                        last = nc.tensor.transpose(turned_ps[h][:, t * 128:(t + 1) * 128],
                                                   result[:, t, h * 128:(h + 1) * 128], ident[:, :])
                    last.then_inc(turned_ready, 1)
            each_block(pe, BLOCKS, products)

        @block.scalar
        def _(act):
            act.sem_inc(turned_copied, HEAD_START)
            for stored in out_stored:
                act.sem_inc(stored, HEAD_START)
            act.wait_ge(weights_loaded, 16 * (3 + hidden_tiles))
            act.sem_inc(hidden_ready, HEAD_START + 1)
            out_view = out.rearrange("(h p) (b n) -> b p h n", p=128, n=BLOCK)

            def activations(b, odd, turn):
                for m in range(hidden_tiles):
                    act.wait_ge(up_ready, b * hidden_tiles + (m + 1))
                    if m == 0:
                        act.wait_ge(down_ready, HEAD_START + b * 2)
                    nc.scalar.activation(hidden[:, m, :], hidden_ps[m % 2][:, :], ACT.Gelu_apprx_tanh,
                                         bias=up_bias[:, m:m + 1]).then_inc(hidden_ready, 1)
                act.wait_ge(out_stored[odd], HEAD_START + turn * 16)
                for h in range(HALVES):
                    act.wait_ge(turned_ready, b * HALVES + (h + 1))
                    nc.scalar.activation(turned[odd][:, h, :], turned_ps[h][:, :], ACT.Copy)\
                        .then_inc(turned_copied, 1)
                act.wait_ge(turned_copied, HEAD_START + (b + 1) * HALVES)
                act.dma_start(out_view[b], turned[odd][:, :, :]).then_inc(out_stored[odd], 16)
            each_block(act, BLOCKS, activations)
            for k in range(2):
                act.wait_ge(out_stored[k], HEAD_START + 16 * BLOCKS // 2)

        @block.vector
        def _(dve):
            dve.sem_inc(result_ready, HEAD_START + 1)
            step = Steps(dve, steps)
            dve.wait_ge(routes_loaded, 32)
            dve.wait_ge(earlier_made, 2)
            dve.wait_ge(weights_loaded, 16 * (3 + hidden_tiles))
            step(nc.vector.memset(counts[:, :, :], 0.0))
            step.wait()

            def count_ahead(n):
                mine = route[:, n:n + 1]
                tile = slice(n * 128, (n + 1) * 128)
                for k, (part, op) in enumerate(((slice(0, n * 128), ALU.is_ge),
                                                (slice((n + 1) * 128, TOKENS), ALU.is_gt), (tile, ALU.is_gt))):
                    if part.stop > part.start:
                        step(nc.vector.tensor_scalar(compared[:, part], all_routes[:, part], mine, 0.0, op, ALU.add,
                                                     accum_out=counts[:, n, k:k + 1]))
                step.wait()
                step.link(nc.vector.scalar_tensor_tensor(compared[:, tile], all_routes[:, tile], mine,
                                                         earlier[:, :], ALU.is_equal, ALU.mult,
                                                         accum_out=counts[:, n, 3:4]))

            for b in range(BLOCKS):
                odd, turn = b % 2, b // 2
                at = slice(b * TILES, (b + 1) * TILES)
                for t in range(TILES):
                    count_ahead(b * TILES + t)
                step.link(nc.vector.tensor_reduce(rank[:, at, 0], counts[:, at, :], AX.X, ALU.add))
                step.link(nc.vector.tensor_scalar(rank[:, at, 1], rank[:, at, 0], float(kept), None, ALU.is_lt))
                step.link(nc.vector.tensor_tensor(share[:, at], rank[:, at, 1], route[:, at], ALU.mult))
                dve.wait_ge(total_loaded[odd], (turn + 1) * 16)
                if b:
                    dve.wait_ge(turned_copied, HEAD_START + b * HALVES)
                for k in range(2):
                    dve.wait_ge(down_ready, HEAD_START + b * 2 + (k + 1))
                    step(nc.vector.tensor_tensor(result[:, 2 * k:2 * k + 2, :],
                                                 result_ps[k][:, :].rearrange("p (t c) -> p t c", t=2),
                                                 down_bias[:, :].unsqueeze(1).to_broadcast([128, 2, DIM]), ALU.add))
                step.wait()
                for t in range(TILES):
                    done = nc.vector.scalar_tensor_tensor(result[:, t, :], result[:, t, :],
                                                          share[:, b * TILES + t:b * TILES + t + 1],
                                                          total[odd][:, t, :], ALU.mult, ALU.add)
                    if t < TILES - 1:
                        step(done)
                    else:
                        done.then_inc(result_ready, 1)


_INS = [("x", (DIM, TOKENS)), ("dw_w", (3, DIM, 9)), ("dw_b", (3, DIM, 1)), ("pw_wt", (3, DIM, 3 * DIM)),
        ("pw_b", (3, 3 * DIM, 1)), ("pos_w", (3, DIM, 9)), ("pos_b", (3, DIM, 1)), ("fusion_wt", (3 * DIM, DIM)),
        ("fusion_b", (DIM, 1)), ("wqk", (DIM, 2 * DIM)), ("wvg", (DIM, 2 * DIM)), ("w_out", (DIM, DIM)),
        ("b_out", (DIM,)), ("bg", (DIM,)), ("lambdas", (4, MAP_DIM)), ("gamma", (32,)), ("beta", (32,)),
        ("w_route", (DIM,)), ("b_route", (1,)), ("w1", (DIM, HIDDEN)), ("b1", (HIDDEN, 1)), ("w2", (HIDDEN, DIM)),
        ("b2", (DIM,))]


class AttentionScratch:

    def __init__(self, scratch, p):
        self.q = scratch(f"{p.name}_q", (p.units, 3 * p.part_rows, p.width))
        self.k = scratch(f"{p.name}_k", (p.maps, 3 * p.part_rows, p.tokens))
        self.v = scratch(f"{p.name}_v", (p.maps // 2 if p.v_shared else p.maps, 128, p.key_tiles, p.v_cols))
        self.out = scratch(f"{p.name}_out", (p.units + 1, 128, p.q_tiles * 32))


def conv_attn_hybrid_kernel(nc, out, x, dw_w, dw_b, pw_wt, pw_b, pos_w, pos_b, fusion_wt, fusion_b, wqk, wvg, w_out,
                            b_out, bg, lambdas, gamma, beta, w_route, b_route, w1, b1, w2, b2):
    def scratch(name, shape):
        return nc.dram_tensor(name, shape, F32).ap()

    plans = [AttentionPlan(f"s{i}", HEADS, TOKENS // s ** 2, min(BLOCK, TOKENS // s ** 2), DIM // HEADS, 32, False)
             for i, s in enumerate(SCALES)]
    diff = AttentionPlan("df", MAPS, TOKENS, BLOCK, MAP_DIM, 31, True)

    fine = [AttentionScratch(scratch, p) for p in plans]
    dw = [scratch(f"dw{i}", (HALVES, 128, p.tokens)) for i, p in enumerate(plans)]
    pos = [scratch(f"pos{i}", (HALVES, 128, p.tokens)) for i, p in enumerate(plans)]
    convolutions(nc, x, dw_w, dw_b, pos_w, pos_b, dw, pos)
    for i, p in enumerate(plans):
        project_scale(nc, i, p, dw, pos, pw_wt, pw_b, fine[i].q, fine[i].k, fine[i].v)
    for i in (2, 1, 0):
        attention(nc, plans[i], fine[i].q, fine[i].k, fine[i].v, fine[i].out)
    base = scratch("base", (HALVES, 128, TOKENS))
    t1 = scratch("t1", (BLOCKS, 128, TILES, DIM))
    n1 = scratch("n1", (BLOCKS, 128, HALVES, BLOCK))
    gates = scratch("gates", (BLOCKS, 128, TILES, DIM))
    fuse_coarse_scales(nc, plans, x, fusion_wt, fusion_b, [f.out for f in fine], base)
    fuse_fine_scale(nc, plans[0], fusion_wt, fine[0].out, base, t1, n1)
    maps = AttentionScratch(scratch, diff)
    project_tokens(nc, n1, wqk, wvg, bg, maps.q, maps.k, maps.v, gates)
    attention(nc, diff, maps.q, maps.k, maps.v, maps.out)
    n2 = scratch("n2", (BLOCKS, 128, HALVES, BLOCK))
    total = scratch("total", (BLOCKS, 128, TILES, DIM))
    route = scratch("route", (BLOCKS, 128, TILES))
    route_rows = scratch("route_rows", (BLOCKS, BLOCK))
    finish_attention(nc, diff, maps.out, gates, t1, lambdas, gamma, beta, w_out, b_out, w_route, b_route, n2, total,
                     route)
    feed_forward(nc, n2, total, route, route_rows, w1, b1, w2, b2, out)


def kernel(**inputs):
    import numpy as np
    import concourse.bacc as bacc
    from concourse.bass_utils import run_bass_kernel_spmd

    a = {name: np.asarray(value) for name, value in inputs.items()}
    conv = {n: a[f"L0_conv_{n}"] for n in ("dw_w", "dw_b", "pw_w", "pw_b", "pos_w", "pos_b", "fusion_w", "fusion_b")}
    attn = {n: a[f"L1_attn_{n}"] for n in ("Wq", "Wkv", "Wout", "bout", "Wg", "bg", "lq1", "lk1", "lq2", "lk2",
                                           "ln_gamma", "ln_beta")}
    ffn = {n: a[f"L1_ffn_{n}"] for n in ("wr", "br", "w1", "b1", "w2", "b2")}
    laid_out = {
        "x": a["x"], "dw_w": conv["dw_w"], "dw_b": conv["dw_b"], "pw_wt": conv["pw_w"].transpose(0, 2, 1),
        "pw_b": conv["pw_b"], "pos_w": conv["pos_w"], "pos_b": conv["pos_b"], "fusion_wt": conv["fusion_w"].T,
        "fusion_b": conv["fusion_b"], "wqk": np.concatenate([attn["Wq"], attn["Wkv"][:, :DIM]], 1),
        "wvg": np.concatenate([attn["Wkv"][:, DIM:], attn["Wg"]], 1), "w_out": attn["Wout"],
        "b_out": attn["bout"], "bg": attn["bg"],
        "lambdas": np.stack([attn["lq1"], attn["lk1"], attn["lq2"], attn["lk2"]]), "gamma": attn["ln_gamma"],
        "beta": attn["ln_beta"], "w_route": ffn["wr"], "b_route": ffn["br"], "w1": ffn["w1"], "b1": ffn["b1"],
        "w2": ffn["w2"], "b2": ffn["b2"]}
    nc = bacc.Bacc("TRN2", target_bir_lowering=False, num_devices=1)
    arrays, args = {}, {}
    for name, shape in _INS:
        array = np.ascontiguousarray(laid_out[name].reshape(shape))
        arrays[f"in_{name}_dram"] = array
        args[name] = nc.dram_tensor(f"in_{name}_dram", array.shape, mybir.dt.from_np(array.dtype),
                                    kind="ExternalInput").ap()
    out = nc.dram_tensor("out_0_dram", (DIM, TOKENS), F32, kind="ExternalOutput").ap()
    conv_attn_hybrid_kernel(nc, out, **args)
    result = run_bass_kernel_spmd(nc, [arrays], core_ids=[0])
    return result.results[0]["out_0_dram"].reshape(1, DIM, SIDE, SIDE)
```

```python
import math
from contextlib import ExitStack

import concourse.bass as bass
from concourse import mybir

F32 = mybir.dt.float32
F32R = mybir.dt.float32r
ACT = mybir.ActivationFunctionType
ALU = mybir.AluOpType
AX = mybir.AxisListType


HEAD_START = 1


class AttentionPlan:

    def __init__(self, name, maps, tokens, width, part_rows, v_cols, v_shared):
        self.name, self.maps, self.tokens, self.width = name, maps, tokens, width
        self.part_rows, self.v_cols, self.v_shared = part_rows, v_cols, v_shared
        self.key_tiles = tokens // 128
        self.blocks = tokens // width
        self.units = maps * self.blocks
        self.pairs = self.key_tiles // 2
        self.q_tiles = width // 128
        self.key_chunk = min(512, tokens)
        self.chunks = tokens // self.key_chunk
        self.maxima = self.q_tiles * self.chunks
        self.lead = 12 if self.maxima > 16 else self.chunks
        self.sums = v_cols + 1
        self.column_tile = 32 if self.sums <= 32 else 64
        self.groups = min(128 // self.column_tile, self.key_tiles)
        self.ring = 4 if self.pairs % 4 == 0 else 2
        self.copy_step = 1 if self.pairs > 4 else 0
        self.place_step = (self.maxima - self.lead) // 2 + 1 if self.pairs > 4 else max(0, self.pairs - 2)
        self.batch = 2 if self.pairs > 4 else max(1, self.groups // 2)
        if self.pairs > 4:
            self.before_sum, self.before_turn = 8, self.maxima - self.lead
        else:
            self.before_sum, self.before_turn = 2 * (self.pairs // 4) + 1, 2 * max(0, self.pairs - 2) + 1

    def max_bank(self, n):
        return (n + 2 * (n > self.before_sum) + 2 * (n > self.before_turn)) % 3

    def max_behind(self, n):
        return min([3] + [n - x for x in (self.before_sum, self.before_turn) if n > x])

    @property
    def sum_bank(self):
        return (self.before_sum + 2) % 3

    @property
    def turn_bank(self):
        return (self.before_turn + 4) % 3

    def first_bank(self, made):
        return (made - self.maxima - self.lead - 1) % 3


class Slot:

    def __init__(self, engine, plan, pair_of_maps, parity, first, odd, block):
        self.unit, self.odd, self.parity, self.pair_of_maps = engine.snap(first), odd, parity, pair_of_maps
        self.blocks, self.block = plan.blocks, block
        self.last = block == plan.blocks - 1

    def maps_ahead(self, n):
        return 0 if self.block is None else (self.block + n) // self.blocks

    def map_parity(self, n):
        return (self.parity + self.maps_ahead(n)) % 2

    def map_turn(self, n):
        return self.pair_of_maps + (self.parity + self.maps_ahead(n)) // 2

    def enters(self, n):
        return self.block is not None and (self.block + n) % self.blocks == 0

    def turn_of(self, n):
        return (self.unit - self.odd) // 2 + (self.odd + n) // 2


def each_unit(engine, plan, body):
    blocks = plan.blocks
    with engine.Fori(0, plan.maps // 2) as pair_of_maps:
        for parity in range(2):
            first = (pair_of_maps * 2 + parity) * blocks
            looped = blocks - 2 if blocks > 4 else 0
            if looped:
                with engine.Fori(0, looped // 2) as turn:
                    for odd in range(2):
                        body(Slot(engine, plan, pair_of_maps, parity, first + turn * 2 + odd, odd, None))
            for block in range(looped, blocks):
                odd = (parity * blocks + block) % 2
                body(Slot(engine, plan, pair_of_maps, parity, first + block, odd, block))


def attention(nc, plan, q_scratch, k_scratch, v_scratch, out_scratch):
    n, w, ring = plan.name, plan.width, plan.ring
    rows = 3 * plan.part_rows
    with nc.cleanup_on_exit(), ExitStack() as ctx:
        def sb(what, shape, dt=F32):
            return ctx.enter_context(nc.sbuf_tensor(f"{n}_{what}", shape, dt))

        def ps(what, shape):
            return ctx.enter_context(nc.psum_tensor(f"{n}_{what}", shape, F32))

        def sem(what):
            return nc.alloc_semaphore(f"{n}_{what}")

        keys = [sb(f"keys{i}", [97, plan.tokens], F32R) for i in range(2)]
        q_max = [sb(f"q_max{i}", [96, w], F32R) for i in range(2)]
        q_exp = [sb(f"q_exp{i}", [97, w], F32R) for i in range(2)]
        values = [sb(f"values{i}", [128, plan.key_tiles, plan.column_tile]) for i in range(2)]
        probs = sb("probs", [128, ring, 2, w])
        maxima = sb("maxima", [128, 2, plan.maxima])
        shift = sb("shift", [128, plan.q_tiles, 97], F32R)
        ident = sb("ident", [128, 128])
        ident_r = sb("ident_r", [128, 128], F32R)
        fold = sb("fold", [128, plan.sums])
        out_t = sb("out_t", [128, w])
        recip = sb("recip", [128, plan.q_tiles])
        result = sb("result", [128, 2, plan.q_tiles, 32])
        scores = [ps(f"scores{i}", [128, 2, 512]) for i in range(2)]
        max_scores = [ps(f"max_scores{i}", [128, 512]) for i in range(3)]
        weighted = ps("weighted", [128, 512])

        keys_loaded = [sem(f"keys_loaded{i}") for i in range(2)]
        values_loaded = [sem(f"values_loaded{i}") for i in range(2)]
        q_max_loaded = [sem(f"q_max_loaded{i}") for i in range(2)]
        q_exp_loaded = [sem(f"q_exp_loaded{i}") for i in range(2)]
        result_stored = [sem(f"result_stored{i}") for i in range(2)]
        consts_made = sem("consts_made")
        padded = sem("padded")
        pool_padded = sem("pool_padded")
        cleared = sem("cleared")
        const_ready = sem("const_ready")
        scores_ready = sem("scores_ready")
        probs_ready = sem("probs_ready")
        probs_free = sem("probs_free")
        max_scores_ready = sem("max_scores_ready")
        max_scores_used = sem("max_scores_used")
        shift_ready = sem("shift_ready")
        shift_turned = sem("shift_turned")
        shift_placed = sem("shift_placed")
        out_copied = sem("out_copied")
        sums_ready = sem("sums_ready")
        recip_ready = sem("recip_ready")
        result_ready = sem("result_ready")
        block = ctx.enter_context(nc.Block())

        P, J, T = plan.pairs, plan.maxima, plan.q_tiles
        units = plan.units

        @block.gpsimd
        def _(pool):
            if rows < 96:
                for k, low in enumerate((32, 64)):
                    nc.gpsimd.memset(keys[1][low:low + 32, :].bitcast(F32), 0.0).then_inc(pool_padded, 1)
                    pool.wait_ge(pool_padded, k + 1)
            nc.gpsimd.memset(ident[:, :], 0.0).then_inc(consts_made, 1)
            pool.wait_ge(consts_made, 1)
            nc.gpsimd.memset(fold[:, :], 0.0).then_inc(consts_made, 1)
            pool.wait_ge(consts_made, 2)
            nc.gpsimd.affine_select(out=ident[:, :], in_=ident[:, :], compare_op=ALU.not_equal, fill=1.0, base=0,
                                    pattern=[[-1, 128]], channel_multiplier=1).then_inc(consts_made, 1)
            for g in range(plan.groups):
                pool.wait_ge(consts_made, 3 + g)
                nc.gpsimd.affine_select(out=fold[:, :], in_=fold[:, :], compare_op=ALU.not_equal, fill=1.0,
                                        base=-plan.column_tile * g, pattern=[[-1, plan.sums]],
                                        channel_multiplier=1).then_inc(consts_made, 1)
            pool.wait_ge(consts_made, 3 + plan.groups)
            nc.gpsimd.memset(keys[1][96:97, :].bitcast(F32), 1.0).then_inc(consts_made, 1)

        @block.sync
        def _(sp):
            for i in range(2):
                sp.sem_inc(result_stored[i], HEAD_START)
            for i in range(2):
                if rows < 96:
                    sp.wait_ge(padded, 10)
                    if i:
                        sp.wait_ge(pool_padded, 2)
                sp.dma_start(q_max[i][0:rows, :].bitcast(F32), q_scratch[i]).then_inc(q_max_loaded[i], 16)
                sp.dma_start(keys[i][0:rows, :].bitcast(F32), k_scratch[i]).then_inc(keys_loaded[i], 16)
                sp.dma_start(q_exp[i][0:rows, :].bitcast(F32), q_scratch[i]).then_inc(q_exp_loaded[i], 16)
                sp.dma_start(values[i][:, :, 0:plan.v_cols],
                             v_scratch[0 if plan.v_shared else i]).then_inc(values_loaded[i], 16)
            sp.wait_ge(max_scores_ready, J)
            sp.dma_start(q_max[0][0:rows, :].bitcast(F32), q_scratch[2 % units]).then_inc(q_max_loaded[0], 16)

            def unit(s):
                sp.wait_ge(max_scores_ready, (s.unit + 2) * J)
                sp.dma_start(q_max[1 - s.odd][0:rows, :].bitcast(F32), q_scratch[(s.unit + 3) % units])\
                    .then_inc(q_max_loaded[1 - s.odd], 16)
                sp.wait_ge(scores_ready, (s.unit + 1) * P)
                sp.dma_start(q_exp[s.odd][0:rows, :].bitcast(F32), q_scratch[(s.unit + 2) % units])\
                    .then_inc(q_exp_loaded[s.odd], 16)
                if s.last:
                    sp.dma_start(keys[s.parity][0:rows, :].bitcast(F32),
                                 k_scratch[(s.pair_of_maps * 2 + s.parity + 2) % plan.maps])\
                        .then_inc(keys_loaded[s.parity], 16)
                    sp.wait_ge(probs_free, (s.unit + 1) * P + ring)
                    head = ((s.pair_of_maps + 1) % (plan.maps // 2) if plan.v_shared
                            else (s.pair_of_maps * 2 + s.parity + 2) % plan.maps)
                    sp.dma_start(values[s.parity][:, :, 0:plan.v_cols], v_scratch[head])\
                        .then_inc(values_loaded[s.parity], 16)
                sp.wait_ge(result_ready, s.unit + 1)
                sp.dma_start(out_scratch[s.unit], result[:, s.odd, :, :]).then_inc(result_stored[s.odd], 16)
            each_unit(sp, plan, unit)
            sp.wait_ge(result_ready, units + 1)
            sp.dma_start(out_scratch[units], result[:, units % 2, :, :]).then_inc(result_stored[units % 2], 16)
            for i in range(2):
                sp.wait_ge(result_stored[i], HEAD_START + 16 * ((units + 2 - i) // 2))
            for i in range(2):
                sp.wait_ge(keys_loaded[i], 16 * (plan.maps // 2 + 1))
                sp.wait_ge(values_loaded[i], 16 * (plan.maps // 2 + 1))
                sp.wait_ge(q_exp_loaded[i], 16 * (units // 2 + 1))
                sp.wait_ge(q_max_loaded[i], 16 * (units // 2 + 1 + (i == 0)))

        @block.scalar
        def _(act):
            act.sem_inc(probs_ready, HEAD_START)

            def place_shift(odd, bank):
                nc.scalar.activation(q_exp[odd][96:97, :], max_scores[bank][96:97, 0:w],
                                     ACT.Copy).then_inc(shift_placed, 1)

            def copy_out(number):
                act.wait_ge(probs_free, number * P + ring)
                act.wait_ge(sums_ready, HEAD_START + number)
                nc.scalar.activation(out_t[:, :], weighted[:, 0:w], ACT.Copy).then_inc(out_copied, 1)

            act.wait_ge(shift_turned, 1)
            place_shift(0, 2)

            def unit(s):
                for p in range(P):
                    at = (s.odd * P + p) if P < 4 else p
                    act.wait_ge(scores_ready, s.unit * P + (p + 1))
                    act.wait_ge(probs_free, s.unit * P + (p + 1))
                    nc.scalar.activation(probs[:, at % ring, :, :], scores[at % 2][:, :, 0:w],
                                         ACT.Exp).then_inc(probs_ready, 1)
                    if p == plan.copy_step:
                        copy_out(s.unit)
                    if p == plan.place_step:
                        act.wait_ge(shift_turned, s.unit + 2)
                        place_shift(1 - s.odd, plan.turn_bank)
            each_unit(act, plan, unit)
            copy_out(units)

        @block.vector
        def _(dve):
            if rows < 96:
                for buffer in (*q_max, *q_exp, keys[0]):
                    for low in (32, 64):
                        nc.vector.memset(buffer[low:low + 32, :].bitcast(F32), 0.0).then_inc(padded, 1)
            nc.vector.memset(keys[0][96:97, :].bitcast(F32), 1.0).then_inc(cleared, 1)
            for i in range(2):
                nc.vector.memset(values[i][:, :, plan.v_cols:plan.column_tile], 0.0).then_inc(cleared, 1)
            nc.vector.memset(shift[:, :, :].bitcast(F32), 0.0).then_inc(cleared, 1)
            nc.vector.memset(weighted[:, :], 1.0).then_inc(cleared, 1)
            dve.wait_ge(cleared, 5)
            for i in range(2):
                nc.vector.memset(values[i][:, :, plan.v_cols:plan.v_cols + 1], 1.0).then_inc(cleared, 1)
            dve.wait_ge(consts_made, 3)
            nc.vector.tensor_copy(ident_r[:, :], ident[:, :]).then_inc(cleared, 1)
            dve.wait_ge(cleared, 8)
            dve.sem_inc(const_ready, 1)

            def row_maxima(made, odd, j, bank):
                dve.wait_ge(max_scores_ready, made + 1)
                nc.vector.tensor_reduce(maxima[:, odd, j:j + 1], max_scores[bank][:, 0:plan.key_chunk], AX.X,
                                        ALU.max).then_inc(max_scores_used, 1)
                if j == J - 1:
                    dve.wait_ge(max_scores_used, made + 1)
                    nc.vector.tensor_reduce(
                        shift[:, :, 96], maxima[:, odd, :].rearrange("p (t c) -> p t c", c=plan.chunks), AX.X,
                        ALU.max, negate=True).then_inc(shift_ready, 1)

            def normalise(number, odd, stores_before):
                dve.wait_ge(sums_ready, HEAD_START + number + 1)
                sums = max_scores[plan.sum_bank][:, 0:T * plan.sums].rearrange("p (t c) -> p t c", c=plan.sums)
                nc.vector.reciprocal(recip[:, :], sums[:, :, plan.v_cols]).then_inc(recip_ready, 1)
                dve.wait_ge(recip_ready, number + 1)
                dve.wait_ge(result_stored[odd], HEAD_START + stores_before)
                nc.vector.tensor_tensor(result[:, odd, :, :], sums[:, :, 0:32],
                                        recip[:, :].unsqueeze(2).to_broadcast([128, T, 32]),
                                        ALU.mult).then_inc(result_ready, 1)

            for j in range(J):
                row_maxima(j, 0, j, plan.first_bank(j))
            for j in range(plan.lead):
                row_maxima(J + j, 1, j, plan.first_bank(J + j))

            def unit(s):
                for p in range(P):
                    for i in range(2):
                        j = plan.lead + 2 * p + i
                        row_maxima((s.unit + 1) * J + j, (s.odd + 1 + j // J) % 2, j % J,
                                   plan.max_bank(2 * p + i))
                        if 2 * p + i == plan.before_sum:
                            normalise(s.unit, s.odd, s.turn_of(0) * 16)
            each_unit(dve, plan, unit)
            normalise(units, units % 2, units // 2 * 16)

        @block.tensor
        def _(pe):
            def max_product(made, odd, j, k_parity, bank, behind):
                if behind:
                    pe.wait_ge(max_scores_used, made - behind + 1)
                t, c = divmod(j, plan.chunks)
                nc.tensor.matmul(max_scores[bank][:, 0:plan.key_chunk], q_max[odd][:, t * 128:(t + 1) * 128],
                                 keys[k_parity][0:96, c * plan.key_chunk:(c + 1) * plan.key_chunk],
                                 start=True, stop=True).then_inc(max_scores_ready, 1)

            def turn_shift(bank):
                for t in range(T):
                    last = nc.tensor.matmul(max_scores[bank][0:97, t * 128:(t + 1) * 128], shift[:, t, :],
                                            ident_r[:, :], start=True, stop=True)
                last.then_inc(shift_turned, 1)

            def score_product(odd, k_parity, p, slot):
                for i in range(2):
                    kt = 2 * p + i
                    last = nc.tensor.matmul(scores[slot][:, i, 0:w], keys[k_parity][:, kt * 128:(kt + 1) * 128],
                                            q_exp[odd][:, :], start=True, stop=True)
                last.then_inc(scores_ready, 1)

            def fold_groups():
                for t in range(T):
                    last = nc.tensor.matmul(max_scores[plan.sum_bank][:, t * plan.sums:(t + 1) * plan.sums],
                                            out_t[:, t * 128:(t + 1) * 128], fold[:, :], start=True, stop=True)
                last.then_inc(sums_ready, 1)

            pe.sem_inc(sums_ready, HEAD_START)
            pe.wait_ge(q_max_loaded[0], 16)
            pe.wait_ge(keys_loaded[0], 16)
            for j in range(J):
                max_product(j, 0, j, 0, plan.first_bank(j), 3 if j >= 3 else 0)
            pe.wait_ge(q_max_loaded[1], 16)
            pe.wait_ge(keys_loaded[1], 16)
            for j in range(plan.lead):
                max_product(J + j, 1, j, 0 if plan.blocks > 1 else 1, plan.first_bank(J + j),
                            3 if J + j >= 3 else 0)
            pe.wait_ge(const_ready, 1)
            pe.wait_ge(consts_made, 4 + plan.groups)
            pe.wait_ge(shift_ready, 1)
            pe.wait_ge(max_scores_used, J + plan.lead)
            turn_shift(2)
            pe.wait_ge(q_exp_loaded[0], 16)
            pe.wait_ge(q_exp_loaded[1], 16)
            pe.wait_ge(shift_placed, 1)
            score_product(0, 0, 0, 0)
            pe.sem_inc(probs_free, ring)

            def unit(s):
                def scores_of_next(p):
                    at = (s.odd * P + p + 1) if P < 4 else p + 1
                    pe.wait_ge(probs_ready, HEAD_START + s.unit * P + p)
                    if p < P - 1:
                        score_product(s.odd, s.parity, p + 1, at % 2)
                    else:
                        pe.wait_ge(q_exp_loaded[1 - s.odd], (s.turn_of(1) + 1) * 16)
                        pe.wait_ge(shift_placed, s.unit + 2)
                        score_product(1 - s.odd, s.map_parity(1), 0, at % 2)

                def maximum_of_next(p, i):
                    j = plan.lead + 2 * p + i
                    ahead = 1 + j // J
                    if j == J:
                        pe.wait_ge(q_max_loaded[s.odd], (s.turn_of(2) + 1) * 16)
                        if s.enters(2):
                            pe.wait_ge(keys_loaded[s.map_parity(2)], (s.map_turn(2) + 1) * 16)
                    n = 2 * p + i
                    if n == plan.before_sum + 3:
                        pe.wait_ge(result_ready, s.unit + 1)
                    if n == plan.before_turn + 3:
                        pe.wait_ge(shift_placed, s.unit + 2)
                    max_product((s.unit + 1) * J + j, (s.odd + ahead) % 2, j % J, s.map_parity(ahead),
                                plan.max_bank(n), plan.max_behind(n))

                def weigh_values(first, end):
                    if first == 0:
                        pe.wait_ge(values_loaded[s.parity], (s.map_turn(0) + 1) * 16)
                        pe.wait_ge(out_copied, s.unit + 1)
                    pe.wait_ge(probs_ready, HEAD_START + s.unit * P + end)
                    for kt in range(2 * first, 2 * end):
                        at = (s.odd * P + kt // 2) if P < 4 else kt // 2
                        g = kt % plan.groups
                        last = nc.tensor.matmul(
                            weighted[g * plan.column_tile:(g + 1) * plan.column_tile, 0:w],
                            values[s.parity][:, kt, :], probs[:, at % ring, kt % 2, :],
                            start=kt < plan.groups, stop=kt >= plan.key_tiles - plan.groups)
                    last.then_inc(probs_free, end - first)

                def between(n):
                    if n == plan.before_sum:
                        pe.wait_ge(out_copied, s.unit + 1)
                        pe.wait_ge(max_scores_used, (s.unit + 1) * J + plan.lead + n)
                        fold_groups()
                    if n == plan.before_turn:
                        pe.wait_ge(shift_ready, s.unit + 2)
                        pe.wait_ge(max_scores_used, (s.unit + 1) * J + plan.lead + n)
                        turn_shift(plan.turn_bank)

                for p in range(P):
                    late = p == plan.before_turn // 2 and p == P - 1
                    if p % 2:
                        maximum_of_next(p, 0)
                    if not late:
                        scores_of_next(p)
                    if not p % 2:
                        maximum_of_next(p, 0)
                    if p and p % plan.batch == 0:
                        weigh_values(p - plan.batch, p)
                    between(2 * p)
                    maximum_of_next(p, 1)
                    between(2 * p + 1)
                    if late:
                        scores_of_next(p)
                weigh_values(P - plan.batch, P)
                if plan.before_sum + 3 >= J:
                    pe.wait_ge(result_ready, s.unit + 1)
            each_unit(pe, plan, unit)
            pe.wait_ge(out_copied, units + 1)
            pe.wait_ge(max_scores_used, (units + 1) * J + plan.lead)
            fold_groups()


class Steps:

    def __init__(self, engine, sem, turn=0, per_turn=0):
        self.engine, self.sem, self.base, self.n, self.per_turn = engine, sem, turn * per_turn, 0, per_turn

    def __call__(self, instruction):
        self.n += 1
        instruction.then_inc(self.sem, 1)
        return self.n

    def wait(self, n=None):
        self.engine.wait_ge(self.sem, self.base + (self.n if n is None else n))

    def link(self, instruction):
        self(instruction)
        self.wait()


DIM, SIDE, TOKENS = 256, 64, 4096
HALVES = DIM // 128
PARTS = ((0, 0), (1, 0), (0, 1))
SCALES = (1, 2, 4)
HEADS = 8
BLOCK = 512


def make_identity(nc, pool, ident, made):
    nc.gpsimd.memset(ident[:, :], 0.0).then_inc(made, 1)
    pool.wait_ge(made, 1)
    nc.gpsimd.affine_select(out=ident[:, :], in_=ident[:, :], compare_op=ALU.not_equal, fill=1.0, base=0,
                            pattern=[[-1, 128]], channel_multiplier=1).then_inc(made, 1)


def convolutions(nc, x, dw_w, dw_b, pos_w, pos_b, dw_scratch, pos_scratch):
    group = 8
    with nc.cleanup_on_exit(), ExitStack() as ctx:
        def sb(what, shape, dt=F32):
            return ctx.enter_context(nc.sbuf_tensor(f"cv_{what}", shape, dt))

        def sem(what):
            return nc.alloc_semaphore(f"cv_{what}")

        sides = [SIDE // s for s in SCALES]
        x_in = sb("x_in", [128, HALVES, TOKENS])
        padded = [sb(f"padded{i}", [128, HALVES, d + 2, d + 2]) for i, d in enumerate(sides)]
        taps = sb("taps", [128, 3, HALVES, 2, 9])
        biases = sb("biases", [128, 3, HALVES, 2])
        diagonal = [sb(f"diagonal{i}", [128, HALVES, 9, 128]) for i in range(3)]
        dw_out = [sb(f"dw_out{i}", [128, HALVES, d, d]) for i, d in enumerate(sides)]
        pos_out = sb("pos_out", [128, 4, BLOCK])
        ident = sb("ident", [128, 128])
        group_mean = sb("group_mean", [128, 128])
        stats = sb("stats", [128, HALVES, 8, 6])
        moments = sb("moments", [128, HALVES, 2])
        group_moments = sb("group_moments", [128, HALVES, 2])
        spread = sb("spread", [128, HALVES, 4])
        groups_ps = ctx.enter_context(nc.psum_tensor("cv_groups", [128, 512], F32))
        pos_ps = [ctx.enter_context(nc.psum_tensor(f"cv_pos{i}", [128, 512], F32)) for i in range(4)]

        x_loaded = [sem(f"x_loaded{i}") for i in range(HALVES)]
        weights_loaded = sem("weights_loaded")
        identity_made = sem("identity_made")
        group_made = sem("group_made")
        borders_cleared = sem("borders_cleared")
        dve_steps = sem("dve_steps")
        moments_ready = sem("moments_ready")
        groups_ready = sem("groups_ready")
        variance_ready = sem("variance_ready")
        deviation_ready = sem("deviation_ready")
        scaled_ready = sem("scaled_ready")
        diagonal_ready = sem("diagonal_ready")
        dw_ready = sem("dw_ready")
        pos_product = sem("pos_product")
        pos_copied = sem("pos_copied")
        pos_stored = [sem(f"pos_stored{i}") for i in range(4)]
        dw_stored = sem("dw_stored")
        block = ctx.enter_context(nc.Block())

        pieces = []
        for i, d in enumerate(sides):
            rows = min(BLOCK // d, d)
            pieces += [(i, h, r, rows) for r in range(0, d, rows) for h in range(HALVES)]

        @block.sync
        def _(sp):
            for h in range(HALVES):
                sp.dma_start(x_in[:, h, :], x[h * 128:(h + 1) * 128, :]).then_inc(x_loaded[h], 16)
            for i in range(3):
                for h in range(HALVES):
                    at = slice(h * 128, (h + 1) * 128)
                    for j, (w, b) in enumerate(((dw_w, dw_b), (pos_w, pos_b))):
                        sp.dma_start(taps[:, i, h, j, :], w[i, at, :]).then_inc(weights_loaded, 16)
                        sp.dma_start(biases[:, i, h, j:j + 1], b[i, at, :]).then_inc(weights_loaded, 16)
            for i in range(3):
                sp.wait_ge(dw_ready, 2 * i + 2)
                sp.dma_start(dw_scratch[i].rearrange("h p n -> p h n"),
                             dw_out[i][:, :, :, :].rearrange("p h r c -> p h (r c)")).then_inc(dw_stored, 16)
            sp.wait_ge(dw_stored, 48)

        @block.gpsimd
        def _(pool):
            make_identity(nc, pool, ident, identity_made)
            nc.gpsimd.memset(group_mean[:, :], 1.0 / group).then_inc(group_made, 1)
            view = group_mean[:, :].rearrange("p (g c) -> p g c", c=group)
            pool.wait_ge(group_made, 1)
            nc.gpsimd.affine_select(out=view, in_=view, compare_op=ALU.is_ge, fill=0.0, base=0,
                                    pattern=[[-group, 128 // group], [0, group]], channel_multiplier=1)\
                .then_inc(group_made, 1)
            pool.wait_ge(group_made, 2)
            nc.gpsimd.affine_select(out=view, in_=view, compare_op=ALU.is_ge, fill=0.0, base=group - 1,
                                    pattern=[[group, 128 // group], [0, group]], channel_multiplier=-1)\
                .then_inc(group_made, 1)
            for i in range(3):
                nc.gpsimd.memset(padded[i][:, :, :, :], 0.0).then_inc(borders_cleared, 1)

        @block.scalar
        def _(act):
            act.wait_ge(variance_ready, 1)
            nc.scalar.activation(spread[:, :, 1], spread[:, :, 0], ACT.Sqrt).then_inc(deviation_ready, 1)
            act.wait_ge(weights_loaded, 16 * 24)
            for n, (i, h, r, rows) in enumerate(pieces):
                act.wait_ge(pos_product, n + 1)
                if n >= 4:
                    act.wait_ge(pos_stored[n % 4], 16 * (n // 4))
                w = rows * sides[i]
                nc.scalar.activation(pos_out[:, n % 4, 0:w], pos_ps[n % 4][:, 0:w], ACT.Identity,
                                     bias=biases[:, i, h, 1:2]).then_inc(pos_copied, 1)
                act.wait_ge(pos_copied, n + 1)
                act.dma_start(pos_scratch[i][h][:, r * sides[i]:r * sides[i] + w], pos_out[:, n % 4, 0:w])\
                    .then_inc(pos_stored[n % 4], 16)
            for k in range(4):
                act.wait_ge(pos_stored[k], 16 * len(range(k, len(pieces), 4)))

        @block.tensor
        def _(pe):
            pe.wait_ge(moments_ready, 1)
            pe.wait_ge(group_made, 3)
            nc.tensor.matmul(groups_ps[:, 0:4], group_mean[:, :],
                             moments[:, :, :].rearrange("p h m -> p (h m)"), start=True, stop=True)\
                .then_inc(groups_ready, 1)
            for n, (i, h, r, rows) in enumerate(pieces):
                pe.wait_ge(scaled_ready, i + 1)
                pe.wait_ge(diagonal_ready, i + 1)
                if n >= 4:
                    pe.wait_ge(pos_copied, n - 3)
                d = sides[i]
                for k in range(9):
                    last = nc.tensor.matmul(pos_ps[n % 4][:, 0:rows * d], diagonal[i][:, h, k, :],
                                            padded[i][:, h, r + k // 3:r + k // 3 + rows, k % 3:k % 3 + d],
                                            start=k == 0, stop=k == 8)
                last.then_inc(pos_product, 1)

        @block.vector
        def _(dve):
            step = Steps(dve, dve_steps)
            for h in range(HALVES):
                dve.wait_ge(x_loaded[h], 16)
                for c in range(8):
                    step(nc.vector.bn_stats(stats[:, h, c, :], x_in[:, h, c * 512:(c + 1) * 512]))
            step.wait()
            for h in range(HALVES):
                step(nc.vector.bn_aggr(moments[:, h, :], stats[:, h, :, :].rearrange("p c s -> p (c s)")))
            step.wait()
            step.link(nc.vector.tensor_tensor(spread[:, :, 2], moments[:, :, 0], moments[:, :, 0], ALU.mult))
            nc.vector.tensor_tensor(moments[:, :, 1], moments[:, :, 1], spread[:, :, 2], ALU.add)\
                .then_inc(moments_ready, 1)
            dve.wait_ge(groups_ready, 1)
            step.link(nc.vector.tensor_copy(group_moments[:, :, :],
                                            groups_ps[:, 0:4].rearrange("p (h m) -> p h m", m=2)))
            step.link(nc.vector.tensor_tensor(spread[:, :, 3], group_moments[:, :, 0], group_moments[:, :, 0],
                                              ALU.mult))
            step.link(nc.vector.tensor_tensor(spread[:, :, 2], group_moments[:, :, 1], spread[:, :, 3],
                                              ALU.subtract))
            nc.vector.tensor_scalar(spread[:, :, 0], spread[:, :, 2], 1e-5, None, ALU.add)\
                .then_inc(variance_ready, 1)
            inverse_root(nc, dve, step, deviation_ready, 1, spread[:, :, 0], spread[:, :, 1], spread[:, :, 2])
            dve.wait_ge(borders_cleared, 3)
            for h in range(HALVES):
                step(nc.vector.tensor_scalar(
                    padded[0][:, h, 1:SIDE + 1, 1:SIDE + 1], x_in[:, h, :].rearrange("p (r c) -> p r c", c=SIDE),
                    group_moments[:, h, 0:1], spread[:, h, 1:2], ALU.subtract, ALU.mult))
            step.wait()
            dve.sem_inc(scaled_ready, 1)
            dve.wait_ge(weights_loaded, 16 * 24)
            dve.wait_ge(identity_made, 2)

            def diagonals(i):
                for h in range(HALVES):
                    for k in range(9):
                        step(nc.vector.tensor_scalar(diagonal[i][:, h, k, :], ident[:, :],
                                                     taps[:, i, h, 1, k:k + 1], None, ALU.mult))
                step.wait()
                dve.sem_inc(diagonal_ready, 1)

            diagonals(0)
            for i in (1, 2):
                d = sides[i]
                for h in range(HALVES):
                    fine = padded[i - 1][:, h, 1:2 * d + 1, 1:2 * d + 1].rearrange("p (r a) c -> p r a c", a=2)
                    rows = x_in[:, h, 0:2 * d * d].rearrange("p (r c) -> p r c", c=2 * d)
                    step.link(nc.vector.tensor_tensor(rows, fine[:, :, 0, :], fine[:, :, 1, :], ALU.add))
                    pairs = rows.rearrange("p r (c b) -> p r c b", b=2)
                    sums = x_in[:, h, 2048:2048 + d * d].rearrange("p (r c) -> p r c", c=d)
                    step.link(nc.vector.tensor_tensor(sums, pairs[:, :, :, 0], pairs[:, :, :, 1], ALU.add))
                    step.link(nc.vector.tensor_scalar(padded[i][:, h, 1:d + 1, 1:d + 1], sums, 0.25, None,
                                                      ALU.mult))
                dve.sem_inc(scaled_ready, 1)
                diagonals(i)
            for i, d in enumerate(sides):
                for k in range(9):
                    for h in range(HALVES):
                        shifted = padded[i][:, h, k // 3:k // 3 + d, k % 3:k % 3 + d]
                        tap = taps[:, i, h, 0, k:k + 1]
                        if k == 0:
                            step(nc.vector.tensor_scalar(dw_out[i][:, h, :, :], shifted, tap,
                                                         biases[:, i, h, 0:1], ALU.mult, ALU.add))
                            continue
                        step.wait(step.n - 1 + (h if k == 8 else 0))
                        done = nc.vector.scalar_tensor_tensor(dw_out[i][:, h, :, :], shifted, tap,
                                                              dw_out[i][:, h, :, :], ALU.mult, ALU.add)
                        if k < 8:
                            step(done)
                        else:
                            done.then_inc(dw_ready, 1)


def each_block(engine, blocks, body):
    if blocks == 1:
        body(0, 0, 0)
        return
    with engine.Fori(0, blocks // 2) as turn:
        for odd in range(2):
            body(engine.snap(turn * 2 + odd), odd, turn)


def each_block_but_last(engine, blocks, body):
    with engine.Fori(0, blocks // 2 - 1) as turn:
        for odd in range(2):
            body(engine.snap(turn * 2 + odd), odd, turn, False)
    for odd in range(2):
        body(blocks - 2 + odd, odd, blocks // 2 - 1, odd == 1)


def project_scale(nc, i, plan, dw_scratch, pos_scratch, pw_wt, pw_b, q_scratch, k_scratch, v_scratch):
    width, blocks = plan.width, plan.blocks
    tiles = width // 128
    scale = (DIM // HEADS) ** -0.5
    with nc.cleanup_on_exit(), ExitStack() as ctx:
        def sb(what, shape, dt=F32):
            return ctx.enter_context(nc.sbuf_tensor(f"pj{i}_{what}", shape, dt))

        def sem(what):
            return nc.alloc_semaphore(f"pj{i}_{what}")

        weights = sb("weights", [128, HALVES, 3 * DIM])
        qk_bias = sb("qk_bias", [128, 4])
        v_bias = sb("v_bias", [128, DIM])
        conv = [sb(f"conv{k}", [128, HALVES, width]) for k in range(2)]
        pos = [sb(f"pos{k}", [128, HALVES, width]) for k in range(2)]
        whole = sb("whole", [128, 4, width])
        high = [sb(f"high{k}", [128, 4, width], F32R) for k in range(2)]
        low = [sb(f"low{k}", [128, 4, width], F32R) for k in range(2)]
        v_out = [sb(f"v_out{k}", [128, tiles, DIM]) for k in range(2)]
        qk_ps = [ctx.enter_context(nc.psum_tensor(f"pj{i}_qk{m}", [128, 512], F32)) for m in range(4)]
        v_ps = [ctx.enter_context(nc.psum_tensor(f"pj{i}_v{m}", [128, 512], F32)) for m in range(2)]

        weights_loaded = sem("weights_loaded")
        conv_loaded = [sem(f"conv_loaded{k}") for k in range(2)]
        pos_loaded = [sem(f"pos_loaded{k}") for k in range(2)]
        qk_ready = sem("qk_ready")
        v_ready = sem("v_ready")
        whole_ready = sem("whole_ready")
        high_ready = sem("high_ready")
        low_ready = sem("low_ready")
        v_copied = sem("v_copied")
        parts_stored = [sem(f"parts_stored{k}") for k in range(2)]
        v_stored = [sem(f"v_stored{k}") for k in range(2)]
        block = ctx.enter_context(nc.Block())
        v_groups = tiles // 2

        @block.sync
        def _(sp):
            sp.dma_start(weights[:, :, :], pw_wt[i].rearrange("(h p) n -> p h n", p=128)).then_inc(weights_loaded, 16)
            for m in range(4):
                sp.dma_start(qk_bias[:, m:m + 1], pw_b[i, m * 128:(m + 1) * 128, :]).then_inc(weights_loaded, 16)
            sp.dma_start(v_bias[:, :], pw_b[i, 2 * DIM:3 * DIM, 0].partition_broadcast(128))\
                .then_inc(weights_loaded, 16)

            def load(b, odd, turn):
                sp.wait_ge(v_copied, HEAD_START + b * v_groups)
                sp.dma_start(conv[odd][:, :, :],
                             dw_scratch[i].rearrange("h p (b n) -> b p h n", n=width)[b]).then_inc(conv_loaded[odd], 16)
                sp.dma_start(pos[odd][:, :, :],
                             pos_scratch[i].rearrange("h p (b n) -> b p h n", n=width)[b]).then_inc(pos_loaded[odd], 16)
            each_block(sp, blocks, load)

        @block.tensor
        def _(pe):
            pe.wait_ge(weights_loaded, 16 * 6)

            def products(b, odd, turn):
                pe.wait_ge(conv_loaded[odd], (turn + 1) * 16)
                for m in range(4):
                    pe.wait_ge(whole_ready, HEAD_START + b * 4)
                    for h in range(HALVES):
                        last = nc.tensor.matmul(qk_ps[m][:, 0:width], weights[:, h, m * 128:(m + 1) * 128],
                                                conv[odd][:, h, :], start=h == 0, stop=h == HALVES - 1)
                    last.then_inc(qk_ready, 1)
                for g in range(v_groups):
                    pe.wait_ge(v_copied, HEAD_START + (b + 1) * v_groups)
                    for t in range(2):
                        at = (2 * g + t) * 128
                        for h in range(HALVES):
                            last = nc.tensor.matmul(v_ps[g][:, t * DIM:(t + 1) * DIM], conv[odd][:, h, at:at + 128],
                                                    weights[:, h, 2 * DIM:3 * DIM], start=h == 0,
                                                    stop=h == HALVES - 1)
                    last.then_inc(v_ready, 1)
            each_block(pe, blocks, products)

        @block.vector
        def _(dve):
            dve.sem_inc(whole_ready, HEAD_START)
            dve.sem_inc(low_ready, HEAD_START)
            dve.sem_inc(v_copied, HEAD_START + v_groups)
            dve.wait_ge(weights_loaded, 16 * 6)

            def block_out(b, odd, turn):
                dve.wait_ge(pos_loaded[odd], (turn + 1) * 16)
                for m in range(4):
                    dve.wait_ge(qk_ready, b * 4 + (m + 1))
                    if m == 0:
                        dve.wait_ge(low_ready, HEAD_START + b * 4)
                        dve.wait_ge(high_ready, HEAD_START + b * 4)
                    nc.vector.scalar_tensor_tensor(whole[:, m, :], qk_ps[m][:, 0:width], qk_bias[:, m:m + 1],
                                                   pos[odd][:, m % 2, :], ALU.add, ALU.add)\
                        .then_inc(whole_ready, 1)
                dve.wait_ge(parts_stored[odd], HEAD_START + turn * 16 * 12)
                for m in range(4):
                    dve.wait_ge(high_ready, HEAD_START + b * 4 + (m + 1))
                    nc.vector.scalar_tensor_tensor(low[odd][:, m, :], whole[:, m, :], scale if m < 2 else 1.0,
                                                   high[odd][:, m, :].bitcast(F32), ALU.mult, ALU.subtract)\
                        .then_inc(low_ready, 1)
                dve.wait_ge(v_stored[odd], HEAD_START + turn * 16 * tiles)
                for g in range(v_groups):
                    dve.wait_ge(v_ready, b * v_groups + (g + 1))
                    nc.vector.tensor_tensor(v_out[odd][:, 2 * g:2 * g + 2, :],
                                            v_ps[g][:, :].rearrange("p (t c) -> p t c", t=2),
                                            v_bias[:, :].unsqueeze(1).to_broadcast([128, 2, DIM]), ALU.add)\
                        .then_inc(v_copied, 1)
            each_block(dve, blocks, block_out)

        @block.scalar
        def _(act):
            act.sem_inc(high_ready, HEAD_START)
            for stored in parts_stored:
                act.sem_inc(stored, HEAD_START)
            for stored in v_stored:
                act.sem_inc(stored, HEAD_START)
            q_view = q_scratch.rearrange("(h b) (s d) n -> b s h d n", b=blocks, s=3)
            k_view = k_scratch.rearrange("h (s d) (b n) -> b s h d n", s=3, n=width)
            v_view = v_scratch.rearrange("h p (b t) d -> b t p h d", t=tiles)


            def highs(b, odd, turn):
                act.wait_ge(parts_stored[odd], HEAD_START + turn * 16 * 12)
                for m in range(4):
                    act.wait_ge(whole_ready, HEAD_START + b * 4 + (m + 1))
                    nc.scalar.activation(high[odd][:, m, :], whole[:, m, :], ACT.Copy,
                                         scale=scale if m < 2 else 1.0).then_inc(high_ready, 1)
                act.wait_ge(low_ready, HEAD_START + (b + 1) * 4)
                for m in range(4):
                    view = q_view if m < 2 else k_view
                    for s, part in enumerate((high, high, low) if m < 2 else (high, low, high)):
                        act.dma_start(view[b, s, 4 * (m % 2):4 * (m % 2) + 4],
                                       part[odd][:, m, :].bitcast(F32)).then_inc(parts_stored[odd], 16)
                act.wait_ge(v_copied, HEAD_START + (b + 2) * v_groups)
                for t in range(tiles):
                    act.dma_start(v_view[b, t], v_out[odd][:, t, :].rearrange("p (h d) -> p h d", h=HEADS))\
                        .then_inc(v_stored[odd], 16)
            each_block(act, blocks, highs)
            for k in range(min(2, blocks)):
                act.wait_ge(parts_stored[k], HEAD_START + 16 * 12 * max(1, blocks // 2))
                act.wait_ge(v_stored[k], HEAD_START + 16 * tiles * max(1, blocks // 2))


def inverse_root(nc, dve, step, root_ready, number, value, root, work):
    dve.wait_ge(root_ready, number)
    step.link(nc.vector.reciprocal(root, root))
    step.link(nc.vector.tensor_tensor(work, root, root, ALU.mult))
    step.link(nc.vector.tensor_tensor(work, work, value, ALU.mult))
    step.link(nc.vector.tensor_scalar(work, work, -0.5, 1.5, ALU.mult, ALU.add))
    step.link(nc.vector.tensor_tensor(root, root, work, ALU.mult))


def fuse_coarse_scales(nc, plans, x, fusion_wt, fusion_b, att_scratch, base_scratch):
    with nc.cleanup_on_exit(), ExitStack() as ctx:
        def sb(what, shape, dt=F32):
            return ctx.enter_context(nc.sbuf_tensor(f"fc_{what}", shape, dt))

        def sem(what):
            return nc.alloc_semaphore(f"fc_{what}")

        coarse = [1, 2]
        tiles = {i: plans[i].tokens // 128 for i in coarse}
        tokens = {i: sb(f"tokens{i}", [128, tiles[i], DIM]) for i in coarse}
        channels = {i: sb(f"channels{i}", [128, HALVES, plans[i].tokens]) for i in coarse}
        fused = {i: sb(f"fused{i}", [128, HALVES, SIDE // SCALES[i], SIDE // SCALES[i]]) for i in coarse}
        wide = {i: sb(f"wide{i}", [128, HALVES, SIDE // SCALES[i], SIDE]) for i in coarse}
        weights = sb("weights", [128, 6, DIM])
        bias = sb("bias", [128, HALVES])
        base = sb("base", [128, HALVES, SIDE, SIDE])
        ident = sb("ident", [128, 128])
        turned_ps = [ctx.enter_context(nc.psum_tensor(f"fc_turned_ps{k}", [128, 512], F32)) for k in range(2)]
        fused_ps = [ctx.enter_context(nc.psum_tensor(f"fc_fused_ps{k}", [128, 512], F32)) for k in range(2)]

        loaded = sem("loaded")
        tokens_loaded = {i: sem(f"tokens{i}_loaded") for i in coarse}
        identity_made = sem("identity_made")
        turned = sem("turned")
        turned_copied = sem("turned_copied")
        fused_ready = sem("fused_ready")
        fused_copied = sem("fused_copied")
        steps = sem("steps")
        base_ready = sem("base_ready")
        stored = sem("stored")
        block = ctx.enter_context(nc.Block())

        pieces = [(i, t, min(4, tiles[i])) for i in coarse for t in range(0, tiles[i], 4)]

        @block.sync
        def _(sp):
            for i in coarse:
                p = plans[i]
                for h in range(HEADS):
                    for b in range(p.blocks):
                        sp.dma_start(tokens[i][:, b * p.q_tiles:(b + 1) * p.q_tiles, h * 32:(h + 1) * 32],
                                     att_scratch[i][h * p.blocks + b + 1].rearrange("p (t d) -> p t d", d=32))\
                            .then_inc(tokens_loaded[i], 16)
            sp.dma_start(base[:, :, :, :].rearrange("p h r c -> p h (r c)"),
                         x.rearrange("(h p) n -> p h n", p=128)).then_inc(loaded, 16)
            sp.dma_start(weights[:, :, :], fusion_wt.rearrange("(k p) n -> p k n", p=128)).then_inc(loaded, 16)
            for h in range(HALVES):
                sp.dma_start(bias[:, h:h + 1], fusion_b[h * 128:(h + 1) * 128, :]).then_inc(loaded, 16)
            for h in range(HALVES):
                sp.wait_ge(base_ready, h + 1)
                sp.dma_start(base_scratch[h], base[:, h, :, :].rearrange("p r c -> p (r c)")).then_inc(stored, 16)
            sp.wait_ge(stored, 32)

        @block.gpsimd
        def _(pool):
            make_identity(nc, pool, ident, identity_made)

        @block.tensor
        def _(pe):
            pe.wait_ge(identity_made, 2)
            n = 0
            for i, first, count in pieces:
                pe.wait_ge(tokens_loaded[i], 16 * HEADS * plans[i].blocks)
                for h in range(HALVES):
                    if n >= 2:
                        pe.wait_ge(turned_copied, n - 1)
                    for t in range(count):
                        last = nc.tensor.transpose(turned_ps[n % 2][:, t * 128:(t + 1) * 128],
                                                   tokens[i][:, first + t, h * 128:(h + 1) * 128], ident[:, :])
                    last.then_inc(turned, 1)
                    n += 1
            pe.wait_ge(turned_copied, n)
            pe.wait_ge(loaded, 64)
            n = 0
            for i, first, count in pieces:
                for m in range(HALVES):
                    if n >= 2:
                        pe.wait_ge(fused_copied, n - 1)
                    for h in range(HALVES):
                        last = nc.tensor.matmul(fused_ps[n % 2][:, 0:count * 128],
                                                weights[:, 2 * i + h, m * 128:(m + 1) * 128],
                                                channels[i][:, h, first * 128:(first + count) * 128],
                                                start=h == 0, stop=h == HALVES - 1)
                    last.then_inc(fused_ready, 1)
                    n += 1

        @block.scalar
        def _(act):
            n = 0
            for i, first, count in pieces:
                for h in range(HALVES):
                    act.wait_ge(turned, n + 1)
                    nc.scalar.activation(channels[i][:, h, first * 128:(first + count) * 128],
                                         turned_ps[n % 2][:, 0:count * 128], ACT.Copy).then_inc(turned_copied, 1)
                    n += 1
            n = 0
            for i, first, count in pieces:
                flat = fused[i][:, :, :, :].rearrange("p h r c -> p h (r c)")
                for m in range(HALVES):
                    act.wait_ge(fused_ready, n + 1)
                    nc.scalar.activation(flat[:, m, first * 128:(first + count) * 128],
                                         fused_ps[n % 2][:, 0:count * 128], ACT.Copy).then_inc(fused_copied, 1)
                    n += 1

        @block.vector
        def _(dve):
            step = Steps(dve, steps)
            dve.wait_ge(loaded, 64)
            for h in range(HALVES):
                step.link(nc.vector.tensor_scalar(base[:, h, :, :], base[:, h, :, :], bias[:, h:h + 1], None, ALU.add))
            dve.wait_ge(fused_copied, 2 * len(pieces))

            def phases(f):
                for r in range(f):
                    c = (r + 0.5) / f - 0.5
                    yield r, 1 - abs(c), abs(c), -1 if c < 0 else 1

            for h in range(HALVES):
                for i in coarse:
                    f = SCALES[i]
                    d = SIDE // f
                    source = fused[i][:, h, :, :]
                    columns = wide[i][:, h, :, :].rearrange("p r (c f) -> p r c f", f=f)
                    for r, near, far, side in phases(f):
                        step.link(nc.vector.tensor_scalar(columns[:, :, :, r], source, near, None, ALU.mult))
                        here, there = (slice(1, d), slice(0, d - 1)) if side < 0 else (slice(0, d - 1), slice(1, d))
                        edge = slice(0, 1) if side < 0 else slice(d - 1, d)
                        for to, of in ((here, there), (edge, edge)):
                            step.link(nc.vector.scalar_tensor_tensor(
                                columns[:, :, to, r], source[:, :, of], far, columns[:, :, to, r],
                                ALU.mult, ALU.add))
                    rows = base[:, h, :, :].rearrange("p (r f) c -> p r f c", f=f)
                    source = wide[i][:, h, :, :]
                    for r, near, far, side in phases(f):
                        here, there = (slice(1, d), slice(0, d - 1)) if side < 0 else (slice(0, d - 1), slice(1, d))
                        edge = slice(0, 1) if side < 0 else slice(d - 1, d)
                        for to, of, weight in ((slice(0, d), slice(0, d), near), (here, there, far),
                                               (edge, edge, far)):
                            step.link(nc.vector.scalar_tensor_tensor(
                                rows[:, to, r, :], source[:, of, :], weight, rows[:, to, r, :],
                                ALU.mult, ALU.add))
                dve.sem_inc(base_ready, 1)


TILES = BLOCK // 128
BLOCKS = TOKENS // BLOCK


def normed_tokens(nc, dve, step, tokens, normed, stats, moments, root, work, variance_ready, root_ready, number):
    for t in range(TILES):
        step(nc.vector.bn_stats(stats[:, t, :], tokens[:, t, :]))
    step.wait()
    mean, variance, apart, within = (moments[:, k, :] for k in range(4))
    step(nc.vector.tensor_tensor(mean, stats[:, :, 1], stats[:, :, 4], ALU.add))
    step(nc.vector.tensor_tensor(apart, stats[:, :, 1], stats[:, :, 4], ALU.subtract))
    step(nc.vector.tensor_tensor(within, stats[:, :, 2], stats[:, :, 5], ALU.add))
    step.wait()
    step(nc.vector.tensor_scalar(mean, mean, 0.5, None, ALU.mult))
    step.link(nc.vector.tensor_tensor(apart, apart, apart, ALU.mult))
    step.link(nc.vector.tensor_scalar(apart, apart, 0.25, 1e-5, ALU.mult, ALU.add))
    nc.vector.scalar_tensor_tensor(variance, within, 1.0 / DIM, apart, ALU.mult, ALU.add)\
        .then_inc(variance_ready, 1)
    inverse_root(nc, dve, step, root_ready, number, variance, root[:, :], work[:, :])
    for t in range(TILES):
        step(nc.vector.tensor_scalar(normed[:, t, :], tokens[:, t, :], moments[:, 0, t:t + 1], root[:, t:t + 1],
                                     ALU.subtract, ALU.mult))
    step.wait()


def fuse_fine_scale(nc, plan, fusion_wt, att_scratch, base_scratch, t1_scratch, n1_scratch):
    with nc.cleanup_on_exit(), ExitStack() as ctx:
        def sb(what, shape, dt=F32):
            return ctx.enter_context(nc.sbuf_tensor(f"ff_{what}", shape, dt))

        def sem(what):
            return nc.alloc_semaphore(f"ff_{what}")

        def pair(what, shape, dt=F32):
            return [sb(f"{what}{k}", shape, dt) for k in range(2)]

        weights = sb("weights", [128, HALVES, DIM])
        ident = sb("ident", [128, 128])
        att = pair("att", [128, TILES, DIM])
        base = pair("base", [128, HALVES, BLOCK])
        channels = pair("channels", [128, HALVES, BLOCK])
        tokens = pair("tokens", [128, TILES, DIM])
        normed = pair("normed", [128, TILES, DIM])
        turned = pair("turned", [128, HALVES, BLOCK])
        stats = sb("stats", [128, TILES, 6])
        moments = sb("moments", [128, 4, TILES])
        root = sb("root", [128, TILES])
        work = sb("work", [128, TILES])
        att_ps = [ctx.enter_context(nc.psum_tensor(f"ff_att_ps{k}", [128, 512], F32)) for k in range(2)]
        tokens_ps = [[ctx.enter_context(nc.psum_tensor(f"ff_tokens_ps{odd}{k}", [128, 512], F32)) for k in range(2)]
                     for odd in range(2)]
        normed_ps = [ctx.enter_context(nc.psum_tensor(f"ff_normed_ps{k}", [128, 512], F32)) for k in range(2)]

        weights_loaded = sem("weights_loaded")
        identity_made = sem("identity_made")
        att_loaded = [sem(f"att_loaded{k}") for k in range(2)]
        base_loaded = [sem(f"base_loaded{k}") for k in range(2)]
        att_turned = sem("att_turned")
        att_copied = sem("att_copied")
        tokens_ready = sem("tokens_ready")
        tokens_copied = sem("tokens_copied")
        steps = sem("steps")
        variance_ready = sem("variance_ready")
        root_ready = sem("root_ready")
        normed_ready = sem("normed_ready")
        normed_turned = sem("normed_turned")
        normed_copied = sem("normed_copied")
        tokens_stored = [sem(f"tokens_stored{k}") for k in range(2)]
        turned_stored = [sem(f"turned_stored{k}") for k in range(2)]
        block = ctx.enter_context(nc.Block())

        @block.sync
        def _(sp):
            sp.dma_start(weights[:, :, :], fusion_wt[0:DIM, :].rearrange("(k p) n -> p k n", p=128))\
                .then_inc(weights_loaded, 16)
            view = att_scratch[1:plan.units + 1].rearrange("(h b) p (t d) -> h b p t d", b=plan.blocks, d=32)

            def load(b, odd, turn):
                sp.wait_ge(tokens_copied, HEAD_START + b * TILES)
                for h in range(HEADS):
                    sp.dma_start(att[odd][:, :, h * 32:(h + 1) * 32], view[h, b]).then_inc(att_loaded[odd], 16)
                sp.dma_start(base[odd][:, :, :], base_scratch.rearrange("h p (b n) -> b p h n", n=BLOCK)[b])\
                    .then_inc(base_loaded[odd], 16)
            each_block(sp, BLOCKS, load)

        @block.gpsimd
        def _(pool):
            make_identity(nc, pool, ident, identity_made)

        @block.tensor
        def _(pe):
            pe.wait_ge(identity_made, 2)
            pe.wait_ge(weights_loaded, 16)

            def tokens_of(b, odd, turn):
                pe.wait_ge(att_loaded[odd], (turn + 1) * 16 * HEADS)
                pe.wait_ge(att_copied, HEAD_START + b * HALVES)
                for h in range(HALVES):
                    for t in range(TILES):
                        last = nc.tensor.transpose(att_ps[h][:, t * 128:(t + 1) * 128],
                                                   att[odd][:, t, h * 128:(h + 1) * 128], ident[:, :])
                    last.then_inc(att_turned, 1)
                pe.wait_ge(att_copied, HEAD_START + (b + 1) * HALVES)
                pe.wait_ge(base_loaded[odd], (turn + 1) * 16)
                pe.wait_ge(tokens_copied, HEAD_START + b * TILES)
                for t in range(TILES):
                    at = slice(t * 128, (t + 1) * 128)
                    out = tokens_ps[odd][t // 2][:, (t % 2) * DIM:(t % 2 + 1) * DIM]
                    nc.tensor.matmul(out, channels[odd][:, 0, at], weights[:, 0, :], start=True, stop=False)
                    for h in range(HALVES):
                        nc.tensor.matmul(out[:, h * 128:(h + 1) * 128], base[odd][:, h, at], ident[:, :],
                                         start=False, stop=False, skip_group_check=True)
                    last = nc.tensor.matmul(out, channels[odd][:, 1, at], weights[:, 1, :], start=False, stop=True)
                    if t % 2:
                        last.then_inc(tokens_ready, 1)

            def products(b, odd, turn, last):
                if not last:
                    tokens_of(b + 1, 1 - odd, turn + odd)
                pe.wait_ge(normed_ready, b + 1)
                pe.wait_ge(normed_copied, HEAD_START + b * HALVES)
                for h in range(HALVES):
                    for t in range(TILES):
                        done = nc.tensor.transpose(normed_ps[h][:, t * 128:(t + 1) * 128],
                                                   normed[odd][:, t, h * 128:(h + 1) * 128], ident[:, :])
                    done.then_inc(normed_turned, 1)

            tokens_of(0, 0, 0)
            each_block_but_last(pe, BLOCKS, products)

        @block.scalar
        def _(act):
            act.sem_inc(att_copied, HEAD_START)
            act.sem_inc(normed_copied, HEAD_START)
            for stored in tokens_stored:
                act.sem_inc(stored, HEAD_START)
            for stored in turned_stored:
                act.sem_inc(stored, HEAD_START)
            def copy_att(b, odd):
                for h in range(HALVES):
                    act.wait_ge(att_turned, b * HALVES + (h + 1))
                    nc.scalar.activation(channels[odd][:, h, :], att_ps[h][:, :], ACT.Copy).then_inc(att_copied, 1)

            def copies(b, odd, turn, last):
                if not last:
                    copy_att(b + 1, 1 - odd)
                act.wait_ge(variance_ready, b + 1)
                nc.scalar.activation(root[:, :], moments[:, 1, :], ACT.Sqrt).then_inc(root_ready, 1)
                act.wait_ge(turned_stored[odd], HEAD_START + turn * 16)
                for h in range(HALVES):
                    act.wait_ge(normed_turned, b * HALVES + (h + 1))
                    nc.scalar.activation(turned[odd][:, h, :], normed_ps[h][:, :], ACT.Copy)\
                        .then_inc(normed_copied, 1)
                act.wait_ge(tokens_copied, HEAD_START + (b + 2) * TILES)
                act.dma_start(t1_scratch[b], tokens[odd][:, :, :]).then_inc(tokens_stored[odd], 16)
                act.wait_ge(normed_copied, HEAD_START + (b + 1) * HALVES)
                act.dma_start(n1_scratch[b], turned[odd][:, :, :]).then_inc(turned_stored[odd], 16)
            copy_att(0, 0)
            each_block_but_last(act, BLOCKS, copies)
            for k in range(2):
                act.wait_ge(tokens_stored[k], HEAD_START + 16 * BLOCKS // 2)
                act.wait_ge(turned_stored[k], HEAD_START + 16 * BLOCKS // 2)

        @block.vector
        def _(dve):
            dve.sem_inc(tokens_copied, HEAD_START + TILES)

            def norm(b, odd, turn):
                step = Steps(dve, steps, b, 19)
                dve.wait_ge(tokens_stored[odd], HEAD_START + turn * 16)
                for t in range(TILES):
                    dve.wait_ge(tokens_ready, b * (TILES // 2) + (t // 2 + 1))
                    nc.vector.tensor_copy(tokens[odd][:, t, :],
                                          tokens_ps[odd][t // 2][:, (t % 2) * DIM:(t % 2 + 1) * DIM])\
                        .then_inc(tokens_copied, 1)
                dve.wait_ge(tokens_copied, HEAD_START + (b + 2) * TILES)
                normed_tokens(nc, dve, step, tokens[odd], normed[odd], stats, moments, root, work, variance_ready,
                              root_ready, b + 1)
                assert step.n == step.per_turn
                dve.sem_inc(normed_ready, 1)
            each_block(dve, BLOCKS, norm)


MAPS = 16
MAP_DIM = 16
LAMBDA_INIT = 0.8 - 0.6 * math.exp(-0.3)
HIDDEN = 4 * DIM


def project_tokens(nc, n1_scratch, wqk, wvg, bg, q_scratch, k_scratch, v_scratch, gate_scratch):
    scale = MAP_DIM ** -0.5
    with nc.cleanup_on_exit(), ExitStack() as ctx:
        def sb(what, shape, dt=F32):
            return ctx.enter_context(nc.sbuf_tensor(f"pt_{what}", shape, dt))

        def sem(what):
            return nc.alloc_semaphore(f"pt_{what}")

        def pair(what, shape, dt=F32):
            return [sb(f"{what}{k}", shape, dt) for k in range(2)]

        qk_weights = sb("qk_weights", [128, HALVES, 2 * DIM])
        vg_weights = sb("vg_weights", [128, HALVES, 2 * DIM])
        gate_bias = sb("gate_bias", [128, DIM])
        normed = pair("normed", [128, HALVES, BLOCK])
        high = pair("high", [128, 4, BLOCK], F32R)
        low = pair("low", [128, 4, BLOCK], F32R)
        value_mean = pair("value_mean", [128, TILES, HEADS])
        centred = pair("centred", [128, TILES, HEADS, 32])
        raw_gates = pair("raw_gates", [128, TILES, DIM])
        gates = pair("gates", [128, TILES, DIM])
        qk_ps = [ctx.enter_context(nc.psum_tensor(f"pt_qk{m}", [128, 512], F32)) for m in range(4)]
        vg_ps = [ctx.enter_context(nc.psum_tensor(f"pt_vg{m}", [128, 512], F32)) for m in range(4)]

        weights_loaded = sem("weights_loaded")
        normed_loaded = [sem(f"normed_loaded{k}") for k in range(2)]
        qk_ready = sem("qk_ready")
        vg_ready = sem("vg_ready")
        high_ready = sem("high_ready")
        low_ready = sem("low_ready")
        mean_ready = sem("mean_ready")
        values_ready = sem("values_ready")
        raw_gates_ready = sem("raw_gates_ready")
        gates_ready = sem("gates_ready")
        parts_stored = [sem(f"parts_stored{k}") for k in range(2)]
        values_stored = [sem(f"values_stored{k}") for k in range(2)]
        gates_stored = [sem(f"gates_stored{k}") for k in range(2)]
        block = ctx.enter_context(nc.Block())

        @block.sync
        def _(sp):
            sp.dma_start(qk_weights[:, :, :], wqk.rearrange("(k p) n -> p k n", p=128)).then_inc(weights_loaded, 16)
            sp.dma_start(vg_weights[:, :, :], wvg.rearrange("(k p) n -> p k n", p=128)).then_inc(weights_loaded, 16)
            sp.dma_start(gate_bias[:, :], bg.partition_broadcast(128)).then_inc(weights_loaded, 16)

            def load(b, odd, turn):
                sp.wait_ge(raw_gates_ready, HEAD_START + b * TILES)
                sp.dma_start(normed[odd][:, :, :], n1_scratch[b]).then_inc(normed_loaded[odd], 16)
            each_block(sp, BLOCKS, load)

        @block.tensor
        def _(pe):
            pe.wait_ge(weights_loaded, 48)

            def products(b, odd, turn):
                pe.wait_ge(normed_loaded[odd], (turn + 1) * 16)
                pe.wait_ge(low_ready, HEAD_START + b * 4)
                for m in range(4):
                    for h in range(HALVES):
                        last = nc.tensor.matmul(qk_ps[m][:, :], qk_weights[:, h, m * 128:(m + 1) * 128],
                                                normed[odd][:, h, :], start=h == 0, stop=h == HALVES - 1)
                    last.then_inc(qk_ready, 1)
                pe.wait_ge(raw_gates_ready, HEAD_START + (b + 1) * TILES)
                for t in range(TILES):
                    for h in range(HALVES):
                        last = nc.tensor.matmul(vg_ps[t][:, :], normed[odd][:, h, t * 128:(t + 1) * 128],
                                                vg_weights[:, h, :], start=h == 0, stop=h == HALVES - 1)
                    last.then_inc(vg_ready, 1)
            each_block(pe, BLOCKS, products)

        @block.vector
        def _(dve):
            dve.sem_inc(low_ready, HEAD_START)
            dve.sem_inc(raw_gates_ready, HEAD_START + TILES)
            dve.wait_ge(weights_loaded, 48)

            def sums(b, odd, turn):
                dve.wait_ge(parts_stored[odd], HEAD_START + turn * 16 * 12)
                for m in range(4):
                    dve.wait_ge(high_ready, b * 4 + (m + 1))
                    nc.vector.scalar_tensor_tensor(low[odd][:, m, :], qk_ps[m][:, :], scale if m < 2 else 1.0,
                                                   high[odd][:, m, :].bitcast(F32), ALU.mult, ALU.subtract)\
                        .then_inc(low_ready, 1)
                dve.wait_ge(values_stored[odd], HEAD_START + turn * 16 * TILES)
                for t in range(TILES):
                    values = vg_ps[t][:, 0:DIM].rearrange("p (h d) -> p h d", d=32)
                    dve.wait_ge(vg_ready, b * TILES + (t + 1))
                    nc.vector.tensor_reduce(value_mean[odd][:, t, :], values, AX.X, ALU.add).then_inc(mean_ready, 1)
                    if t == 0:
                        dve.wait_ge(gates_ready, HEAD_START + b)
                    dve.wait_ge(mean_ready, 2 * (b * TILES + t) + 1)
                    nc.vector.tensor_scalar(value_mean[odd][:, t, :], value_mean[odd][:, t, :], 1.0 / 32, None,
                                            ALU.mult).then_inc(mean_ready, 1)
                    dve.wait_ge(mean_ready, 2 * (b * TILES + t) + 2)
                    nc.vector.tensor_tensor(
                        centred[odd][:, t, :, :], values,
                        value_mean[odd][:, t, :].unsqueeze(2).to_broadcast([128, HEADS, 32]), ALU.subtract)\
                        .then_inc(values_ready, 1)
                    nc.vector.tensor_tensor(raw_gates[odd][:, t, :], vg_ps[t][:, DIM:2 * DIM], gate_bias[:, :],
                                            ALU.add).then_inc(raw_gates_ready, 1)
            each_block(dve, BLOCKS, sums)

        @block.scalar
        def _(act):
            for stored in parts_stored:
                act.sem_inc(stored, HEAD_START)
            for stored in values_stored:
                act.sem_inc(stored, HEAD_START)
            for stored in gates_stored:
                act.sem_inc(stored, HEAD_START)
            act.sem_inc(gates_ready, HEAD_START)
            q_view = q_scratch.rearrange("(h b) (s d) n -> b s h d n", b=BLOCKS, s=3)
            k_view = k_scratch.rearrange("h (s d) (b n) -> b s h d n", s=3, n=BLOCK)
            v_view = v_scratch.rearrange("h p (b t) d -> b t p h d", t=TILES)

            def parts(b, odd, turn):
                act.wait_ge(parts_stored[odd], HEAD_START + turn * 16 * 12)
                for m in range(4):
                    act.wait_ge(qk_ready, b * 4 + (m + 1))
                    nc.scalar.activation(high[odd][:, m, :], qk_ps[m][:, :], ACT.Copy,
                                         scale=scale if m < 2 else 1.0).then_inc(high_ready, 1)
                act.wait_ge(low_ready, HEAD_START + (b + 1) * 4)
                for m in range(4):
                    view = q_view if m < 2 else k_view
                    for s, part in enumerate((high, high, low) if m < 2 else (high, low, high)):
                        act.dma_start(view[b, s, 8 * (m % 2):8 * (m % 2) + 8],
                                      part[odd][:, m, :].bitcast(F32)).then_inc(parts_stored[odd], 16)
                act.wait_ge(raw_gates_ready, HEAD_START + (b + 2) * TILES)
                act.wait_ge(gates_stored[odd], HEAD_START + turn * 16)
                nc.scalar.activation(gates[odd][:, :, :], raw_gates[odd][:, :, :], ACT.Sigmoid)\
                    .then_inc(gates_ready, 1)
                act.wait_ge(values_ready, (b + 1) * TILES)
                for t in range(TILES):
                    act.dma_start(v_view[b, t], centred[odd][:, t, :, 0:31]).then_inc(values_stored[odd], 16)
                act.wait_ge(gates_ready, HEAD_START + b + 1)
                act.dma_start(gate_scratch[b], gates[odd][:, :, :]).then_inc(gates_stored[odd], 16)
            each_block(act, BLOCKS, parts)
            for k in range(2):
                act.wait_ge(parts_stored[k], HEAD_START + 16 * 12 * BLOCKS // 2)
                act.wait_ge(values_stored[k], HEAD_START + 16 * TILES * BLOCKS // 2)
                act.wait_ge(gates_stored[k], HEAD_START + 16 * BLOCKS // 2)


def finish_attention(nc, plan, att_scratch, gate_scratch, t1_scratch, lambdas, gamma, beta, w_out, b_out, w_route,
                     b_route, n2_scratch, sum_scratch, route_scratch):
    with nc.cleanup_on_exit(), ExitStack() as ctx:
        def sb(what, shape, dt=F32):
            return ctx.enter_context(nc.sbuf_tensor(f"fa_{what}", shape, dt))

        def sem(what):
            return nc.alloc_semaphore(f"fa_{what}")

        def pair(what, shape, dt=F32):
            return [sb(f"{what}{k}", shape, dt) for k in range(2)]

        rows = TILES * HEADS
        weights = sb("weights", [128, HALVES, DIM])
        ident = sb("ident", [128, 128])
        out_bias = sb("out_bias", [128, DIM])
        route_weights = sb("route_weights", [128, DIM])
        route_bias = sb("route_bias", [128, 1])
        head_scale = sb("head_scale", [128, 32])
        head_shift = sb("head_shift", [128, 32])
        vectors = sb("vectors", [128, 4, MAP_DIM])
        dots = sb("dots", [128, 2])
        dot_junk = sb("dot_junk", [128, MAP_DIM])
        powers = sb("powers", [128, 2])
        minus_lambda = sb("minus_lambda", [128, 1])
        maps = pair("maps", [128, rows, 2, 32])
        t1 = pair("t1", [128, TILES, DIM])
        gates = pair("gates", [128, TILES, DIM])
        heads = pair("heads", [128, rows, 32])
        gate_scale = pair("gate_scale", [128, rows, 32])
        gate_shift = pair("gate_shift", [128, rows, 32])
        squares = sb("squares", [128, rows, 32])
        variance = sb("variance", [128, rows])
        head_root = sb("head_root", [128, rows])
        head_work = sb("head_work", [128, rows])
        channels = sb("channels", [128, HALVES, BLOCK])
        tokens = sb("tokens", [128, TILES, DIM])
        normed = sb("normed", [128, TILES, DIM])
        junk = sb("junk", [128, DIM])
        total = pair("total", [128, TILES, DIM])
        turned = pair("turned", [128, HALVES, BLOCK])
        stats = sb("stats", [128, TILES, 6])
        moments = sb("moments", [128, 4, TILES])
        root = sb("root", [128, TILES])
        work = sb("work", [128, TILES])
        routed = sb("routed", [128, TILES])
        route = pair("route", [128, TILES])
        heads_ps = [ctx.enter_context(nc.psum_tensor(f"fa_heads_ps{k}", [128, 512], F32)) for k in range(2)]
        tokens_ps = [ctx.enter_context(nc.psum_tensor(f"fa_tokens_ps{k}", [128, 512], F32)) for k in range(2)]
        normed_ps = [ctx.enter_context(nc.psum_tensor(f"fa_normed_ps{k}", [128, 512], F32)) for k in range(2)]

        weights_loaded = sem("weights_loaded")
        identity_made = sem("identity_made")
        dots_ready = sem("dots_ready")
        powers_ready = sem("powers_ready")
        maps_loaded = [sem(f"maps_loaded{k}") for k in range(2)]
        t1_loaded = [sem(f"t1_loaded{k}") for k in range(2)]
        gates_loaded = [sem(f"gates_loaded{k}") for k in range(2)]
        const_steps = sem("const_steps")
        head_steps = sem("head_steps")
        token_steps = sem("token_steps")
        gate_steps = sem("gate_steps")
        affine_ready = sem("affine_ready")
        difference_ready = sem("difference_ready")
        squares_ready = sem("squares_ready")
        heads_variance_ready = sem("heads_variance_ready")
        heads_root_ready = sem("heads_root_ready")
        heads_ready = sem("heads_ready")
        heads_turned = sem("heads_turned")
        heads_copied = sem("heads_copied")
        tokens_ready = sem("tokens_ready")
        variance_ready = sem("variance_ready")
        root_ready = sem("root_ready")
        normed_ready = sem("normed_ready")
        normed_turned = sem("normed_turned")
        normed_copied = sem("normed_copied")
        total_ready = sem("total_ready")
        turned_stored = [sem(f"turned_stored{k}") for k in range(2)]
        total_stored = [sem(f"total_stored{k}") for k in range(2)]
        route_stored = [sem(f"route_stored{k}") for k in range(2)]
        block = ctx.enter_context(nc.Block())

        @block.sync
        def _(sp):
            for k in range(4):
                sp.dma_start(vectors[:, k, :], lambdas[k].partition_broadcast(128)).then_inc(weights_loaded, 16)
            sp.dma_start(head_scale[:, :], gamma.partition_broadcast(128)).then_inc(weights_loaded, 16)
            sp.dma_start(head_shift[:, :], beta.partition_broadcast(128)).then_inc(weights_loaded, 16)
            sp.dma_start(weights[:, :, :], w_out.rearrange("(k p) n -> p k n", p=128)).then_inc(weights_loaded, 16)
            sp.dma_start(out_bias[:, :], b_out.partition_broadcast(128)).then_inc(weights_loaded, 16)
            sp.dma_start(route_weights[:, :], w_route.partition_broadcast(128)).then_inc(weights_loaded, 16)
            sp.dma_start(route_bias[:, :], b_route.partition_broadcast(128)).then_inc(weights_loaded, 16)
            view = att_scratch[1:plan.units + 1].rearrange("(h b) p (t d) -> h b p t d", b=BLOCKS, d=32)

            def load(b, odd, turn):
                sp.wait_ge(difference_ready, HEAD_START + b)
                for a in range(MAPS):
                    sp.dma_start(maps[odd][:, :, a % 2, :].rearrange("p (t h) d -> p t h d", h=HEADS)[:, :, a // 2, :],
                                 view[a, b]).then_inc(maps_loaded[odd], 16)
                sp.wait_ge(heads_ready, HEAD_START + b)
                sp.dma_start(gates[odd][:, :, :], gate_scratch[b]).then_inc(gates_loaded[odd], 16)
                sp.wait_ge(total_ready, HEAD_START + b)
                sp.dma_start(t1[odd][:, :, :], t1_scratch[b]).then_inc(t1_loaded[odd], 16)
            each_block(sp, BLOCKS, load)

        @block.gpsimd
        def _(pool):
            make_identity(nc, pool, ident, identity_made)
            pool.wait_ge(affine_ready, 1)

            def gate(b, odd, turn):
                step = Steps(pool, gate_steps, b, 3)
                gates_of_head = gates[odd][:, :, :].rearrange("p t (h d) -> p (t h) d", d=32)
                pool.wait_ge(gates_loaded[odd], (turn + 1) * 16)
                for to, of in ((gate_scale, head_scale), (gate_shift, head_shift)):
                    step.link(nc.gpsimd.tensor_tensor(to[odd][:, :, :], gates_of_head,
                                                      of[:, :].unsqueeze(1).to_broadcast([128, rows, 32]), ALU.mult))
                pool.wait_ge(t1_loaded[odd], (turn + 1) * 16)
                step.link(nc.gpsimd.tensor_tensor(t1[odd][:, :, :], t1[odd][:, :, :],
                                                  out_bias[:, :].unsqueeze(1).to_broadcast([128, TILES, DIM]),
                                                  ALU.add))
            each_block(pool, BLOCKS, gate)

        @block.tensor
        def _(pe):
            pe.wait_ge(identity_made, 2)
            pe.wait_ge(weights_loaded, 160)

            def products(b, odd, turn):
                pe.wait_ge(heads_ready, HEAD_START + b + 2)
                view = heads[odd][:, :, :].rearrange("p (t h) d -> p t (h d)", h=HEADS)
                for h in range(HALVES):
                    for t in range(TILES):
                        last = nc.tensor.transpose(heads_ps[h][:, t * 128:(t + 1) * 128],
                                                   view[:, t, h * 128:(h + 1) * 128], ident[:, :])
                    last.then_inc(heads_turned, 1)
                pe.wait_ge(heads_copied, HEAD_START + (b + 1) * HALVES)
                for t in range(TILES):
                    out = tokens_ps[t // 2][:, (t % 2) * DIM:(t % 2 + 1) * DIM]
                    for h in range(HALVES):
                        last = nc.tensor.matmul(out, channels[:, h, t * 128:(t + 1) * 128], weights[:, h, :],
                                                start=h == 0, stop=h == HALVES - 1)
                    if t % 2:
                        last.then_inc(tokens_ready, 1)
                pe.wait_ge(normed_ready, b + 1)
                pe.wait_ge(normed_copied, HEAD_START + b * HALVES)
                for h in range(HALVES):
                    for t in range(TILES):
                        last = nc.tensor.transpose(normed_ps[h][:, t * 128:(t + 1) * 128],
                                                   normed[:, t, h * 128:(h + 1) * 128], ident[:, :])
                    last.then_inc(normed_turned, 1)
            each_block(pe, BLOCKS, products)

        @block.scalar
        def _(act):
            act.sem_inc(normed_copied, HEAD_START)
            for stored in turned_stored:
                act.sem_inc(stored, HEAD_START)
            act.sem_inc(heads_copied, HEAD_START)
            for stored in route_stored:
                act.sem_inc(stored, HEAD_START)
            for stored in total_stored:
                act.sem_inc(stored, HEAD_START)
            act.wait_ge(dots_ready, 2)
            nc.scalar.activation(powers[:, :], dots[:, :], ACT.Exp).then_inc(powers_ready, 1)

            def squares_and_roots(b, odd):
                act.wait_ge(difference_ready, HEAD_START + b + 2)
                nc.scalar.activation(squares[:, :, :], heads[odd][:, :, :], ACT.Square).then_inc(squares_ready, 1)
                act.wait_ge(heads_variance_ready, b + 1)
                nc.scalar.activation(head_root[:, :], variance[:, :], ACT.Sqrt).then_inc(heads_root_ready, 1)

            squares_and_roots(0, 0)

            def copies(b, odd, turn, last):
                for h in range(HALVES):
                    act.wait_ge(heads_turned, b * HALVES + (h + 1))
                    nc.scalar.activation(channels[:, h, :], heads_ps[h][:, :], ACT.Copy).then_inc(heads_copied, 1)
                if not last:
                    squares_and_roots(b + 1, 1 - odd)
                act.wait_ge(variance_ready, b + 1)
                nc.scalar.activation(root[:, :], moments[:, 1, :], ACT.Sqrt).then_inc(root_ready, 1)
                act.wait_ge(turned_stored[odd], HEAD_START + turn * 16)
                for h in range(HALVES):
                    act.wait_ge(normed_turned, b * HALVES + (h + 1))
                    nc.scalar.activation(turned[odd][:, h, :], normed_ps[h][:, :], ACT.Copy)\
                        .then_inc(normed_copied, 1)
                act.wait_ge(total_ready, HEAD_START + b + 2)
                act.dma_start(sum_scratch[b], total[odd][:, :, :]).then_inc(total_stored[odd], 16)
                act.dma_start(route_scratch[b], route[odd][:, :]).then_inc(route_stored[odd], 16)
                act.wait_ge(normed_copied, HEAD_START + (b + 1) * HALVES)
                act.dma_start(n2_scratch[b], turned[odd][:, :, :]).then_inc(turned_stored[odd], 16)
            each_block_but_last(act, BLOCKS, copies)
            for k in range(2):
                act.wait_ge(turned_stored[k], HEAD_START + 16 * BLOCKS // 2)
                act.wait_ge(total_stored[k], HEAD_START + 16 * BLOCKS // 2)
                act.wait_ge(route_stored[k], HEAD_START + 16 * BLOCKS // 2)

        @block.vector
        def _(dve):
            for done in (difference_ready, heads_ready, total_ready):
                dve.sem_inc(done, HEAD_START + 1)
            dve.wait_ge(weights_loaded, 160)
            const = Steps(dve, const_steps)
            for k in range(2):
                nc.vector.tensor_tensor_reduce(out=dot_junk[:, :], in0=vectors[:, 2 * k, :],
                                               in1=vectors[:, 2 * k + 1, :], scale=1.0, scalar=0.0, op0=ALU.mult,
                                               op1=ALU.add, accum_out=dots[:, k:k + 1]).then_inc(dots_ready, 1)
                dve.wait_ge(dots_ready, k + 1)
            dve.wait_ge(powers_ready, 1)
            const.link(nc.vector.tensor_tensor(minus_lambda[:, :], powers[:, 1:2], powers[:, 0:1], ALU.subtract))
            const.link(nc.vector.tensor_scalar(minus_lambda[:, :], minus_lambda[:, :], -LAMBDA_INIT, None, ALU.add))
            const.link(nc.vector.tensor_scalar(head_scale[:, :], head_scale[:, :], 1 - LAMBDA_INIT, None, ALU.mult))
            const.link(nc.vector.tensor_scalar(head_shift[:, :], head_shift[:, :], 1 - LAMBDA_INIT, None, ALU.mult))
            dve.sem_inc(affine_ready, 1)

            def difference(b, odd, turn):
                step = Steps(dve, head_steps, b, 9)
                head = heads[odd]
                dve.wait_ge(maps_loaded[odd], (turn + 1) * 16 * MAPS)
                step.link(nc.vector.scalar_tensor_tensor(head[:, :, 0:31], maps[odd][:, :, 1, 0:31],
                                                         minus_lambda[:, 0:1], maps[odd][:, :, 0, 0:31],
                                                         ALU.mult, ALU.add))
                nc.vector.tensor_reduce(head[:, :, 31], head[:, :, 0:31], AX.X, ALU.add, negate=True)\
                    .then_inc(difference_ready, 1)
                dve.wait_ge(squares_ready, b + 1)
                step.link(nc.vector.tensor_reduce(variance[:, :], squares[:, :, :], AX.X, ALU.add))
                nc.vector.tensor_scalar(variance[:, :], variance[:, :], 1.0 / 32, 1e-5, ALU.mult, ALU.add)\
                    .then_inc(heads_variance_ready, 1)
                inverse_root(nc, dve, step, heads_root_ready, b + 1, variance[:, :], head_root[:, :],
                             head_work[:, :])
                step.link(nc.vector.tensor_tensor(head[:, :, :], head[:, :, :],
                                                  head_root[:, :].unsqueeze(2).to_broadcast([128, rows, 32]),
                                                  ALU.mult))
                dve.wait_ge(gate_steps, b * 3 + 2)
                step.link(nc.vector.tensor_tensor(head[:, :, :], head[:, :, :], gate_scale[odd][:, :, :], ALU.mult))
                nc.vector.tensor_tensor(head[:, :, :], head[:, :, :], gate_shift[odd][:, :, :], ALU.add)\
                    .then_inc(heads_ready, 1)
                assert step.n == step.per_turn, step.n

            def finish(b, odd, turn, last):
                if not last:
                    dve.wait_ge(heads_copied, HEAD_START + b * HALVES)
                    difference(b + 1, 1 - odd, turn + odd)
                step = Steps(dve, token_steps, b, 26)
                dve.wait_ge(gate_steps, b * 3 + 3)
                for k in range(2):
                    dve.wait_ge(tokens_ready, b * 2 + (k + 1))
                    step(nc.vector.tensor_tensor(tokens[:, 2 * k:2 * k + 2, :],
                                                 tokens_ps[k][:, :].rearrange("p (t c) -> p t c", t=2),
                                                 t1[odd][:, 2 * k:2 * k + 2, :], ALU.add))
                step.wait()
                dve.wait_ge(normed_copied, HEAD_START + b * HALVES)
                normed_tokens(nc, dve, step, tokens, normed, stats, moments, root, work, variance_ready,
                              root_ready, b + 1)
                dve.sem_inc(normed_ready, 1)
                for t in range(TILES):
                    step.link(nc.vector.tensor_tensor_reduce(
                        out=junk[:, :], in0=normed[:, t, :], in1=route_weights[:, :], scale=1.0, scalar=0.0,
                        op0=ALU.mult, op1=ALU.add, accum_out=routed[:, t:t + 1]))
                dve.wait_ge(route_stored[odd], HEAD_START + turn * 16)
                dve.wait_ge(total_stored[odd], HEAD_START + turn * 16)
                step.link(nc.vector.tensor_scalar(route[odd][:, :], routed[:, :], route_bias[:, 0:1], None,
                                                  ALU.add))
                nc.vector.tensor_tensor(total[odd][:, :, :], tokens[:, :, :], normed[:, :, :], ALU.add)\
                    .then_inc(total_ready, 1)
                assert step.n == step.per_turn, step.n
            difference(0, 0, 0)
            each_block_but_last(dve, BLOCKS, finish)


def feed_forward(nc, n2_scratch, sum_scratch, route_scratch, route_rows, w1, b1, w2, b2, out):
    kept = TOKENS // 2 - 1
    hidden_tiles = HIDDEN // 128
    with nc.cleanup_on_exit(), ExitStack() as ctx:
        def sb(what, shape, dt=F32):
            return ctx.enter_context(nc.sbuf_tensor(f"fn_{what}", shape, dt))

        def sem(what):
            return nc.alloc_semaphore(f"fn_{what}")

        def pair(what, shape, dt=F32):
            return [sb(f"{what}{k}", shape, dt) for k in range(2)]

        up = sb("up", [128, HALVES, HIDDEN])
        down = sb("down", [128, hidden_tiles, DIM])
        up_parts = pair("up_parts", [128, HALVES, HIDDEN], F32R)
        down_parts = pair("down_parts", [128, hidden_tiles, DIM], F32R)
        up_bias = sb("up_bias", [128, hidden_tiles])
        down_bias = sb("down_bias", [128, DIM])
        ident = sb("ident", [128, 128])
        earlier = sb("earlier", [128, 128])
        normed = pair("normed", [128, HALVES, BLOCK])
        total = pair("total", [128, TILES, DIM])
        normed_high = pair("normed_high", [128, HALVES, BLOCK], F32R)
        normed_low = pair("normed_low", [128, HALVES, BLOCK], F32R)
        hidden = pair("hidden", [128, BLOCK])
        hidden_high = sb("hidden_high", [128, hidden_tiles, BLOCK], F32R)
        hidden_low = sb("hidden_low", [128, hidden_tiles, BLOCK], F32R)
        all_routes = sb("all_routes", [128, TOKENS])
        route = sb("route", [128, BLOCKS * TILES])
        compared = sb("compared", [128, TOKENS])
        counts = sb("counts", [128, BLOCKS * TILES, 4])
        rank = sb("rank", [128, BLOCKS * TILES, 3])
        share = sb("share", [128, BLOCKS * TILES])
        result = sb("result", [128, TILES, DIM])
        turned = pair("turned", [128, HALVES, BLOCK])
        hidden_ps = [ctx.enter_context(nc.psum_tensor(f"fn_hidden_ps{k}", [128, 512], F32)) for k in range(2)]
        result_ps = [ctx.enter_context(nc.psum_tensor(f"fn_result_ps{k}", [128, 512], F32)) for k in range(2)]
        turned_ps = [ctx.enter_context(nc.psum_tensor(f"fn_turned_ps{k}", [128, 512], F32)) for k in range(2)]

        weights_loaded = sem("weights_loaded")
        routes_written = sem("routes_written")
        routes_loaded = sem("routes_loaded")
        identity_made = sem("identity_made")
        earlier_made = sem("earlier_made")
        normed_loaded = [sem(f"normed_loaded{k}") for k in range(2)]
        total_loaded = [sem(f"total_loaded{k}") for k in range(2)]
        up_ready = sem("up_ready")
        hidden_ready = sem("hidden_ready")
        down_ready = sem("down_ready")
        weights_high_ready = sem("weights_high_ready")
        weights_low_ready = sem("weights_low_ready")
        normed_high_ready = sem("normed_high_ready")
        normed_low_ready = sem("normed_low_ready")
        hidden_high_ready = sem("hidden_high_ready")
        hidden_low_ready = sem("hidden_low_ready")
        steps = sem("steps")
        result_ready = sem("result_ready")
        turned_ready = sem("turned_ready")
        turned_copied = sem("turned_copied")
        out_stored = [sem(f"out_stored{k}") for k in range(2)]
        block = ctx.enter_context(nc.Block())

        @block.sync
        def _(sp):
            with nc.allow_non_contiguous_dma(reason="4096 words in all"):
                for b in range(BLOCKS):
                    sp.dma_start(route_rows[b].rearrange("(t p) -> p t", p=128), route_scratch[b])\
                        .then_inc(routes_written, 16)
            sp.dma_start(up[:, :, :], w1.rearrange("(k p) n -> p k n", p=128)).then_inc(weights_loaded, 16)
            sp.dma_start(down[:, :, :], w2.rearrange("(k p) n -> p k n", p=128)).then_inc(weights_loaded, 16)
            for m in range(hidden_tiles):
                sp.dma_start(up_bias[:, m:m + 1], b1[m * 128:(m + 1) * 128, :]).then_inc(weights_loaded, 16)
            sp.dma_start(down_bias[:, :], b2.partition_broadcast(128)).then_inc(weights_loaded, 16)
            sp.wait_ge(routes_written, 16 * BLOCKS)
            sp.dma_start(all_routes[:, :], route_rows.rearrange("b n -> (b n)").partition_broadcast(128))\
                .then_inc(routes_loaded, 16)
            sp.dma_start(route[:, :].rearrange("p (b t) -> p b t", t=TILES),
                         route_scratch.rearrange("b p t -> p b t")).then_inc(routes_loaded, 16)

            def load(b, odd, turn):
                sp.wait_ge(result_ready, HEAD_START + b)
                sp.dma_start(normed[odd][:, :, :], n2_scratch[b]).then_inc(normed_loaded[odd], 16)
                sp.dma_start(total[odd][:, :, :], sum_scratch[b]).then_inc(total_loaded[odd], 16)
            each_block(sp, BLOCKS, load)

        @block.gpsimd
        def _(pool):
            make_identity(nc, pool, ident, identity_made)
            nc.gpsimd.memset(earlier[:, :], 1.0).then_inc(earlier_made, 1)
            pool.wait_ge(earlier_made, 1)
            nc.gpsimd.affine_select(out=earlier[:, :], in_=earlier[:, :], compare_op=ALU.is_gt, fill=0.0, base=0,
                                    pattern=[[-1, 128]], channel_multiplier=1).then_inc(earlier_made, 1)
            pool.wait_ge(earlier_made, 2)
            pool.sem_inc(hidden_low_ready, HEAD_START + 1)

            def lows(b, odd, turn):
                pool.wait_ge(normed_high_ready, b + 1)
                nc.gpsimd.tensor_tensor(normed_low[odd][:, :, :], normed[odd][:, :, :],
                                        normed_high[odd][:, :, :].bitcast(F32), ALU.subtract)\
                    .then_inc(normed_low_ready, 1)
                pool.wait_ge(normed_low_ready, b + 1)
                for m in range(hidden_tiles):
                    pool.wait_ge(hidden_high_ready, b * hidden_tiles + (m + 1))
                    nc.gpsimd.tensor_tensor(hidden_low[:, m, :], hidden[m % 2][:, :],
                                            hidden_high[:, m, :].bitcast(F32), ALU.subtract)\
                        .then_inc(hidden_low_ready, 1)
                    pool.wait_ge(hidden_low_ready, HEAD_START + b * hidden_tiles + (m + 2))
            each_block(pool, BLOCKS, lows)

        @block.tensor
        def _(pe):
            pe.sem_inc(down_ready, HEAD_START)
            pe.wait_ge(identity_made, 2)
            pe.wait_ge(weights_low_ready, 2)
            def up_products(b, odd):
                pe.wait_ge(normed_low_ready, b + 1)
                normed_parts = normed_high[odd], normed_low[odd]
                for m in range(hidden_tiles):
                    pe.wait_ge(hidden_ready, HEAD_START + b * hidden_tiles + m)
                    for h in range(HALVES):
                        for k, (weight, token) in enumerate(PARTS):
                            last = nc.tensor.matmul(hidden_ps[m % 2][:, :],
                                                    up_parts[weight][:, h, m * 128:(m + 1) * 128],
                                                    normed_parts[token][:, h, :], start=h + k == 0,
                                                    stop=h == HALVES - 1 and k == 2)
                    last.then_inc(up_ready, 1)

            def down_products(b):
                hidden_parts = hidden_high, hidden_low
                pe.wait_ge(hidden_low_ready, HEAD_START + (b + 1) * hidden_tiles + 1)
                pe.wait_ge(result_ready, HEAD_START + b + 1)
                for t in range(TILES):
                    for m in range(hidden_tiles):
                        for k, (weight, part) in enumerate(PARTS):
                            last = nc.tensor.matmul(result_ps[t // 2][:, (t % 2) * DIM:(t % 2 + 1) * DIM],
                                                    hidden_parts[part][:, m, t * 128:(t + 1) * 128],
                                                    down_parts[weight][:, m, :], start=m + k == 0,
                                                    stop=m == hidden_tiles - 1 and k == 2)
                    if t % 2:
                        last.then_inc(down_ready, 1)

            def products(b, odd, turn, last):
                down_products(b)
                if not last:
                    up_products(b + 1, 1 - odd)
                pe.wait_ge(result_ready, HEAD_START + b + 2)
                pe.wait_ge(turned_copied, HEAD_START + b * HALVES)
                for h in range(HALVES):
                    for t in range(TILES):
                        last = nc.tensor.transpose(turned_ps[h][:, t * 128:(t + 1) * 128],
                                                   result[:, t, h * 128:(h + 1) * 128], ident[:, :])
                    last.then_inc(turned_ready, 1)
            up_products(0, 0)
            each_block_but_last(pe, BLOCKS, products)

        @block.scalar
        def _(act):
            act.sem_inc(turned_copied, HEAD_START)
            for stored in out_stored:
                act.sem_inc(stored, HEAD_START)
            act.wait_ge(weights_loaded, 16 * (3 + hidden_tiles))
            act.sem_inc(hidden_ready, HEAD_START + 1)
            out_view = out.rearrange("(h p) (b n) -> b p h n", p=128, n=BLOCK)

            for parts, whole in ((up_parts, up), (down_parts, down)):
                nc.scalar.activation(parts[0][:, :, :], whole[:, :, :], ACT.Copy).then_inc(weights_high_ready, 1)

            def activations(b, odd, turn):
                act.wait_ge(normed_loaded[odd], (turn + 1) * 16)
                nc.scalar.activation(normed_high[odd][:, :, :], normed[odd][:, :, :], ACT.Copy)\
                    .then_inc(normed_high_ready, 1)

                for m in range(hidden_tiles):
                    act.wait_ge(up_ready, b * hidden_tiles + (m + 1))
                    if m == 0:
                        act.wait_ge(down_ready, HEAD_START + b * 2)
                    act.wait_ge(hidden_low_ready, HEAD_START + b * hidden_tiles + m)
                    nc.scalar.activation(hidden[m % 2][:, :], hidden_ps[m % 2][:, :], ACT.Gelu_apprx_tanh,
                                         bias=up_bias[:, m:m + 1]).then_inc(hidden_ready, 1)
                    act.wait_ge(hidden_ready, HEAD_START + b * hidden_tiles + (m + 2))
                    nc.scalar.activation(hidden_high[:, m, :], hidden[m % 2][:, :], ACT.Copy)\
                        .then_inc(hidden_high_ready, 1)

            def copies(b, odd, turn, last):
                if not last:
                    activations(b + 1, 1 - odd, turn + odd)
                act.wait_ge(out_stored[odd], HEAD_START + turn * 16)
                for h in range(HALVES):
                    act.wait_ge(turned_ready, b * HALVES + (h + 1))
                    nc.scalar.activation(turned[odd][:, h, :], turned_ps[h][:, :], ACT.Copy)\
                        .then_inc(turned_copied, 1)
                act.wait_ge(turned_copied, HEAD_START + (b + 1) * HALVES)
                act.dma_start(out_view[b], turned[odd][:, :, :]).then_inc(out_stored[odd], 16)
            activations(0, 0, 0)
            each_block_but_last(act, BLOCKS, copies)
            for k in range(2):
                act.wait_ge(out_stored[k], HEAD_START + 16 * BLOCKS // 2)

        @block.vector
        def _(dve):
            dve.sem_inc(result_ready, HEAD_START + 1)
            for k, (parts, whole) in enumerate(((up_parts, up), (down_parts, down))):
                dve.wait_ge(weights_high_ready, k + 1)
                nc.vector.tensor_tensor(parts[1][:, :, :], whole[:, :, :], parts[0][:, :, :].bitcast(F32),
                                        ALU.subtract).then_inc(weights_low_ready, 1)
            step = Steps(dve, steps)
            dve.wait_ge(routes_loaded, 32)
            dve.wait_ge(earlier_made, 2)
            dve.wait_ge(weights_loaded, 16 * (3 + hidden_tiles))
            step(nc.vector.memset(counts[:, :, :], 0.0))
            step.wait()

            def count_ahead(n):
                mine = route[:, n:n + 1]
                tile = slice(n * 128, (n + 1) * 128)
                for k, (part, op) in enumerate(((slice(0, n * 128), ALU.is_ge),
                                                (slice((n + 1) * 128, TOKENS), ALU.is_gt), (tile, ALU.is_gt))):
                    if part.stop > part.start:
                        step(nc.vector.tensor_scalar(compared[:, part], all_routes[:, part], mine, 0.0, op, ALU.add,
                                                     accum_out=counts[:, n, k:k + 1]))
                step.wait()
                step.link(nc.vector.scalar_tensor_tensor(compared[:, tile], all_routes[:, tile], mine,
                                                         earlier[:, :], ALU.is_equal, ALU.mult,
                                                         accum_out=counts[:, n, 3:4]))

            for b in range(BLOCKS):
                odd, turn = b % 2, b // 2
                at = slice(b * TILES, (b + 1) * TILES)
                for t in range(TILES):
                    count_ahead(b * TILES + t)
                step.link(nc.vector.tensor_reduce(rank[:, at, 0], counts[:, at, :], AX.X, ALU.add))
                step.link(nc.vector.tensor_scalar(rank[:, at, 1], rank[:, at, 0], float(kept), None, ALU.is_lt))
                step.link(nc.vector.tensor_tensor(share[:, at], rank[:, at, 1], route[:, at], ALU.mult))
                dve.wait_ge(total_loaded[odd], (turn + 1) * 16)
                if b:
                    dve.wait_ge(turned_copied, HEAD_START + b * HALVES)
                for k in range(2):
                    dve.wait_ge(down_ready, HEAD_START + b * 2 + (k + 1))
                    step(nc.vector.tensor_tensor(result[:, 2 * k:2 * k + 2, :],
                                                 result_ps[k][:, :].rearrange("p (t c) -> p t c", t=2),
                                                 down_bias[:, :].unsqueeze(1).to_broadcast([128, 2, DIM]), ALU.add))
                step.wait()
                for t in range(TILES):
                    done = nc.vector.scalar_tensor_tensor(result[:, t, :], result[:, t, :],
                                                          share[:, b * TILES + t:b * TILES + t + 1],
                                                          total[odd][:, t, :], ALU.mult, ALU.add)
                    if t < TILES - 1:
                        step(done)
                    else:
                        done.then_inc(result_ready, 1)


_INS = [("x", (DIM, TOKENS)), ("dw_w", (3, DIM, 9)), ("dw_b", (3, DIM, 1)), ("pw_wt", (3, DIM, 3 * DIM)),
        ("pw_b", (3, 3 * DIM, 1)), ("pos_w", (3, DIM, 9)), ("pos_b", (3, DIM, 1)), ("fusion_wt", (3 * DIM, DIM)),
        ("fusion_b", (DIM, 1)), ("wqk", (DIM, 2 * DIM)), ("wvg", (DIM, 2 * DIM)), ("w_out", (DIM, DIM)),
        ("b_out", (DIM,)), ("bg", (DIM,)), ("lambdas", (4, MAP_DIM)), ("gamma", (32,)), ("beta", (32,)),
        ("w_route", (DIM,)), ("b_route", (1,)), ("w1", (DIM, HIDDEN)), ("b1", (HIDDEN, 1)), ("w2", (HIDDEN, DIM)),
        ("b2", (DIM,))]


class AttentionScratch:

    def __init__(self, scratch, p):
        self.q = scratch(f"{p.name}_q", (p.units, 3 * p.part_rows, p.width))
        self.k = scratch(f"{p.name}_k", (p.maps, 3 * p.part_rows, p.tokens))
        self.v = scratch(f"{p.name}_v", (p.maps // 2 if p.v_shared else p.maps, 128, p.key_tiles, p.v_cols))
        self.out = scratch(f"{p.name}_out", (p.units + 1, 128, p.q_tiles * 32))


def conv_attn_hybrid_kernel(nc, out, x, dw_w, dw_b, pw_wt, pw_b, pos_w, pos_b, fusion_wt, fusion_b, wqk, wvg, w_out,
                            b_out, bg, lambdas, gamma, beta, w_route, b_route, w1, b1, w2, b2):
    def scratch(name, shape):
        return nc.dram_tensor(name, shape, F32).ap()

    plans = [AttentionPlan(f"s{i}", HEADS, TOKENS // s ** 2, min(BLOCK, TOKENS // s ** 2), DIM // HEADS, 32, False)
             for i, s in enumerate(SCALES)]
    diff = AttentionPlan("df", MAPS, TOKENS, BLOCK, MAP_DIM, 31, True)

    fine = [AttentionScratch(scratch, p) for p in plans]
    dw = [scratch(f"dw{i}", (HALVES, 128, p.tokens)) for i, p in enumerate(plans)]
    pos = [scratch(f"pos{i}", (HALVES, 128, p.tokens)) for i, p in enumerate(plans)]
    convolutions(nc, x, dw_w, dw_b, pos_w, pos_b, dw, pos)
    for i, p in enumerate(plans):
        project_scale(nc, i, p, dw, pos, pw_wt, pw_b, fine[i].q, fine[i].k, fine[i].v)
    for i in (2, 1, 0):
        attention(nc, plans[i], fine[i].q, fine[i].k, fine[i].v, fine[i].out)
    base = scratch("base", (HALVES, 128, TOKENS))
    t1 = scratch("t1", (BLOCKS, 128, TILES, DIM))
    n1 = scratch("n1", (BLOCKS, 128, HALVES, BLOCK))
    gates = scratch("gates", (BLOCKS, 128, TILES, DIM))
    fuse_coarse_scales(nc, plans, x, fusion_wt, fusion_b, [f.out for f in fine], base)
    fuse_fine_scale(nc, plans[0], fusion_wt, fine[0].out, base, t1, n1)
    maps = AttentionScratch(scratch, diff)
    project_tokens(nc, n1, wqk, wvg, bg, maps.q, maps.k, maps.v, gates)
    attention(nc, diff, maps.q, maps.k, maps.v, maps.out)
    n2 = scratch("n2", (BLOCKS, 128, HALVES, BLOCK))
    total = scratch("total", (BLOCKS, 128, TILES, DIM))
    route = scratch("route", (BLOCKS, 128, TILES))
    route_rows = scratch("route_rows", (BLOCKS, BLOCK))
    finish_attention(nc, diff, maps.out, gates, t1, lambdas, gamma, beta, w_out, b_out, w_route, b_route, n2, total,
                     route)
    feed_forward(nc, n2, total, route, route_rows, w1, b1, w2, b2, out)


def kernel(**inputs):
    import numpy as np
    import concourse.bacc as bacc
    from concourse.bass_utils import run_bass_kernel_spmd

    a = {name: np.asarray(value) for name, value in inputs.items()}
    conv = {n: a[f"L0_conv_{n}"] for n in ("dw_w", "dw_b", "pw_w", "pw_b", "pos_w", "pos_b", "fusion_w", "fusion_b")}
    attn = {n: a[f"L1_attn_{n}"] for n in ("Wq", "Wkv", "Wout", "bout", "Wg", "bg", "lq1", "lk1", "lq2", "lk2",
                                           "ln_gamma", "ln_beta")}
    ffn = {n: a[f"L1_ffn_{n}"] for n in ("wr", "br", "w1", "b1", "w2", "b2")}
    laid_out = {
        "x": a["x"], "dw_w": conv["dw_w"], "dw_b": conv["dw_b"], "pw_wt": conv["pw_w"].transpose(0, 2, 1),
        "pw_b": conv["pw_b"], "pos_w": conv["pos_w"], "pos_b": conv["pos_b"], "fusion_wt": conv["fusion_w"].T,
        "fusion_b": conv["fusion_b"], "wqk": np.concatenate([attn["Wq"], attn["Wkv"][:, :DIM]], 1),
        "wvg": np.concatenate([attn["Wkv"][:, DIM:], attn["Wg"]], 1), "w_out": attn["Wout"],
        "b_out": attn["bout"], "bg": attn["bg"],
        "lambdas": np.stack([attn["lq1"], attn["lk1"], attn["lq2"], attn["lk2"]]), "gamma": attn["ln_gamma"],
        "beta": attn["ln_beta"], "w_route": ffn["wr"], "b_route": ffn["br"], "w1": ffn["w1"], "b1": ffn["b1"],
        "w2": ffn["w2"], "b2": ffn["b2"]}
    nc = bacc.Bacc("TRN2", target_bir_lowering=False, num_devices=1)
    arrays, args = {}, {}
    for name, shape in _INS:
        array = np.ascontiguousarray(laid_out[name].reshape(shape))
        arrays[f"in_{name}_dram"] = array
        args[name] = nc.dram_tensor(f"in_{name}_dram", array.shape, mybir.dt.from_np(array.dtype),
                                    kind="ExternalInput").ap()
    out = nc.dram_tensor("out_0_dram", (DIM, TOKENS), F32, kind="ExternalOutput").ap()
    conv_attn_hybrid_kernel(nc, out, **args)
    result = run_bass_kernel_spmd(nc, [arrays], core_ids=[0])
    return result.results[0]["out_0_dram"].reshape(1, DIM, SIDE, SIDE)
```
